# Optimizing a Trainium2 kernel written in Bass

```python
import numpy as np
import jax
import jax.numpy as jnp

def _softmax(x, axis=-1):
    return jax.nn.softmax(x, axis=axis)

def _gelu(x):
    return jax.nn.gelu(x, approximate=True)

def _silu(x):
    return jax.nn.silu(x)

def _sigmoid(x):
    return jax.nn.sigmoid(x)

def _layernorm(x, axis=-1, eps=1e-05):
    m = jnp.mean(x, axis=axis, keepdims=True)
    v = jnp.var(x, axis=axis, keepdims=True)
    return (x - m) / jnp.sqrt(v + eps)

def _scatter_add(tgt, idx, src, axis=0):
    return tgt.at[idx].add(src)

def _segment_sum(src, seg, n):
    return jax.ops.segment_sum(src, seg, n)
kernel_name = 'mk_gps_d1_gnn_r32_877eb1'

def setup_inputs(seed: int=0):
    np.random.seed(seed)
    _w = jnp.asarray

    def _rec_inputs():
        import jax
        import jax.numpy as jnp
        _gk = jax.random.key(seed)
        x = -0.000364 + 1 * jax.random.normal(jax.random.fold_in(_gk, 1), (625, 768), jnp.float32)
        _s = jax.random.randint(jax.random.fold_in(_gk, 2), (5000,), 0, 625, jnp.int32)
        _d = jax.random.randint(jax.random.fold_in(_gk, 3), (5000,), 0, 625, jnp.int32)
        _loop = jnp.arange(625, dtype=jnp.int32)
        src = jnp.concatenate([_s, _d, _loop])
        dst = jnp.concatenate([_d, _s, _loop])
        _o = jnp.argsort(dst, stable=True)
        src = src[_o]
        dst = dst[_o]
        return (x, src, dst)
    x, src, dst = _rec_inputs()

    def _L0_gnn_setup():
        import jax, jax.numpy as jnp
        import numpy as np
        N, E, DIM, HEADS = (625, 10000, 768, 8)
        HD = DIM // HEADS
        EPS = 1e-05

        def layer_norm(x, w, b):
            mu = jnp.mean(x, axis=-1, keepdims=True)
            var = jnp.var(x, axis=-1, keepdims=True)
            return (x - mu) * jax.lax.rsqrt(var + EPS) * w + b

        def gatv2(x, src, dst, Ws, bs, Wd, bd, attn):
            H, D = attn.shape
            fs = (x @ Ws + bs).reshape(-1, H, D)
            fd = (x @ Wd + bd).reshape(-1, H, D)
            e = jax.nn.leaky_relu(fs[src] + fd[dst], 0.2)
            logits = jnp.einsum('ehd,hd->eh', e, attn)
            m = jax.ops.segment_max(logits, dst, num_segments=N)
            ex = jnp.exp(logits - m[dst])
            denom = jax.ops.segment_sum(ex, dst, num_segments=N)
            alpha = ex / denom[dst]
            out = jax.ops.segment_sum(alpha[:, :, None] * fs[src], dst, num_segments=N)
            return jax.nn.elu(out)
        key = jax.random.key(seed)
        ks = jax.random.split(key, 10)
        s = 1.0 / np.sqrt(DIM)
        return {'x': jax.random.normal(ks[0], (N, DIM), jnp.float32), 'src': jax.random.randint(ks[1], (E,), 0, N, jnp.int32), 'dst': jax.random.randint(ks[2], (E,), 0, N, jnp.int32), 'W1s': jax.random.normal(ks[3], (DIM, DIM), jnp.float32) * s, 'b1s': jnp.zeros((DIM,), jnp.float32), 'W1d': jax.random.normal(ks[4], (DIM, DIM), jnp.float32) * s, 'b1d': jnp.zeros((DIM,), jnp.float32), 'attn1': jax.random.normal(ks[5], (HEADS, HD), jnp.float32) * s, 'ln1_w': jnp.ones((DIM,), jnp.float32), 'ln1_b': jnp.zeros((DIM,), jnp.float32), 'Wos': jax.random.normal(ks[6], (DIM, DIM), jnp.float32) * s, 'bos': jnp.zeros((DIM,), jnp.float32), 'Wod': jax.random.normal(ks[7], (DIM, DIM), jnp.float32) * s, 'bod': jnp.zeros((DIM,), jnp.float32), 'attno': jax.random.normal(ks[8], (1, DIM), jnp.float32) * s, 'lno_w': jnp.ones((DIM,), jnp.float32), 'lno_b': jnp.zeros((DIM,), jnp.float32)}
    _L0_gnn_all = _L0_gnn_setup()
    _L0_gnn_in = {k: v for k, v in _L0_gnn_all.items() if k in ('W1s', 'b1s', 'W1d', 'b1d', 'attn1', 'ln1_w', 'ln1_b', 'Wos', 'bos', 'Wod', 'bod', 'attno', 'lno_w', 'lno_b')}
    del _L0_gnn_all

    def _L0_mix_setup():
        import jax, jax.numpy as jnp
        import numpy as np
        import math
        EPS = 0.001

        def _relu_features(t, proj_mat):
            ratio = 1.0 / math.sqrt(float(proj_mat.shape[0]))
            z = ratio * jnp.einsum('blhd,md->blhm', t, proj_mat)
            return jax.nn.relu(z) + EPS
        key = jax.random.key(seed)
        ks = jax.random.split(key, 6)
        B, L, DIM = (8, 128, 768)
        H, D, M = (12, 64, 256)
        x = jax.random.normal(ks[0], (B, L, DIM), dtype=jnp.float32)
        qkv_w = jax.random.normal(ks[1], (3 * DIM, DIM), dtype=jnp.float32) * DIM ** (-0.5)
        qkv_b = jnp.zeros((3 * DIM,), dtype=jnp.float32)
        proj_w = jax.random.normal(ks[2], (DIM, DIM), dtype=jnp.float32) * DIM ** (-0.5)
        proj_b = jnp.zeros((DIM,), dtype=jnp.float32)
        blocks = []
        for i in range(M // D):
            g = jax.random.normal(ks[3 + 0] if False else jax.random.fold_in(ks[3], i), (D, D), dtype=jnp.float32)
            q, _ = jnp.linalg.qr(g)
            blocks.append(q.T)
        pm = jnp.concatenate(blocks, axis=0)
        mult = jnp.linalg.norm(jax.random.normal(ks[4], (M, D), dtype=jnp.float32), axis=1)
        proj_mat = mult[:, None] * pm
        return {'x': x, 'qkv_w': qkv_w, 'qkv_b': qkv_b, 'proj_w': proj_w, 'proj_b': proj_b, 'proj_mat': proj_mat}
    _L0_mix_all = _L0_mix_setup()
    _L0_mix_in = {k: v for k, v in _L0_mix_all.items() if k in ('qkv_w', 'qkv_b', 'proj_w', 'proj_b', 'proj_mat')}
    del _L0_mix_all

    def _L0_ffn_setup():
        import jax, jax.numpy as jnp
        import numpy as np
        from jax import lax
        DIM = 768
        INTER = 512
        E = 8
        G = 4
        TOPK_G = 2
        TOPK = 2
        ROUTE_SCALE = 1.0

        def _gate(x2, gate_weight, gate_bias):
            T = x2.shape[0]
            scores = jax.nn.sigmoid(x2 @ gate_weight.T)
            s = scores + gate_bias
            sv = s.reshape(T, G, E // G)
            top2, _ = lax.top_k(sv, 2)
            group_scores = top2.sum(-1)
            _, gidx = lax.top_k(group_scores, TOPK_G)
            gmask = jnp.zeros((T, G), bool).at[jnp.arange(T)[:, None], gidx].set(True)
            masked = jnp.where(gmask[:, :, None], sv, -jnp.inf).reshape(T, E)
            _, idx = lax.top_k(masked, TOPK)
            w = jnp.take_along_axis(scores, idx, axis=1)
            w = w / (w.sum(-1, keepdims=True) + 1e-06) * ROUTE_SCALE
            return (w, idx)
        key = jax.random.key(seed)
        ks = jax.random.split(key, 9)
        s = 1.0 / np.sqrt(DIM)
        si = 1.0 / np.sqrt(INTER)
        return {'x': jax.random.normal(ks[0], (4, 128, DIM), jnp.float32), 'gate_weight': jax.random.uniform(ks[1], (E, DIM), jnp.float32, -s, s), 'gate_bias': jnp.zeros((E,), jnp.float32), 'w1': jax.random.uniform(ks[2], (E, INTER, DIM), jnp.float32, -s, s), 'w2': jax.random.uniform(ks[3], (E, DIM, INTER), jnp.float32, -si, si), 'w3': jax.random.uniform(ks[4], (E, INTER, DIM), jnp.float32, -s, s), 'sw1': jax.random.uniform(ks[5], (INTER, DIM), jnp.float32, -s, s), 'sw2': jax.random.uniform(ks[6], (DIM, INTER), jnp.float32, -si, si), 'sw3': jax.random.uniform(ks[7], (INTER, DIM), jnp.float32, -s, s)}
    _L0_ffn_all = _L0_ffn_setup()
    _L0_ffn_in = {k: v for k, v in _L0_ffn_all.items() if k in ('gate_weight', 'gate_bias', 'w1', 'w2', 'w3', 'sw1', 'sw2', 'sw3')}
    del _L0_ffn_all
    return {'x': x, 'src': src, 'dst': dst, 'L0_gnn_W1s': _L0_gnn_in['W1s'], 'L0_gnn_b1s': _L0_gnn_in['b1s'], 'L0_gnn_W1d': _L0_gnn_in['W1d'], 'L0_gnn_b1d': _L0_gnn_in['b1d'], 'L0_gnn_attn1': _L0_gnn_in['attn1'], 'L0_gnn_ln1_w': _L0_gnn_in['ln1_w'], 'L0_gnn_ln1_b': _L0_gnn_in['ln1_b'], 'L0_gnn_Wos': _L0_gnn_in['Wos'], 'L0_gnn_bos': _L0_gnn_in['bos'], 'L0_gnn_Wod': _L0_gnn_in['Wod'], 'L0_gnn_bod': _L0_gnn_in['bod'], 'L0_gnn_attno': _L0_gnn_in['attno'], 'L0_gnn_lno_w': _L0_gnn_in['lno_w'], 'L0_gnn_lno_b': _L0_gnn_in['lno_b'], 'L0_mix_qkv_w': _L0_mix_in['qkv_w'], 'L0_mix_qkv_b': _L0_mix_in['qkv_b'], 'L0_mix_proj_w': _L0_mix_in['proj_w'], 'L0_mix_proj_b': _L0_mix_in['proj_b'], 'L0_mix_proj_mat': _L0_mix_in['proj_mat'], 'L0_ffn_gate_weight': _L0_ffn_in['gate_weight'], 'L0_ffn_gate_bias': _L0_ffn_in['gate_bias'], 'L0_ffn_w1': _L0_ffn_in['w1'], 'L0_ffn_w2': _L0_ffn_in['w2'], 'L0_ffn_w3': _L0_ffn_in['w3'], 'L0_ffn_sw1': _L0_ffn_in['sw1'], 'L0_ffn_sw2': _L0_ffn_in['sw2'], 'L0_ffn_sw3': _L0_ffn_in['sw3']}

def reference(x, src, dst, L0_gnn_W1s, L0_gnn_b1s, L0_gnn_W1d, L0_gnn_b1d, L0_gnn_attn1, L0_gnn_ln1_w, L0_gnn_ln1_b, L0_gnn_Wos, L0_gnn_bos, L0_gnn_Wod, L0_gnn_bod, L0_gnn_attno, L0_gnn_lno_w, L0_gnn_lno_b, L0_mix_qkv_w, L0_mix_qkv_b, L0_mix_proj_w, L0_mix_proj_b, L0_mix_proj_mat, L0_ffn_gate_weight, L0_ffn_gate_bias, L0_ffn_w1, L0_ffn_w2, L0_ffn_w3, L0_ffn_sw1, L0_ffn_sw2, L0_ffn_sw3):
    import jax
    import jax.numpy as jnp

    def _L0_gnn_ref(x, src, dst, W1s, b1s, W1d, b1d, attn1, ln1_w, ln1_b, Wos, bos, Wod, bod, attno, lno_w, lno_b):
        import jax, jax.numpy as jnp
        import numpy as np
        N, E, DIM, HEADS = (625, 10000, 768, 8)
        HD = DIM // HEADS
        EPS = 1e-05

        def layer_norm(x, w, b):
            mu = jnp.mean(x, axis=-1, keepdims=True)
            var = jnp.var(x, axis=-1, keepdims=True)
            return (x - mu) * jax.lax.rsqrt(var + EPS) * w + b

        def gatv2(x, src, dst, Ws, bs, Wd, bd, attn):
            H, D = attn.shape
            fs = (x @ Ws + bs).reshape(-1, H, D)
            fd = (x @ Wd + bd).reshape(-1, H, D)
            e = jax.nn.leaky_relu(fs[src] + fd[dst], 0.2)
            logits = jnp.einsum('ehd,hd->eh', e, attn)
            m = jax.ops.segment_max(logits, dst, num_segments=N)
            ex = jnp.exp(logits - m[dst])
            denom = jax.ops.segment_sum(ex, dst, num_segments=N)
            alpha = ex / denom[dst]
            out = jax.ops.segment_sum(alpha[:, :, None] * fs[src], dst, num_segments=N)
            return jax.nn.elu(out)
        h = gatv2(x, src, dst, W1s, b1s, W1d, b1d, attn1).reshape(N, DIM)
        h = layer_norm(h + x, ln1_w, ln1_b)
        out = gatv2(h, src, dst, Wos, bos, Wod, bod, attno).reshape(N, DIM)
        return layer_norm(out, lno_w, lno_b)

    def _L0_mix_ref(x, qkv_w, qkv_b, proj_w, proj_b, proj_mat):
        import jax, jax.numpy as jnp
        import numpy as np
        import math
        EPS = 0.001

        def _relu_features(t, proj_mat):
            ratio = 1.0 / math.sqrt(float(proj_mat.shape[0]))
            z = ratio * jnp.einsum('blhd,md->blhm', t, proj_mat)
            return jax.nn.relu(z) + EPS
        B, L, DIM = x.shape
        H = 12
        D = DIM // H
        qkv = x @ qkv_w.T + qkv_b
        qkv = qkv.reshape(B, L, 3, H, D)
        q, k, v = (qkv[:, :, 0], qkv[:, :, 1], qkv[:, :, 2])
        q_p = _relu_features(q, proj_mat)
        k_p = _relu_features(k, proj_mat)
        kv = jnp.einsum('blhm,blhd->bhmd', k_p, v)
        k_sum = k_p.sum(axis=1)
        num = jnp.einsum('blhm,bhmd->blhd', q_p, kv)
        den = jnp.einsum('blhm,bhm->blh', q_p, k_sum)
        out = num / den[..., None]
        out = out.reshape(B, L, DIM)
        return out @ proj_w.T + proj_b

    def _L0_ffn_ref(x, gate_weight, gate_bias, w1, w2, w3, sw1, sw2, sw3):
        import jax, jax.numpy as jnp
        import numpy as np
        from jax import lax
        DIM = 768
        INTER = 512
        E = 8
        G = 4
        TOPK_G = 2
        TOPK = 2
        ROUTE_SCALE = 1.0

        def _gate(x2, gate_weight, gate_bias):
            T = x2.shape[0]
            scores = jax.nn.sigmoid(x2 @ gate_weight.T)
            s = scores + gate_bias
            sv = s.reshape(T, G, E // G)
            top2, _ = lax.top_k(sv, 2)
            group_scores = top2.sum(-1)
            _, gidx = lax.top_k(group_scores, TOPK_G)
            gmask = jnp.zeros((T, G), bool).at[jnp.arange(T)[:, None], gidx].set(True)
            masked = jnp.where(gmask[:, :, None], sv, -jnp.inf).reshape(T, E)
            _, idx = lax.top_k(masked, TOPK)
            w = jnp.take_along_axis(scores, idx, axis=1)
            w = w / (w.sum(-1, keepdims=True) + 1e-06) * ROUTE_SCALE
            return (w, idx)
        B, S, D = x.shape
        x2 = x.reshape(-1, D)
        T = x2.shape[0]
        weights, indices = _gate(x2, gate_weight, gate_bias)
        cw = jnp.zeros((T, E), x.dtype).at[jnp.arange(T)[:, None], indices].add(weights)
        h1 = jnp.einsum('td,eid->tei', x2, w1)
        h3 = jnp.einsum('td,eid->tei', x2, w3)
        h = jax.nn.silu(h1) * h3
        y = jnp.einsum('tei,edi,te->td', h, w2, cw)
        z = jax.nn.silu(x2 @ sw1.T) * (x2 @ sw3.T) @ sw2.T
        return (y + z).reshape(B, S, D)
    xn = _layernorm(x, axis=-1)
    x = x + _L0_gnn_ref(xn, src, dst, L0_gnn_W1s, L0_gnn_b1s, L0_gnn_W1d, L0_gnn_b1d, L0_gnn_attn1, L0_gnn_ln1_w, L0_gnn_ln1_b, L0_gnn_Wos, L0_gnn_bos, L0_gnn_Wod, L0_gnn_bod, L0_gnn_attno, L0_gnn_lno_w, L0_gnn_lno_b) + _L0_mix_ref(xn[None], L0_mix_qkv_w, L0_mix_qkv_b, L0_mix_proj_w, L0_mix_proj_b, L0_mix_proj_mat)[0]
    x = x + _L0_ffn_ref(_layernorm(x, axis=-1)[None], L0_ffn_gate_weight, L0_ffn_gate_bias, L0_ffn_w1, L0_ffn_w2, L0_ffn_w3, L0_ffn_sw1, L0_ffn_sw2, L0_ffn_sw3)[0]
    return x

_drawn_inputs = setup_inputs


def setup_inputs(seed=0):
    import zlib

    import numpy as np

    out = dict(_drawn_inputs(seed))
    spreads = {'L0_gnn_b1s': (0.0, 0.1),
     'L0_gnn_b1d': (0.0, 0.8),
     'L0_gnn_ln1_w': (1.0, 0.2),
     'L0_gnn_ln1_b': (0.0, 0.1),
     'L0_gnn_bos': (0.0, 0.1),
     'L0_gnn_bod': (0.0, 0.447),
     'L0_gnn_lno_w': (1.0, 0.2),
     'L0_gnn_lno_b': (0.0, 0.1),
     'L0_mix_qkv_b': (0.0, 0.1),
     'L0_mix_proj_b': (0.0, 0.1),
     'L0_ffn_gate_bias': (0.0, 0.1)}
    factors = {'L0_gnn_W1d': 3.216, 'L0_mix_proj_mat': 8.0}
    for name, (base, spread) in spreads.items():
        noise = np.random.default_rng([zlib.crc32(name.encode()), seed]).standard_normal(out[name].shape)
        drawn = base * np.exp(spread * noise) if base else spread * noise
        out[name] = jnp.asarray(drawn.astype(out[name].dtype))
    for name, factor in factors.items():
        out[name] = (out[name] * factor).astype(out[name].dtype)
    return out
```

```python
from contextlib import ExitStack

import concourse.bass as bass
from concourse import mybir

ACT = mybir.ActivationFunctionType
ALU = mybir.AluOpType
AX = mybir.AxisListType
F32 = mybir.dt.float32
F32R = mybir.dt.float32r
F16 = mybir.dt.float16
I32 = mybir.dt.int32

N = 625
P = 125
T = N // P
D = 768
KC = D // 128
HALF = D // 2
TP = 626
EDGES = 10625
ET = EDGES // P
G = 5
NG = ET // G
HEADS1 = 8
MH = 12
MD = 64
MF = 256
EXPERTS = 9
INTER = 512
IC = INTER // 128
LN_EPS = 1e-5
NEG = -1.0e30
BIG = 1.0e30
PIECE = 1536


def build(nc, x, src, dst, W1s, b1s, W1d, b1d, attn1, ln1_w, ln1_b, Wos, bos, Wod, bod, attno, lno_w,
          lno_b, qkv_wT, qk_bcols, v_brow, proj_wT, proj_b, proj_matT, gate_wT, gate_bias, moe_w, out):
    ctx = ExitStack()
    with ctx:
        def sem(name):
            return ctx.enter_context(nc.semaphore(name))

        def sb(name, shape, dt, stack=ctx):
            return stack.enter_context(nc.sbuf_tensor(name, shape, dt))

        def zone(tensors):
            with ExitStack() as here:
                return [sb(name, shape, dt, here) for name, shape, dt in tensors]

        def dram(name, shape):
            return nc.dram_tensor(name, shape, F32, kind="Internal").ap()

        table_src = [dram(f"table_src{l}", (N, D)) for l in range(2)]
        table_dst = [dram(f"table_dst{l}", (N, D)) for l in range(2)]
        HL = [HEADS1, 1]
        dense_logits = [dram(f"dense_logits{l}", (N * N, HL[l])) for l in range(2)]

        ident = sb("ident", [128, 128], F32)
        iota_i = sb("iota_i", [128, TP], I32)
        iota_h = sb("iota_h", [128, TP], F16)
        src_i = sb("src_i", [P, ET], I32)
        dst_i = sb("dst_i", [P, ET], I32)
        src_f = sb("src_f", [P, ET], F32)
        dst_f = sb("dst_f", [P, ET], F32)
        idx_all = sb("idx_all", [P, ET, 3], I32)
        idx_cur = sb("idx_cur", [P, G, 3], I32)
        logits = sb("logits", [P, G, HEADS1], F32)
        stats = sb("stats", [P, T, 2, 6], F32)
        mv = sb("mv", [P, T, 2], F32)
        std = sb("std", [P, T], F32)
        rstd = sb("rstd", [P, T], F32)
        eps_ln = sb("eps_ln", [128, 1], F32)
        mxv = sb("mxv", [P, T, HEADS1], F32)
        den = sb("den", [P, T, HEADS1], F32)
        rden = sb("rden", [P, T, HEADS1], F32)
        mix_rden = sb("mix_rden", [P, T, MH], F32)
        qk_bias = sb("qk_bias", [128, 2 * KC], F32)
        cw = sb("cw", [P, T, EXPERTS], F32)
        gate_s = sb("gate_s", [P, T, 8], F32)
        gate_k = sb("gate_k", [P, T, 8], F32)
        gate_r = sb("gate_r", [P, T, 8], F32)
        gate_t = sb("gate_t", [P, T, 8], F32)
        gate_g = sb("gate_g", [P, T, 4], F32)
        gate_b = sb("gate_b", [P, 8], F32)
        gate_w_raw = sb("gate_w_raw", [128, KC, 8], F32)
        gate_w_hi = sb("gate_w_hi", [128, KC, 8], F32R)
        gate_w_lo = sb("gate_w_lo", [128, KC, 8], F32R)
        ones_row = sb("ones_row", [1, P], F32)

        counts, rows = zone([("counts", [P, T, N], F32), ("rows", [P, 4, D], F32)])
        (hid,) = zone([("hid", [128, 2, IC, TP], F32R)])
        sb("zone_d", [128, T * N + 4 * D], F32)
        fs = sb("fs", [P, T, D], F32)
        xt = sb("xt", [128, T * D], F32)
        xt_v = xt[:, 0:KC * N].rearrange("p (k n) -> p k n", k=KC)
        x2 = xt[0:P, :].rearrange("p (t d) -> p t d", t=T)
        (at,) = zone([("at", [128, 2, KC, TP], F32R)])
        mix_qt, mix_kt, mix_v, mix_kp, mix_qp, mix_kv = zone([
            ("mix_qt", [128, N], F32), ("mix_kt", [128, N], F32), ("mix_v", [P, T, 2, MD + 1], F32),
            ("mix_kp", [P, T, MF], F32), ("mix_qp", [128, 2, N], F32), ("mix_kv", [128, 2, 2, MD + 1], F32)])
        dl1 = zone([("dl_a", [P, N * 8], F32), ("dl_b", [P, N * 8], F32), ("de_a", [P, 8, N], F32),
                    ("de_b", [P, 8, N], F32), ("dpt", [P, 40 * P], F32)])
        sb("zone_a", [128, 2 * KC * TP], F32)
        wp0, wp1, wraw0, wraw1, fd_stage = zone([
            ("wp0", [128, 2, KC, HALF], F32R), ("wp1", [128, 2, KC, HALF], F32R),
            ("wraw0", [128, KC, HALF], F32), ("wraw1", [128, KC, HALF], F32), ("fd_stage", [P, T, D], F32)])
        wp, wraw = [wp0, wp1], [wraw0, wraw1]
        ring_s, ring_d, hot_s, hot_d = zone([
            ("ring_s", [P, G, D], F32), ("ring_d", [P, G, D], F32),
            ("hot_s", [P, G, TP], F16), ("hot_d", [P, G, TP], F16)])
        _, mix_w, mix_out, pmt, v_row = zone([
            ("under_ring", [P, 2 * G * D], F32), ("mix_w", [128, KC, 3 * 128], F32),
            ("mix_out", [P, T, MH, MD + 1], F32), ("pmt", [128, MF], F32), ("v_row", [1, D], F32)])
        _, dl2a, dl2b, de2a, de2b, dpt2, _, gnn, neg, elu_o_t, elu_m_t = zone([
            ("under_w", [P, 4 * KC * HALF], F32),
            ("dl2_a", [P, N], F32), ("dl2_b", [P, N], F32), ("de2_a", [P, 1, N], F32), ("de2_b", [P, 1, N], F32),
            ("dpt2", [P, 5 * P], F32), ("between", [P, 2 * KC * HALF - 5 * N], F32), ("gnn", [P, T, D], F32),
            ("neg", [P, N], F32), ("elu_o", [P, D], F32), ("elu_m", [P, D], F32)])
        (we,) = zone([("we", [128, 6, 6 * INTER], F32R)])
        _, eraw, silu = zone([("under_we", [128, 6 * 6 * INTER], F32), ("eraw", [128, 3, PIECE], F32),
                              ("silu", [128, 2, TP], F32)])
        sb("zone_c", [128, 6 * 6 * INTER + 3 * PIECE + 2 * TP - T * D], F32)
        b1 = sb("b1", [P, T, D], F32)
        ps = ctx.enter_context(nc.psum_tensor("ps", [128, 8, 512], F32))
        elu_o, elu_m = elu_o_t[:, :], elu_m_t[:, :]

        x_loaded, idx_loaded, const_ready, prep_done = (sem(n) for n in
            ("x_loaded", "idx_loaded", "const_ready", "prep_done"))
        small_loaded = sem("small_loaded")
        rows_loaded = {name: sem("rows_" + name) for name in ("gat1", "ln1", "attn2", "gat2", "ln2", "proj")}
        ln_var, ln_std, ln_done = sem("ln_var"), sem("ln_std"), sem("ln_done")
        tr_full, tr_hi, tr_lo, xt_copied = sem("tr_full"), sem("tr_hi"), sem("tr_lo"), sem("xt_copied")
        raw_loaded = [sem(f"raw_loaded{i}") for i in range(2)]
        w_hi, w_lo = sem("w_hi"), sem("w_lo")
        mm_full, mm_used = sem("mm_full"), sem("mm_used")
        tables_written = sem("tables_written")
        pool_turn = sem("pool_turn")
        neg_ready, filled = sem("neg_ready"), sem("filled")
        gathered = [[sem(f"gathered{l}_{j}") for j in range(G)] for l in range(2)]
        edge_done = [sem(f"edge_done{l}") for l in range(2)]
        scattered = [sem(f"scattered{l}") for l in range(2)]
        hot_ready, hot_used, counts_ready = sem("hot_ready"), sem("hot_used"), sem("counts_ready")
        dl_loaded = [[sem(f"dl_loaded{l}_{i}") for i in range(2)] for l in range(2)]
        max_ready = [sem(f"max_ready{l}") for l in range(2)]
        exp_ready = [sem(f"exp_ready{l}") for l in range(2)]
        probs_ready = [sem(f"probs_ready{l}") for l in range(2)]
        pt_full = [sem(f"pt_full{l}") for l in range(2)]
        pt_copied = [sem(f"pt_copied{l}") for l in range(2)]
        agg_full = [sem(f"agg_full{l}") for l in range(2)]
        elu_min = [sem(f"elu_min{l}") for l in range(2)]
        elu_exp = [sem(f"elu_exp{l}") for l in range(2)]
        out_ready = [sem(f"out_ready{l}") for l in range(2)]
        mixw_loaded, mixw_used = sem("mixw_loaded"), sem("mixw_used")
        mix_full, mix_used = sem("mix_full"), sem("mix_used")
        mix_step = sem("mix_step")
        mixo_done = sem("mixo_done")
        xagain_loaded = sem("xagain_loaded")
        gate_full, gate_exp, gate_done = sem("gate_full"), sem("gate_exp"), sem("gate_done")
        gw_hi, gw_lo = sem("gw_hi"), sem("gw_lo")
        eraw_loaded = [sem(f"eraw_loaded{i}") for i in range(3)]
        e_hi, e_lo = sem("e_hi"), sem("e_lo")
        up_full, silu_done, hid_f, hid_hi, hid_lo = (sem(n) for n in
            ("up_full", "silu_done", "hid_f", "hid_hi", "hid_lo"))
        down_full, down_used = sem("down_full"), sem("down_used")
        out_stored = sem("out_stored")
        step = sem("step")
        astep = sem("astep")

        block = ctx.enter_context(nc.Block())
        TR = KC
        MM = 10
        cell_rows = [dense_logits[l].rearrange("(t p s) h -> t p (s h)", t=T, p=P) for l in range(2)]
        weights = [W1s, W1d, Wos, Wod, proj_wT]
        half_of = [(w, h) for w in weights for h in range(2)]
        gd_groups = [(HL[l] * T + 3) // 4 for l in range(2)]

        def row(v):
            return v.rearrange("(a d) -> a d", a=1).to_broadcast([P, D])

        @block.sync
        def _(sp):
            sp.dma_start(b1[:, :, :], x.rearrange("(t p) d -> p t d", p=P)).then_inc(x_loaded, 16)
            sp.dma_start(src_i[:, :], src.rearrange("(p t) -> p t", p=P)).then_inc(idx_loaded, 16)
            sp.dma_start(dst_i[:, :], dst.rearrange("(p t) -> p t", p=P)).then_inc(idx_loaded, 16)

            def load_rows(slot, v, name):
                sp.dma_start(rows[:, slot, :], row(v)).then_inc(rows_loaded[name], 16)

            def load_half(q):
                if q >= 2:
                    sp.wait_ge(w_lo, q - 1)
                w, h = half_of[q]
                sp.dma_start(wraw[q % 2][:, :, :], w.rearrange("(k p) n -> p k n", p=128)
                             [:, :, h * HALF:(h + 1) * HALF]).then_inc(raw_loaded[q % 2], 16)

            load_half(0)
            load_rows(0, b1s, 'gat1')
            load_rows(1, b1d, 'gat1')
            load_rows(2, attn1, 'gat1')
            load_half(1)
            sp.dma_start(qk_bias[:, :], qk_bcols).then_inc(small_loaded, 16)
            sp.dma_start(gate_b[:, :], gate_bias.rearrange("(a d) -> a d", a=1).to_broadcast([P, 8])).then_inc(small_loaded, 16)
            sp.dma_start(gate_w_raw[:, :, :], gate_wT.rearrange("(k p) n -> p k n", p=128)).then_inc(small_loaded, 16)

            def fill(l, cs):
                for c in cs:
                    sp.dma_start(cell_rows[l][c].rearrange("p (h s) -> p h s", s=N),
                                 neg[:, :].unsqueeze(1).to_broadcast([P, HL[l], N])).then_inc(filled, 16)

            load_half(2)
            sp.wait_ge(neg_ready, 1)
            fill(0, (0,))
            load_half(3)
            fill(0, range(1, T))
            fill(1, range(T))

            def store_tables(l):
                sp.wait_ge(mm_used, 20 * l + 10)
                sp.dma_start(table_src[l].rearrange("(t p) d -> p t d", p=P), fs[:, :, :]).then_inc(tables_written, 16)
                sp.wait_ge(mm_used, 20 * l + 20)
                sp.dma_start(table_dst[l].rearrange("(t p) d -> p t d", p=P), fd_stage[:, :, :]).then_inc(tables_written, 16)

            def load_logits(l):
                sp.wait_ge(scattered[l], 16 * ET)
                bufs = [dl1[0], dl1[1]] if l == 0 else [dl2a, dl2b]
                if l == 0:
                    sp.wait_ge(edge_done[0], ET)
                    sp.wait_ge(hot_used, ET)
                for c in range(T):
                    if c >= 2:
                        sp.wait_ge(exp_ready[l], (c - 1) * HL[l])
                    sp.dma_start(bufs[c % 2][:, :], cell_rows[l][c]).then_inc(dl_loaded[l][c % 2], 16)

            store_tables(0)
            load_rows(0, ln1_w, 'ln1')
            load_rows(1, ln1_b, 'ln1')
            load_logits(0)
            load_rows(2, attno, 'attn2')
            sp.wait_ge(ln_done, 2)
            load_rows(0, bos, 'gat2')
            load_rows(1, bod, 'gat2')
            for q in range(4, 8):
                if q == 4:
                    sp.wait_ge(out_ready[0], T)
                load_half(q)
            store_tables(1)
            load_rows(0, lno_w, 'ln2')
            load_rows(1, lno_b, 'ln2')
            load_rows(3, proj_b, 'proj')
            sp.wait_ge(tables_written, 64)
            sp.dma_start(pmt[0:MD, :], proj_matT).then_inc(mixw_loaded, 16)
            sp.dma_start(pmt[MD:128, :], proj_matT).then_inc(mixw_loaded, 16)
            sp.dma_start(v_row[:, :], v_brow).then_inc(mixw_loaded, 16)
            qkv_pairs = qkv_wT.rearrange("(k p) (s r m) -> r p k s m", p=128, s=3, m=128)
            for r in range(KC):
                if r >= 1:
                    sp.wait_ge(mixw_used, r)
                for s in range(3):
                    sp.dma_start(mix_w[:, :, s * 128:(s + 1) * 128], qkv_pairs[r][:, :, s, :]).then_inc(mixw_loaded, 16)
            sp.wait_ge(edge_done[1], ET)
            sp.wait_ge(mixo_done, 1)
            load_half(8)
            load_half(9)
            sp.wait_ge(w_lo, 10)
            load_logits(1)
            sp.wait_ge(out_ready[1], T)
            sp.wait_ge(mm_used, 50)
            sp.dma_start(fs[:, :, :], x.rearrange("(t p) d -> p t d", p=P)).then_inc(xagain_loaded, 16)

            def load_piece(e, q):
                sp.dma_start(eraw[:, q % 3, :], moe_w[bass.ds(e, 1) if not isinstance(e, int) else slice(e, e + 1), q, :, :]
                             .rearrange("a p n -> (a p) n")).then_inc(eraw_loaded[q % 3], 16)

            sp.wait_ge(tr_lo, 4 * TR)
            sp.wait_ge(gate_full, 1)
            for q in range(6):
                if q >= 3:
                    sp.wait_ge(e_lo, q - 2)
                load_piece(0, q)
            with sp.Fori(1, EXPERTS) as e:
                for q in range(6):
                    sp.wait_ge(e_lo, 6 * e + q - 2)
                    load_piece(e, q)
            sp.wait_ge(down_used, EXPERTS * 10)
            sp.dma_start(out.rearrange("(t p) d -> p t d", p=P), x2).then_inc(out_stored, 16)
            sp.wait_ge(out_stored, 16)

        @block.gpsimd
        def _(pool):
            pool.memset(ident[:, :], 0.0).then_inc(const_ready, 1)
            pool.wait_ge(const_ready, 1)
            pool.affine_select(out=ident[:, :], in_=ident[:, :], compare_op=ALU.not_equal, fill=1.0, base=0,
                               pattern=[[-1, 128]], channel_multiplier=1).then_inc(const_ready, 1)
            pool.iota(iota_i[:, :], pattern=[[1, TP]], base=0, channel_multiplier=0).then_inc(const_ready, 1)
            pool.memset(eps_ln[:, :], LN_EPS).then_inc(const_ready, 1)
            pool.memset(neg[:, :], NEG).then_inc(neg_ready, 1)

            def edges(l):
                pool.wait_ge(tables_written, 32 * (l + 1))
                pool.wait_ge(prep_done, 1)
                pool.wait_ge(filled, 160)

                def gather(j):
                    pool.indirect_dma_start(
                        out=ring_s[:, j, :], out_offset=None, in_=table_src[l],
                        in_offset=bass.IndirectOffsetOnAxis(ap=idx_cur[:, j, 0:1], axis=0)).then_inc(gathered[l][j], 16)
                    pool.indirect_dma_start(
                        out=ring_d[:, j, :], out_offset=None, in_=table_dst[l],
                        in_offset=bass.IndirectOffsetOnAxis(ap=idx_cur[:, j, 1:2], axis=0)).then_inc(gathered[l][j], 16)

                def scatter(j):
                    pool.indirect_dma_start(
                        out=dense_logits[l], out_offset=bass.IndirectOffsetOnAxis(ap=idx_cur[:, j, 2:3], axis=0),
                        in_=logits[:, j, 0:HL[l]], in_offset=None).then_inc(scattered[l], 16)

                for j in range(G):
                    gather(j)
                def gather_scatter(i, j):
                    pool.wait_ge(edge_done[l], G * i + j + 1)
                    pool.sem_inc(pool_turn, 1)
                    gather(j)
                    if not (isinstance(i, int) and i + j == 0):
                        pool.wait_ge(scattered[l], 16 * (G * i + j))
                    pool.sem_inc(pool_turn, 1)
                    scatter(j)

                for j in range(G):
                    gather_scatter(0, j)
                with pool.Fori(1, NG - 1) as i:
                    for j in range(G):
                        gather_scatter(i, j)
                for j in range(G):
                    pool.wait_ge(edge_done[l], G * (NG - 1) + j + 1)
                    pool.wait_ge(scattered[l], 16 * (G * (NG - 1) + j))
                    scatter(j)

            edges(0)
            pool.wait_ge(prep_done, 2)
            edges(1)

        @block.scalar
        def _(act):
            ticks = [0]

            def after(ins):
                ticks[0] += 1
                ins.then_inc(astep, 1)
                act.wait_ge(astep, ticks[0])

            def ln_sqrt(n):
                act.wait_ge(ln_var, n + 1)
                act.activation(std[:, :], mv[:, :, 1], ACT.Sqrt, bias=eps_ln[0:P, :]).then_inc(ln_std, 1)

            def transposed_hi(n, keep=False):
                for k in range(KC):
                    u = n * TR + k
                    a = 4 + 2 * (u % 2)
                    act.wait_ge(tr_full, u + 1)
                    act.copy(at[:, 0, k, 0:4 * P], ps[:, a, 0:4 * P])
                    act.copy(at[:, 0, k, 4 * P:N], ps[:, a + 1, 0:P]).then_inc(tr_hi, 1)

            def weights_hi(qs):
                for q in qs:
                    act.wait_ge(raw_loaded[q % 2], 16 * (q // 2 + 1))
                    if q >= 2:
                        act.wait_ge(mm_full, 5 * (q - 1))
                    act.copy(wp[q % 2][:, 0, :, :], wraw[q % 2][:, :, :]).then_inc(w_hi, 1)

            act.wait_ge(const_ready, 4)
            ln_sqrt(0)
            weights_hi([0, 1])
            transposed_hi(0)
            weights_hi([2, 3])
            act.wait_ge(hot_used, ET)
            for c in range(T):
                act.copy(counts[:, c, 0:512], ps[0:P, c, :])
                b, o = (5, c * 113) if c < 4 else (6, 0)
                last = act.copy(counts[:, c, 512:N], ps[0:P, b, o:o + 113])
            last.then_inc(counts_ready, 1)

            def dense(l):
                H = HL[l]
                bufs = [dl1[0], dl1[1]] if l == 0 else [dl2a, dl2b]
                ebufs = [dl1[2], dl1[3]] if l == 0 else [de2a, de2b]
                pt = dl1[4] if l == 0 else dpt2

                def exps(c):
                    act.wait_ge(max_ready[l], c + 1)
                    if c >= 2:
                        act.wait_ge(pt_full[l], gd_groups[l] * (c - 1))
                    lv = bufs[c % 2][:, :].rearrange("p (s h) -> p h s", h=H)
                    for h in range(H):
                        act.activation(ebufs[c % 2][:, h, :], lv[:, h, :], ACT.Exp,
                                       bias=mxv[:, c, h:h + 1]).then_inc(exp_ready[l], 1)

                def copies(c):
                    for g in range(gd_groups[l]):
                        act.wait_ge(pt_full[l], gd_groups[l] * c + g + 1)
                        if g == 0 and c >= 1:
                            act.wait_ge(agg_full[l], c)
                        n = min(4, T * H - 4 * g)
                        act.copy(pt[:, 4 * g * P:(4 * g + n) * P], ps[0:P, g % 4, 0:n * P]).then_inc(pt_copied[l], 1)

                exps(0)
                for c in range(T):
                    copies(c)
                    if c + 1 < T:
                        exps(c + 1)
                    act.wait_ge(elu_min[l], c + 1)
                    act.activation(elu_m, elu_m, ACT.Exp).then_inc(elu_exp[l], 1)

            dense(0)
            ln_sqrt(1)
            weights_hi([4, 5])
            transposed_hi(1)
            weights_hi([6, 7])

            act.wait_ge(edge_done[1], 1)
            U = [0]

            def unit(outs, func=ACT.Identity, **kw):
                act.wait_ge(mix_full, U[0] + 1)
                for o, s in outs:
                    last = act.activation(o, s, func, **kw)
                last.then_inc(mix_used, 1)
                U[0] += 1

            act.wait_ge(tables_written, 64)
            for r in range(KC):
                for which, dstt in ((0, mix_qt), (1, mix_kt)):
                    for a, b in ((0, 313), (313, N)):
                        unit([(dstt[:, a:b], ps[:, U[0] % 4, 0:b - a])], bias=qk_bias[:, which * KC + r:which * KC + r + 1])
                unit([(mix_v[:, 0:4, :, 0:MD], ps[0:P, U[0] % 4, :].rearrange("p (t h d) -> p t h d", t=4, h=2))])
                unit([(mix_v[:, 4, :, 0:MD], ps[0:P, U[0] % 4, 0:128].rearrange("p (h d) -> p h d", h=2))])
                for h in range(2):
                    for t in (0, 2, 4):
                        n = min(2, T - t)
                        v = mix_kp[:, t:t + n, :]
                        if h == 1 or r >= 1:
                            act.wait_ge(mix_step, 2 * (2 * r + h))
                        act.wait_ge(mix_full, U[0] + 1)
                        after(act.activation(v, ps[0:P, U[0] % 4, 0:n * MF].rearrange("p (t m) -> p t m", m=MF),
                                             ACT.Relu, scale=1.0 / 16))
                        act.activation(v, v, ACT.Copy, bias=1e-3).then_inc(mix_used, 1)
                        U[0] += 1
                    for m in range(2):
                        for a, b in ((0, 313), (313, N)):
                            v = mix_qp[:, m, a:b]
                            act.wait_ge(mix_full, U[0] + 1)
                            after(act.activation(v, ps[:, U[0] % 4, 0:b - a], ACT.Relu, scale=1.0 / 16))
                            act.activation(v, v, ACT.Copy, bias=1e-3).then_inc(mix_used, 1)
                            U[0] += 1
                    act.wait_ge(mix_step, 2 * (2 * r + h) + 1)
                    act.copy(mix_kv[:, h, :, :], ps[:, 4, 0:2 * (MD + 1)].rearrange("p (m d) -> p m d", m=2)).then_inc(mix_used, 1)
                    act.wait_ge(mix_step, 2 * (2 * r + h) + 2)
                    act.copy(mix_out[:, :, 2 * r + h, :], ps[0:P, 6, 0:T * (MD + 1)].rearrange("p (t d) -> p t d", t=T)).then_inc(mix_used, 1)

            weights_hi([8, 9])
            transposed_hi(2)
            dense(1)
            ln_sqrt(2)
            act.wait_ge(small_loaded, 48)
            act.copy(gate_w_hi[:, :, :], gate_w_raw[:, :, :]).then_inc(gw_hi, 1)
            ln_sqrt(3)
            transposed_hi(3)
            act.wait_ge(gate_full, 1)
            act.activation(gate_s[:, :, :], ps[0:P, 0, 0:T * 8].rearrange("p (t e) -> p t e", t=T), ACT.Exp,
                           scale=-1.0).then_inc(gate_exp, 1)

            def split_hi(e, qs):
                for q in qs:
                    act.wait_ge(eraw_loaded[q % 3], 32 * e + 16 * (q // 3 + 1))
                    m, h = q // 2, q % 2
                    act.copy(we[:, 2 * m, h * PIECE:(h + 1) * PIECE], eraw[:, q % 3, :]).then_inc(e_hi, 1)

            def expert(e, first):
                if not first:
                    act.wait_ge(up_full, IC * e)
                split_hi(e, range(4))
                if not first:
                    act.wait_ge(down_full, 10 * e)
                split_hi(e, (4, 5))
                for j in range(IC):
                    a = 4 * (j % 2)
                    act.wait_ge(up_full, IC * e + j + 1)
                    if not first or j >= 2:
                        act.wait_ge(hid_lo, IC * e + j - 1)
                    act.activation(silu[:, j % 2, 0:314], ps[:, a, 0:314], ACT.Silu)
                    act.activation(silu[:, j % 2, 314:TP], ps[:, a + 1, 0:312], ACT.Silu).then_inc(silu_done, 1)
                    act.wait_ge(hid_f, IC * e + j + 1)
                    act.copy(hid[:, 0, j, :], silu[:, j % 2, :]).then_inc(hid_hi, 1)

            expert(0, True)
            with act.Fori(1, EXPERTS) as e:
                expert(e, False)

        @block.vector
        def _(dve):
            ticks = [0]

            def after(ins):
                ticks[0] += 1
                ins.then_inc(step, 1)
                dve.wait_ge(step, ticks[0])

            def layer_norm(n, srct, dstt, wb=None):
                for t in range(T):
                    for h in range(2):
                        last = dve.bn_stats(stats[:, t, h, :], srct[:, t, h * HALF:(h + 1) * HALF])
                after(last)
                for t in range(T):
                    last = dve.bn_aggr(mv[:, t, :], stats[:, t, :, :].rearrange("p a b -> p (a b)"))
                last.then_inc(ln_var, 1)
                dve.wait_ge(ln_std, n + 1)
                after(dve.reciprocal(rstd[:, :], std[:, :]))
                for t in range(T):
                    last = dve.tensor_scalar(dstt[:, t, :], srct[:, t, :], mv[:, t, 0:1], rstd[:, t:t + 1],
                                             ALU.subtract, ALU.mult)
                if wb is None:
                    last.then_inc(ln_done, 1)
                    dve.wait_ge(ln_done, n + 1)
                    return
                after(last)
                for op, s in ((ALU.mult, 0), (ALU.add, 1)):
                    for t in range(T):
                        last = dve.tensor_tensor(dstt[:, t, :], dstt[:, t, :], rows[:, s, :], op)
                    if s == 0:
                        after(last)
                last.then_inc(ln_done, 1)
                dve.wait_ge(ln_done, n + 1)

            def transposed_lo(n):
                for k in range(KC):
                    u = n * TR + k
                    a = 4 + 2 * (u % 2)
                    dve.wait_ge(tr_hi, u + 1)
                    if n == 0:
                        dve.tensor_copy(xt_v[:, k, 0:4 * P], ps[:, a, 0:4 * P])
                        dve.tensor_copy(xt_v[:, k, 4 * P:N], ps[:, a + 1, 0:P])
                    dve.tensor_tensor(at[:, 1, k, 0:4 * P], ps[:, a, 0:4 * P], at[:, 0, k, 0:4 * P].bitcast(F32), ALU.subtract)
                    dve.tensor_tensor(at[:, 1, k, 4 * P:N], ps[:, a + 1, 0:P], at[:, 0, k, 4 * P:N].bitcast(F32),
                                      ALU.subtract).then_inc(tr_lo, 1)

            def weights_lo(qs):
                for q in qs:
                    dve.wait_ge(w_hi, q + 1)
                    dve.tensor_tensor(wp[q % 2][:, 1, :, :], wraw[q % 2][:, :, :], wp[q % 2][:, 0, :, :].bitcast(F32),
                                      ALU.subtract).then_inc(w_lo, 1)

            def products_out(q, dest, bias_row, name):
                h = q % 2
                dve.wait_ge(rows_loaded[name], 48 if name == "gat1" else 32 if name == "gat2" else 16)
                for t in range(T):
                    u = 5 * q + t
                    dve.wait_ge(mm_full, u + 1)
                    dve.tensor_tensor(dest[:, t, h * HALF:(h + 1) * HALF], ps[0:P, u % 4, 0:HALF],
                                      rows[:, bias_row, h * HALF:(h + 1) * HALF], ALU.add).then_inc(mm_used, 1)

            def first_indices():
                dve.tensor_copy(idx_cur[:, :, 0], src_i[:, 0:G])
                dve.tensor_copy(idx_cur[:, :, 1], dst_i[:, 0:G]).then_inc(prep_done, 1)

            dve.wait_ge(idx_loaded, 32)
            dve.wait_ge(const_ready, 3)
            dve.tensor_copy(iota_h[:, :], iota_i[:, :])
            dve.tensor_copy(src_f[:, :], src_i[:, :])
            dve.tensor_copy(dst_f[:, :], dst_i[:, :])
            dve.memset(idx_all[:, ET - G:ET, 0:2], 0)
            dve.tensor_copy(idx_all[:, 0:ET - G, 0], src_i[:, G:ET])
            dve.tensor_copy(idx_all[:, 0:ET - G, 1], dst_i[:, G:ET])
            dve.memset(ones_row[:, :], 1.0)
            after(dve.memset(cw[:, :, 8:9], 1.0))
            after(dve.scalar_tensor_tensor(out=idx_all[:, :, 2], in0=dst_f[:, :], scalar=float(N), in1=src_f[:, :],
                                           op0=ALU.mult, op1=ALU.add))
            first_indices()

            dve.wait_ge(x_loaded, 16)
            layer_norm(0, b1, b1)
            weights_lo([0, 1])
            transposed_lo(0)
            products_out(0, fs, 0, "gat1")
            weights_lo([2])
            products_out(1, fs, 0, "gat1")
            weights_lo([3])
            products_out(2, fd_stage, 1, "gat1")
            products_out(3, fd_stage, 1, "gat1")

            def edges(l):
                H = HL[l]
                DH = D // H
                per = 2
                base = ticks[0]
                dve.wait_ge(prep_done, l + 1)
                dve.wait_ge(tables_written, 32 * (l + 1))
                if l == 1:
                    dve.wait_ge(rows_loaded["attn2"], 16)

                def tile(i, j, first):
                    t = i * G + j
                    one = slice(t, t + 1) if isinstance(t, int) else bass.ds(t, 1)
                    n = base + per * t
                    if l == 0:
                        if not first:
                            dve.wait_ge(hot_used, t - G + 1)
                        dve.tensor_scalar(hot_s[:, j, :], iota_h[0:P, :], src_f[:, one], None, ALU.is_equal)
                        dve.tensor_scalar(hot_d[:, j, :], iota_h[0:P, :], dst_f[:, one], None, ALU.is_equal).then_inc(hot_ready, 1)
                    dve.wait_ge(gathered[l][j], 32 * (i + 1))
                    if not first:
                        dve.wait_ge(scattered[l], 16 * (t - G + 1))
                    dve.tensor_copy(idx_cur[:, j, :], idx_all[:, one, :].rearrange("p a b -> p (a b)"))
                    dve.tensor_tensor(ring_s[:, j, :], ring_s[:, j, :], ring_d[:, j, :], ALU.add).then_inc(step, 1)
                    dve.wait_ge(step, n + 1)
                    dve.scalar_tensor_tensor(out=ring_s[:, j, :], in0=ring_s[:, j, :], scalar=0.2, in1=ring_s[:, j, :],
                                             op0=ALU.mult, op1=ALU.max).then_inc(step, 1)
                    dve.wait_ge(step, n + 2)
                    for h in range(H):
                        last = dve.tensor_tensor_reduce(ring_d[:, j, h * DH:(h + 1) * DH], ring_s[:, j, h * DH:(h + 1) * DH],
                                                        rows[:, 2, h * DH:(h + 1) * DH], 1.0, 0.0, ALU.mult, ALU.add,
                                                        logits[:, j, h:h + 1])
                    last.then_inc(edge_done[l], 1)

                for j in range(G):
                    tile(0, j, True)
                with dve.Fori(1, NG) as i:
                    for j in range(G):
                        tile(i, j, False)
                ticks[0] = base + per * ET

            edges(0)

            def dense(l, dest):
                H = HL[l]
                DH = D // H
                bufs = [dl1[0], dl1[1]] if l == 0 else [dl2a, dl2b]
                ebufs = [dl1[2], dl1[3]] if l == 0 else [de2a, de2b]

                def maxima(c):
                    dve.wait_ge(dl_loaded[l][c % 2], 16 * (c // 2 + 1))
                    lv = bufs[c % 2][:, :].rearrange("p (s h) -> p h s", h=H)
                    after(dve.tensor_reduce(mxv[:, c, 0:H], lv, AX.X, ALU.max))
                    dve.tensor_scalar(mxv[:, c, 0:H], mxv[:, c, 0:H], -1.0, None, ALU.mult).then_inc(max_ready[l], 1)

                maxima(0)
                for c in range(T):
                    for h in range(H):
                        dve.wait_ge(exp_ready[l], H * c + h + 1)
                        last = dve.tensor_tensor_reduce(ebufs[c % 2][:, h, :], ebufs[c % 2][:, h, :], counts[:, c, :],
                                                        1.0, 0.0, ALU.mult, ALU.add, den[:, c, h:h + 1])
                    last.then_inc(probs_ready[l], 1)
                    if c + 1 < T:
                        maxima(c + 1)
                    dve.wait_ge(probs_ready[l], c + 1)
                    after(dve.tensor_scalar(rden[:, c, 0:H], den[:, c, 0:H], 1e-30, None, ALU.max))
                    after(dve.reciprocal(rden[:, c, 0:H], rden[:, c, 0:H]))
                    dve.wait_ge(agg_full[l], c + 1)
                    pv = ps[0:P, 4 + 2 * (c % 2):6 + 2 * (c % 2), 0:HALF]
                    if H == 1:
                        last = dve.tensor_scalar(elu_o.rearrange("p (a d) -> p a d", a=2), pv, rden[:, c, 0:1], None, ALU.mult)
                    else:
                        for b in range(2):
                            last = dve.tensor_tensor(
                                elu_o[:, b * HALF:(b + 1) * HALF].rearrange("p (h d) -> p h d", d=DH),
                                pv[:, b, :].rearrange("p (h d) -> p h d", d=DH),
                                rden[:, c, 4 * b:4 * b + 4].unsqueeze(2).to_broadcast([P, 4, DH]), ALU.mult)
                    after(last)
                    dve.tensor_scalar(elu_m, elu_o, 0.0, None, ALU.min).then_inc(elu_min[l], 1)
                    dve.wait_ge(elu_exp[l], c + 1)
                    after(dve.scalar_tensor_tensor(out=elu_o, in0=elu_o, scalar=0.0, in1=elu_m, op0=ALU.max, op1=ALU.add))
                    if l == 0:
                        dve.scalar_tensor_tensor(out=dest[:, c, :], in0=elu_o, scalar=-1.0, in1=b1[:, c, :],
                                                 op0=ALU.add, op1=ALU.add).then_inc(out_ready[l], 1)
                    else:
                        dve.tensor_scalar(dest[:, c, :], elu_o, -1.0, None, ALU.add).then_inc(out_ready[l], 1)
                dve.wait_ge(out_ready[l], T)

            dve.wait_ge(counts_ready, 1)
            dve.wait_ge(scattered[0], 16 * ET)
            first_indices()
            dense(0, b1)
            dve.wait_ge(rows_loaded["ln1"], 32)
            layer_norm(1, b1, b1, wb=True)
            weights_lo([4, 5])
            transposed_lo(1)
            products_out(4, fs, 0, "gat2")
            weights_lo([6])
            products_out(5, fs, 0, "gat2")
            weights_lo([7])
            products_out(6, fd_stage, 1, "gat2")
            products_out(7, fd_stage, 1, "gat2")
            dve.memset(mix_v[:, :, :, MD:MD + 1], 1.0).then_inc(prep_done, 1)
            edges(1)

            dve.wait_ge(mix_used, MIX_USED_TOTAL)
            after(dve.reciprocal(mix_rden[:, :, :], mix_out[:, :, :, MD]))
            for t in range(T):
                last = dve.tensor_tensor(b1[:, t, :].rearrange("p (h d) -> p h d", d=MD), mix_out[:, t, :, 0:MD],
                                         mix_rden[:, t, :].unsqueeze(2).to_broadcast([P, MH, MD]), ALU.mult)
            last.then_inc(mixo_done, 1)
            weights_lo([8, 9])
            transposed_lo(2)
            products_out(8, x2, 3, "proj")
            products_out(9, x2, 3, "proj")
            dense(1, gnn)
            dve.wait_ge(rows_loaded["ln2"], 32)
            layer_norm(2, gnn, gnn, wb=True)
            dve.wait_ge(mm_used, 50)
            dve.wait_ge(xagain_loaded, 16)
            for t in range(T):
                last = dve.tensor_tensor(x2[:, t, :], x2[:, t, :], gnn[:, t, :], ALU.add)
            after(last)
            for t in range(T):
                last = dve.tensor_tensor(x2[:, t, :], x2[:, t, :], fs[:, t, :], ALU.add)
            after(last)
            dve.wait_ge(gw_hi, 1)
            dve.tensor_tensor(gate_w_lo[:, :, :], gate_w_raw[:, :, :], gate_w_hi[:, :, :].bitcast(F32), ALU.subtract).then_inc(gw_lo, 1)
            layer_norm(3, x2, b1)
            dve.memset(at[:, :, :, N:TP].bitcast(F32), 0.0)
            transposed_lo(3)

            def cmp(o, a, b, op):
                after(dve.tensor_tensor(o, a, b, op))

            dve.wait_ge(gate_exp, 1)
            after(dve.tensor_scalar(gate_s[:, :, :], gate_s[:, :, :], 1.0, None, ALU.add))
            after(dve.reciprocal(gate_s[:, :, :], gate_s[:, :, :]))
            after(dve.tensor_tensor(gate_k[:, :, :], gate_s[:, :, :], gate_b[:, :].unsqueeze(1).to_broadcast([P, T, 8]), ALU.add))
            pairs = gate_k[:, :, :].rearrange("p t (g e) -> p t g e", e=2)
            after(dve.tensor_tensor(gate_g[:, :, :], pairs[:, :, :, 0], pairs[:, :, :, 1], ALU.add))

            def ranks(score, n):
                after(dve.memset(gate_r[:, :, 0:n], 0.0))
                for i in range(n):
                    o = score[:, :, i:i + 1]
                    if i > 0:
                        dve.tensor_tensor(gate_t[:, :, 0:i], o.to_broadcast([P, T, i]), score[:, :, 0:i], ALU.is_gt)
                    if i + 1 < n:
                        dve.tensor_tensor(gate_t[:, :, i + 1:n], o.to_broadcast([P, T, n - i - 1]), score[:, :, i + 1:n], ALU.is_ge)
                    after(dve.memset(gate_t[:, :, i:i + 1], 0.0))
                    after(dve.tensor_tensor(gate_r[:, :, 0:n], gate_r[:, :, 0:n], gate_t[:, :, 0:n], ALU.add))

            ranks(gate_g, 4)
            after(dve.tensor_scalar(gate_t[:, :, 0:4], gate_r[:, :, 0:4], 2.0, -BIG, ALU.is_ge, ALU.mult))
            gt2 = gate_t[:, :, 0:4].unsqueeze(3).to_broadcast([P, T, 4, 2])
            after(dve.tensor_tensor(pairs, pairs, gt2, ALU.add))
            ranks(gate_k, 8)
            after(dve.tensor_scalar(gate_t[:, :, :], gate_r[:, :, :], 2.0, None, ALU.is_lt))
            after(dve.tensor_tensor(gate_s[:, :, :], gate_s[:, :, :], gate_t[:, :, :], ALU.mult))
            after(dve.tensor_reduce(gate_g[:, :, 0:1].rearrange("p t a -> p (t a)"), gate_s[:, :, :], AX.X, ALU.add))
            after(dve.tensor_scalar(gate_g[:, :, 0:1], gate_g[:, :, 0:1], 1e-6, None, ALU.add))
            after(dve.reciprocal(gate_g[:, :, 0:1], gate_g[:, :, 0:1]))
            after(dve.tensor_tensor(cw[:, :, 0:8], gate_s[:, :, :], gate_g[:, :, 0:1].to_broadcast([P, T, 8]), ALU.mult))

            def split_lo(e, qs):
                for q in qs:
                    dve.wait_ge(e_hi, 6 * e + q + 1)
                    m, h = q // 2, q % 2
                    part = slice(h * PIECE, (h + 1) * PIECE)
                    dve.tensor_tensor(we[:, 2 * m + 1, part], eraw[:, q % 3, :], we[:, 2 * m, part].bitcast(F32),
                                      ALU.subtract).then_inc(e_lo, 1)

            def down_out(e):
                for u in range(10):
                    t, h = u // 2, u % 2
                    w = cw[:, t, slice(e, e + 1) if isinstance(e, int) else bass.ds(e, 1)]
                    dve.wait_ge(down_full, 10 * e + u + 1)
                    if u > 0:
                        dve.wait_ge(down_used, 10 * e + u)
                    dve.scalar_tensor_tensor(out=x2[:, t, h * HALF:(h + 1) * HALF], in0=ps[0:P, u % 8, 0:HALF], scalar=w,
                                             in1=x2[:, t, h * HALF:(h + 1) * HALF], op0=ALU.mult, op1=ALU.add).then_inc(down_used, 1)

            def hidden(e, first):
                for j in range(IC):
                    a = 4 * (j % 2) + 2
                    dve.wait_ge(silu_done, IC * e + j + 1)
                    dve.tensor_tensor(silu[:, j % 2, 0:314], silu[:, j % 2, 0:314], ps[:, a, 0:314], ALU.mult)
                    dve.tensor_tensor(silu[:, j % 2, 314:TP], silu[:, j % 2, 314:TP], ps[:, a + 1, 0:312], ALU.mult).then_inc(hid_f, 1)
                    dve.wait_ge(hid_hi, IC * e + j + 1)
                    dve.tensor_tensor(hid[:, 1, j, :], silu[:, j % 2, :], hid[:, 0, j, :].bitcast(F32),
                                      ALU.subtract).then_inc(hid_lo, 1)

            split_lo(0, range(6))
            hidden(0, True)
            with dve.Fori(1, EXPERTS) as e:
                split_lo(e, range(4))
                down_out(e - 1)
                split_lo(e, (4, 5))
                hidden(e, False)
            down_out(EXPERTS - 1)

        @block.tensor
        def _(pe):
            def mm3(o, lt, r, start, stop):
                pe.matmul(o, lt(0), r(0), start=start, stop=False)
                pe.matmul(o, lt(0), r(1), start=False, stop=False)
                return pe.matmul(o, lt(1), r(0), start=False, stop=stop)

            def transposes(n, srct):
                for k in range(KC):
                    u = n * TR + k
                    a = 4 + 2 * (u % 2)
                    if u >= 2:
                        pe.wait_ge(tr_lo, u - 1)
                    for t in range(T):
                        o = ps[:, a, t * P:(t + 1) * P] if t < 4 else ps[:, a + 1, 0:P]
                        last = pe.transpose(o, srct[:, t, k * 128:(k + 1) * 128], ident[0:P, 0:P])
                    last.then_inc(tr_full, 1)

            def products(q):
                pe.wait_ge(w_lo, q + 1)
                for t in range(T):
                    u = 5 * q + t
                    if u >= 4:
                        pe.wait_ge(mm_used, u - 3)
                    for k in range(KC):
                        last = mm3(ps[0:P, u % 4, 0:HALF],
                                   lambda s: at[:, s, k, t * P:(t + 1) * P],
                                   lambda s: wp[q % 2][:, s, k, :], k == 0, k == KC - 1)
                    last.then_inc(mm_full, 1)

            pe.wait_ge(const_ready, 2)
            pe.wait_ge(ln_done, 1)
            transposes(0, b1)
            pe.wait_ge(tr_lo, TR)
            for q in range(4):
                products(q)

            pe.wait_ge(mm_used, 20)
            pe.wait_ge(prep_done, 1)
            pe.wait_ge(hot_ready, 1)
            cbanks = [(c, 0, 0, 512) for c in range(T)] + [(5 if c < 4 else 6, c * 113 if c < 4 else 0, 512, N) for c in range(T)]

            def count(j, start):
                for n, (b, o, s0, s1) in enumerate(cbanks):
                    c = n % T
                    last = pe.matmul(ps[0:P, b, o:o + s1 - s0], hot_d[:, j, c * P:(c + 1) * P], hot_s[:, j, s0:s1],
                                     start=start and (n <= 5 or n == 9), stop=False, skip_group_check=True)
                last.then_inc(hot_used, 1)

            count(0, True)
            for j in range(1, G):
                pe.wait_ge(hot_ready, j + 1)
                count(j, False)
            with pe.Fori(1, NG) as i:
                for j in range(G):
                    pe.wait_ge(hot_ready, G * i + j + 1)
                    count(j, False)

            def dense(l):
                H = HL[l]
                DH = D // H
                ebufs = [dl1[2], dl1[3]] if l == 0 else [de2a, de2b]
                pt = dl1[4] if l == 0 else dpt2
                for c in range(T):
                    pe.wait_ge(probs_ready[l], c + 1)
                    for g in range(gd_groups[l]):
                        if g >= 4:
                            pe.wait_ge(pt_copied[l], gd_groups[l] * c + g - 3)
                        for n in range(4 * g, min(4 * g + 4, H * T)):
                            h, s = n // T, n % T
                            last = pe.transpose(ps[0:P, g % 4, (n % 4) * P:(n % 4 + 1) * P],
                                                ebufs[c % 2][:, h, s * P:(s + 1) * P], ident[0:P, 0:P])
                        last.then_inc(pt_full[l], 1)
                    pe.wait_ge(pt_copied[l], gd_groups[l] * (c + 1))
                    if c >= 2:
                        pe.wait_ge(elu_min[l], c - 1)
                    for h in range(H):
                        for part in range(1 if H > 1 else 2):
                            w = DH if H > 1 else HALF
                            col = h * DH + part * HALF
                            o = ps[0:P, 4 + 2 * (c % 2) + col // HALF, col % HALF:col % HALF + w]
                            for s in range(T):
                                last = pe.matmul(o, pt[:, (h * T + s) * P:(h * T + s + 1) * P], fs[:, s, col:col + w],
                                                 start=s == 0, stop=s == T - 1)
                    last.then_inc(agg_full[l], 1)

            pe.wait_ge(counts_ready, 1)
            dense(0)
            pe.wait_ge(out_ready[0], T)
            pe.wait_ge(ln_done, 2)
            transposes(1, b1)
            pe.wait_ge(tr_lo, 2 * TR)
            for q in range(4, 8):
                products(q)

            pe.wait_ge(mm_used, 40)
            pe.wait_ge(prep_done, 3)
            U = [0]
            used = [0]
            slots = [0, 0, 0, 0]

            def open_unit():
                b = U[0] % 4
                if slots[b]:
                    pe.wait_ge(mix_used, slots[b])
                return b

            def close_unit(last, b):
                last.then_inc(mix_full, 1)
                U[0] += 1
                used[0] += 1
                slots[b] = used[0]

            for r in range(KC):
                pe.wait_ge(mixw_loaded, 48 * (r + 2))
                for s, _ in ((0, mix_qt), (1, mix_kt)):
                    for a, b_ in ((0, 313), (313, N)):
                        b = open_unit()
                        for k in range(KC):
                            last = pe.matmul(ps[:, b, 0:b_ - a], mix_w[:, k, s * 128:(s + 1) * 128], xt_v[:, k, a:b_],
                                             start=k == 0, stop=k == KC - 1)
                        close_unit(last, b)
                for ts in (range(4), range(4, 5)):
                    b = open_unit()
                    for n, t in enumerate(ts):
                        o = ps[0:P, b, n * 128:(n + 1) * 128]
                        pe.matmul(o, ones_row[:, :], v_row[:, r * 128:(r + 1) * 128], start=True, stop=False)
                        for k in range(KC):
                            last = pe.matmul(o, xt_v[:, k, t * P:(t + 1) * P], mix_w[:, k, 256:384], start=False, stop=k == KC - 1)
                    close_unit(last, b)
                MARK = used[0]
                for h in range(2):
                    hp = slice(h * MD, (h + 1) * MD)
                    if h == 0:
                        pe.wait_ge(mix_used, MARK)
                    for t0 in (0, 2, 4):
                        b = open_unit()
                        for t in range(t0, min(t0 + 2, T)):
                            last = pe.matmul(ps[0:P, b, (t - t0) * MF:(t - t0 + 1) * MF], mix_kt[hp, t * P:(t + 1) * P],
                                             pmt[hp, :], start=True, stop=True)
                            if h == 0 and t == 0:
                                last.then_inc(mixw_used, 1)
                        close_unit(last, b)
                    for m in range(2):
                        for a, b_ in ((0, 313), (313, N)):
                            b = open_unit()
                            last = pe.matmul(ps[:, b, 0:b_ - a], pmt[hp, m * 128:(m + 1) * 128], mix_qt[hp, a:b_], start=True, stop=True)
                            close_unit(last, b)
                    pe.wait_ge(mix_used, used[0])
                    for m in range(2):
                        for t in range(T):
                            last = pe.matmul(ps[:, 4, m * (MD + 1):(m + 1) * (MD + 1)], mix_kp[:, t, m * 128:(m + 1) * 128],
                                             mix_v[:, t, h, :], start=t == 0, stop=t == T - 1)
                    last.then_inc(mix_step, 1)
                    used[0] += 1
                    pe.wait_ge(mix_used, used[0])
                    for t in range(T):
                        for m in range(2):
                            last = pe.matmul(ps[0:P, 6, t * (MD + 1):(t + 1) * (MD + 1)], mix_qp[:, m, t * P:(t + 1) * P],
                                             mix_kv[:, h, m, :], start=m == 0, stop=m == 1)
                    last.then_inc(mix_step, 1)
                    used[0] += 1
            assert used[0] == MIX_USED_TOTAL

            pe.wait_ge(mixo_done, 1)
            transposes(2, b1)
            pe.wait_ge(tr_lo, 3 * TR)
            for q in (8, 9):
                products(q)
            pe.wait_ge(mm_used, 50)
            dense(1)
            pe.wait_ge(ln_done, 4)
            transposes(3, b1)
            pe.wait_ge(tr_lo, 4 * TR)
            pe.wait_ge(gw_lo, 1)
            for t in range(T):
                for k in range(KC):
                    last = mm3(ps[0:P, 0, t * 8:(t + 1) * 8], lambda s: at[:, s, k, t * P:(t + 1) * P],
                               lambda s: (gate_w_hi, gate_w_lo)[s][:, k, :], k == 0, k == KC - 1)
            last.then_inc(gate_full, 1)
            pe.wait_ge(gate_exp, 1)

            w13 = [[we[:, 2 * m + s, :].rearrange("p (k i) -> p k i", i=INTER) for s in range(2)] for m in range(2)]
            w2v = [we[:, 4 + s, :].rearrange("p (k d) -> p k d", d=D) for s in range(2)]

            def expert(e, first):
                pe.wait_ge(e_lo, 6 * e + 4)
                for j in range(IC):
                    if j >= 2:
                        pe.wait_ge(hid_f, IC * e + j - 1)
                    elif not first:
                        pe.wait_ge(down_used, 10 * e - (0 if j == 0 else 2))
                    for m in range(2):
                        for n, (a, b_) in enumerate(((0, 314), (314, TP))):
                            o = ps[:, 4 * (j % 2) + 2 * m + n, 0:b_ - a]
                            for k in range(KC):
                                last = mm3(o, lambda s: w13[m][s][:, k, j * 128:(j + 1) * 128],
                                           lambda s: at[:, s, k, a:b_], k == 0, k == KC - 1)
                    last.then_inc(up_full, 1)
                pe.wait_ge(e_lo, 6 * e + 6)
                pe.wait_ge(hid_f, IC * e + IC - 1)
                for us in (range(4), range(4, 8), range(8, 10)):
                    for k in range(IC):
                        if us[0] == 0:
                            pe.wait_ge(hid_lo, IC * e + k + 1)
                        for u in us:
                            t, h = u // 2, u % 2
                            if u >= 8 and k == 0:
                                pe.wait_ge(down_used, 10 * e + u - 7)
                            last = mm3(ps[0:P, u % 8, 0:HALF], lambda s: hid[:, s, k, t * P:(t + 1) * P],
                                       lambda s: w2v[s][:, k, h * HALF:(h + 1) * HALF], k == 0, k == IC - 1)
                            if k == IC - 1:
                                last.then_inc(down_full, 1)

            expert(0, True)
            with pe.Fori(1, EXPERTS) as e:
                expert(e, False)


MIX_USED_TOTAL = KC * (6 + 2 * (3 + 4 + 2))


_ORDER = ['x', 'src', 'dst', 'W1s', 'b1s', 'W1d', 'b1d', 'attn1', 'ln1_w', 'ln1_b', 'Wos', 'bos', 'Wod', 'bod',
          'attno', 'lno_w', 'lno_b', 'qkv_wT', 'qk_bcols', 'v_brow', 'proj_wT', 'proj_b', 'proj_matT', 'gate_wT',
          'gate_bias', 'moe_w']


def lay_out(inputs):
    import numpy as np
    a = {k: np.asarray(v) for k, v in inputs.items()}
    g = {k: a['L0_gnn_' + k] for k in ('W1s', 'b1s', 'W1d', 'b1d', 'ln1_w', 'ln1_b', 'Wos', 'bos', 'Wod', 'bod', 'lno_w', 'lno_b')}
    g['attn1'] = a['L0_gnn_attn1'].reshape(-1)
    g['attno'] = a['L0_gnn_attno'].reshape(-1)
    g['x'], g['src'], g['dst'] = a['x'], a['src'], a['dst']
    g['qkv_wT'] = a['L0_mix_qkv_w'].T
    g['qk_bcols'] = a['L0_mix_qkv_b'][:2 * D].reshape(2 * KC, 128).T
    g['v_brow'] = a['L0_mix_qkv_b'][2 * D:].reshape(1, D)
    g['proj_wT'] = a['L0_mix_proj_w'].T
    g['proj_b'] = a['L0_mix_proj_b']
    g['proj_matT'] = a['L0_mix_proj_mat'].T
    g['gate_wT'] = a['L0_ffn_gate_weight'].T
    g['gate_bias'] = a['L0_ffn_gate_bias']

    def pieces(w, chunks):
        e, o, i = w.shape
        t = w.transpose(0, 2, 1).reshape(e, 2, chunks // 2, 128, o)
        return t.transpose(0, 1, 3, 2, 4).reshape(e, 2, 128, PIECE)

    cat = lambda w, s: np.concatenate([a['L0_ffn_' + w], a['L0_ffn_' + s][None]], 0)
    g['moe_w'] = np.concatenate([pieces(cat('w1', 'sw1'), KC), pieces(cat('w3', 'sw3'), KC),
                                 pieces(cat('w2', 'sw2'), IC)], 1)
    return {k: np.ascontiguousarray(g[k]) for k in _ORDER}


def kernel(**inputs):
    import numpy as _np
    import concourse.bacc as _bacc
    from concourse import mybir as _mybir
    from concourse.bass_utils import run_bass_kernel_spmd as _run

    nc = _bacc.Bacc("TRN2", target_bir_lowering=False, num_devices=1)
    laid = lay_out(inputs)
    arrays, args = {}, {}
    for name in _ORDER:
        v = laid[name]
        arrays[f"in_{name}_dram"] = v
        args[name] = nc.dram_tensor(f"in_{name}_dram", v.shape, _mybir.dt.from_np(v.dtype), kind="ExternalInput").ap()
    args['out'] = nc.dram_tensor("out_0_dram", (N, D), _mybir.dt.from_np(_np.dtype('float32')), kind="ExternalOutput").ap()
    build(nc, **args)
    r = _run(nc, [arrays], core_ids=[0])
    return r.results[0]["out_0_dram"]
```

```python
from contextlib import ExitStack

import concourse.bass as bass
from concourse import mybir

ACT = mybir.ActivationFunctionType
ALU = mybir.AluOpType
AX = mybir.AxisListType
F32 = mybir.dt.float32
F32R = mybir.dt.float32r
F16 = mybir.dt.float16
I32 = mybir.dt.int32

N = 625
P = 125
T = N // P
D = 768
KC = D // 128
HALF = D // 2
TP = 626
EDGES = 10625
ET = EDGES // P
G = 5
NG = ET // G
HEADS1 = 8
DX = D + HEADS1
MH = 12
MD = 64
MF = 256
EXPERTS = 9
INTER = 512
IC = INTER // 128
LN_EPS = 1e-5
NEG = -1.0e30
BIG = 1.0e30
PIECE = 1536


def build(nc, x, src, dst, W1s, b1s, W1d, b1d, attn1, ln1_w, ln1_b, Wos, bos, Wod, bod, attno, lno_w,
          lno_b, qkv_wT, qk_bcols, v_brow, proj_wT, proj_b, proj_matT, gate_wT, gate_bias, moe_w, out):
    ctx = ExitStack()
    with ctx:
        def sem(name):
            return ctx.enter_context(nc.semaphore(name))

        def sb(name, shape, dt, stack=ctx):
            return stack.enter_context(nc.sbuf_tensor(name, shape, dt))

        def zone(tensors):
            with ExitStack() as here:
                return [sb(name, shape, dt, here) for name, shape, dt in tensors]

        def dram(name, shape):
            return nc.dram_tensor(name, shape, F32, kind="Internal").ap()

        WL = [DX, D]
        table_src = [dram(f"table_src{l}", (N, WL[l])) for l in range(2)]
        table_dst = [dram(f"table_dst{l}", (N, WL[l])) for l in range(2)]
        HL = [HEADS1, 1]
        dense_logits = [dram(f"dense_logits{l}", (N * N, HL[l])) for l in range(2)]

        ident = sb("ident", [128, 128], F32)
        iota_i = sb("iota_i", [128, TP], I32)
        iota_h = sb("iota_h", [128, TP], F16)
        src_i = sb("src_i", [P, ET], I32)
        dst_i = sb("dst_i", [P, ET], I32)
        src_f = sb("src_f", [P, ET], F32)
        dst_f = sb("dst_f", [P, ET], F32)
        idx_all = sb("idx_all", [P, ET, 3], I32)
        idx_cur = sb("idx_cur", [P, G, 3], I32)
        logits = sb("logits", [P, G, HEADS1], F32)
        stats = sb("stats", [P, T, 2, 6], F32)
        mv = sb("mv", [P, T, 2], F32)
        std = sb("std", [P, T], F32)
        rstd = sb("rstd", [P, T], F32)
        eps_ln = sb("eps_ln", [128, 1], F32)
        mxv = sb("mxv", [P, T, HEADS1], F32)
        den = sb("den", [P, T, HEADS1], F32)
        rden = sb("rden", [P, T, HEADS1], F32)
        mix_rden = sb("mix_rden", [P, T, MH], F32)
        qk_bias = sb("qk_bias", [128, 2 * KC], F32)
        cw = sb("cw", [P, T, EXPERTS], F32)
        gate_s = sb("gate_s", [P, T, 8], F32)
        gate_k = sb("gate_k", [P, T, 8], F32)
        gate_r = sb("gate_r", [P, T, 8], F32)
        gate_t = sb("gate_t", [P, T, 8], F32)
        gate_g = sb("gate_g", [P, T, 4], F32)
        gate_b = sb("gate_b", [P, 8], F32)
        gate_w_raw = sb("gate_w_raw", [128, KC, 8], F32)
        gate_w_hi = sb("gate_w_hi", [128, KC, 8], F32R)
        gate_w_lo = sb("gate_w_lo", [128, KC, 8], F32R)
        ones_row = sb("ones_row", [1, P], F32)

        counts, rows = zone([("counts", [P, T, N], F32), ("rows", [P, 4, D], F32)])
        (hid,) = zone([("hid", [128, 2, IC, TP], F32R)])
        sb("zone_d", [128, T * N + 4 * D], F32)
        fs = sb("fs", [P, T, DX], F32)
        (wraw8,) = zone([("wraw8", [128, KC, HALF], F32)])
        xt = sb("xt", [128, T * D], F32)
        xt_v = xt[:, 0:KC * N].rearrange("p (k n) -> p k n", k=KC)
        x2 = xt[0:P, :].rearrange("p (t d) -> p t d", t=T)
        (at,) = zone([("at", [128, 2, KC, TP], F32R)])
        mix_qt, mix_kt, mix_v, mix_kp, mix_kv = zone([
            ("mix_qt", [128, 2, N], F32), ("mix_kt", [128, 2, N], F32), ("mix_v", [P, 2, T, 2, MD + 1], F32),
            ("mix_kp", [P, 2, T, MF], F32), ("mix_kv", [128, 2, 2, MD + 1], F32)])
        dl1 = zone([("dl_a", [P, N * 8], F32), ("dl_b", [P, N * 8], F32), ("de_a", [P, 8, N], F32),
                    ("de_b", [P, 8, N], F32), ("dpt", [P, 40 * P], F32)])
        sb("zone_a", [128, 2 * KC * TP], F32)
        wp0, wp1, wraw0, wraw1, fd_stage = zone([
            ("wp0", [128, 2, KC, HALF], F32R), ("wp1", [128, 2, KC, HALF], F32R),
            ("wraw0", [128, KC, HALF], F32), ("wraw1", [128, KC, HALF], F32), ("fd_stage", [P, T, DX], F32)])
        ring_s, ring_d, hot_s, hot_d = zone([
            ("ring_s", [P, G, DX], F32), ("ring_d", [P, G, DX], F32),
            ("hot_s", [P, G, TP], F16), ("hot_d", [P, G, TP], F16)])
        _, mix_w, mix_out, pmt, v_row, mix_qp = zone([
            ("under_ring", [P, 2 * G * DX], F32), ("mix_w", [128, 2, KC, 3 * 128], F32),
            ("mix_out", [P, T, MH, MD + 1], F32), ("pmt", [128, MF], F32), ("v_row", [1, D], F32),
            ("mix_qp", [128, 2, 2, N], F32)])
        _, wraw9, wp8, wp9 = zone([
            ("under_ring2", [P, 2 * G * DX], F32), ("wraw9", [128, KC, HALF], F32),
            ("wp8", [128, 2, KC, HALF], F32R), ("wp9", [128, 2, KC, HALF], F32R)])
        wp, wraw = [wp0, wp1] * 4 + [wp8, wp9], [wraw0, wraw1] * 4 + [wraw8, wraw9]
        _, neg, elu_o_t, elu_m_t = zone([
            ("under_neg", [P, 6 * KC * HALF + T * DX], F32), ("neg", [P, N], F32),
            ("elu_o", [P, D], F32), ("elu_m", [P, D], F32)])
        dl2a, dl2b, de2a, de2b, dpt2, gnn, elu_m2 = zone([
            ("dl2_a", [P, N], F32), ("dl2_b", [P, N], F32), ("de2_a", [P, 1, N], F32), ("de2_b", [P, 1, N], F32),
            ("dpt2", [P, 5 * P], F32), ("gnn", [P, T, D], F32), ("elu_m2", [P, D], F32)])
        _, elu_o2 = zone([("under_elu2", [P, 2 * G * DX + 5 * KC * HALF], F32), ("elu_o2", [P, D], F32)])
        (we,) = zone([("we", [128, 6, 6 * INTER], F32R)])
        _, eraw, silu = zone([("under_we", [128, 6 * 6 * INTER], F32), ("eraw", [128, 3, PIECE], F32),
                              ("silu", [128, 2, TP], F32)])
        sb("zone_c", [128, 6 * 6 * INTER + 3 * PIECE + 2 * TP - T * D], F32)
        b1 = sb("b1", [P, T, D], F32)
        ps = ctx.enter_context(nc.psum_tensor("ps", [128, 8, 512], F32))

        x_loaded, idx_loaded, const_ready, prep_done = (sem(n) for n in
            ("x_loaded", "idx_loaded", "const_ready", "prep_done"))
        small_loaded = sem("small_loaded")
        rows_loaded = {name: sem("rows_" + name) for name in ("gat1", "ln1", "attn2", "gat2", "ln2", "proj")}
        ln_var, ln_std, ln_done = sem("ln_var"), sem("ln_std"), sem("ln_done")
        tr_full, tr_hi, tr_lo, xt_copied = sem("tr_full"), sem("tr_hi"), sem("tr_lo"), sem("xt_copied")
        raw_loaded = [sem(f"raw_loaded{i}") for i in range(2)]
        w_hi, w_lo = sem("w_hi"), sem("w_lo")
        mm_full, mm_used = sem("mm_full"), sem("mm_used")
        tables_written = sem("tables_written")
        pool_turn = sem("pool_turn")
        neg_ready, filled = sem("neg_ready"), sem("filled")
        gathered = [[sem(f"gathered{l}_{j}") for j in range(G)] for l in range(2)]
        ext_ready, z_ready, relu_ready = sem("ext_ready"), sem("z_ready"), sem("relu_ready")
        edge_done = [sem(f"edge_done{l}") for l in range(2)]
        scattered = [sem(f"scattered{l}") for l in range(2)]
        hot_ready, hot_used, counts_ready = sem("hot_ready"), sem("hot_used"), sem("counts_ready")
        dl_loaded = [[sem(f"dl_loaded{l}_{i}") for i in range(2)] for l in range(2)]
        max_ready = [sem(f"max_ready{l}") for l in range(2)]
        exp_ready = [sem(f"exp_ready{l}") for l in range(2)]
        probs_ready = [sem(f"probs_ready{l}") for l in range(2)]
        pt_full = [sem(f"pt_full{l}") for l in range(2)]
        pt_copied = [sem(f"pt_copied{l}") for l in range(2)]
        agg_full = [sem(f"agg_full{l}") for l in range(2)]
        elu_min = [sem(f"elu_min{l}") for l in range(2)]
        elu_exp = [sem(f"elu_exp{l}") for l in range(2)]
        out_ready = [sem(f"out_ready{l}") for l in range(2)]
        mixc_loaded = sem("mixc_loaded")
        mixw_loaded = [sem(f"mixw_loaded{i}") for i in range(2)]
        mix_full, mix_used = sem("mix_full"), sem("mix_used")
        mixr_done = sem("mixr_done")
        mixo_done = sem("mixo_done")
        xagain_loaded = sem("xagain_loaded")
        gate_full, gate_exp, gate_done = sem("gate_full"), sem("gate_exp"), sem("gate_done")
        gw_hi, gw_lo = sem("gw_hi"), sem("gw_lo")
        eraw_loaded = [sem(f"eraw_loaded{i}") for i in range(3)]
        e_hi, e_lo = sem("e_hi"), sem("e_lo")
        up_full, silu_done, hid_f, hid_hi, hid_lo = (sem(n) for n in
            ("up_full", "silu_done", "hid_f", "hid_hi", "hid_lo"))
        down_full, down_used = sem("down_full"), sem("down_used")
        out_stored = sem("out_stored")
        step = sem("step")
        astep = sem("astep")

        block = ctx.enter_context(nc.Block())
        TR = KC
        MM = 10
        cell_rows = [dense_logits[l].rearrange("(t p s) h -> t p (s h)", t=T, p=P) for l in range(2)]
        weights = [W1s, W1d, Wos, Wod, proj_wT]
        half_of = [(w, h) for w in weights for h in range(2)]
        gd_groups = [(HL[l] * T + 3) // 4 for l in range(2)]

        def row(v):
            return v.rearrange("(a d) -> a d", a=1).to_broadcast([P, D])

        @block.sync
        def _(sp):
            sp.dma_start(b1[:, :, :], x.rearrange("(t p) d -> p t d", p=P)).then_inc(x_loaded, 16)
            sp.dma_start(src_i[:, :], src.rearrange("(p t) -> p t", p=P)).then_inc(idx_loaded, 16)
            sp.dma_start(dst_i[:, :], dst.rearrange("(p t) -> p t", p=P)).then_inc(idx_loaded, 16)

            def load_rows(slot, v, name):
                sp.dma_start(rows[:, slot, :], row(v)).then_inc(rows_loaded[name], 16)

            def load_half(q):
                if q >= 2:
                    sp.wait_ge(w_lo, q - 1)
                w, h = half_of[q]
                sp.dma_start(wraw[q][:, :, :], w.rearrange("(k p) n -> p k n", p=128)
                             [:, :, h * HALF:(h + 1) * HALF]).then_inc(raw_loaded[q % 2], 16)

            load_half(0)
            load_rows(0, b1s, 'gat1')
            load_rows(1, b1d, 'gat1')
            load_rows(2, attn1, 'gat1')
            load_half(1)
            sp.dma_start(qk_bias[:, :], qk_bcols).then_inc(small_loaded, 16)
            sp.dma_start(gate_b[:, :], gate_bias.rearrange("(a d) -> a d", a=1).to_broadcast([P, 8])).then_inc(small_loaded, 16)
            sp.dma_start(gate_w_raw[:, :, :], gate_wT.rearrange("(k p) n -> p k n", p=128)).then_inc(small_loaded, 16)

            def fill(l, cs):
                for c in cs:
                    sp.dma_start(cell_rows[l][c].rearrange("p (h s) -> p h s", s=N),
                                 neg[:, :].unsqueeze(1).to_broadcast([P, HL[l], N])).then_inc(filled, 16)

            load_half(2)
            sp.wait_ge(neg_ready, 1)
            fill(0, (0,))
            load_half(3)
            fill(0, range(1, T))
            fill(1, range(T))

            def store_tables(l):
                sp.wait_ge(mm_used, 20 * l + 10)
                if l == 0:
                    sp.wait_ge(ext_ready, T)
                sp.dma_start(table_src[l].rearrange("(t p) d -> p t d", p=P), fs[:, :, 0:WL[l]]).then_inc(tables_written, 16)
                sp.wait_ge(mm_used, 20 * l + 20)
                if l == 0:
                    sp.wait_ge(ext_ready, 2 * T)
                sp.dma_start(table_dst[l].rearrange("(t p) d -> p t d", p=P), fd_stage[:, :, 0:WL[l]]).then_inc(tables_written, 16)

            def load_logits(l):
                sp.wait_ge(scattered[l], 16 * ET)
                bufs = [dl1[0], dl1[1]] if l == 0 else [dl2a, dl2b]
                sp.wait_ge(edge_done[l], ET)
                if l == 0:
                    sp.wait_ge(hot_used, ET)
                for c in range(T):
                    if c >= 2:
                        sp.wait_ge(exp_ready[l], (c - 1) * HL[l])
                    sp.dma_start(bufs[c % 2][:, :], cell_rows[l][c]).then_inc(dl_loaded[l][c % 2], 16)

            store_tables(0)
            load_rows(0, ln1_w, 'ln1')
            load_rows(1, ln1_b, 'ln1')
            load_logits(0)
            load_rows(2, attno, 'attn2')
            sp.wait_ge(ln_done, 2)
            load_rows(0, bos, 'gat2')
            load_rows(1, bod, 'gat2')
            for q in range(4, 8):
                if q == 4:
                    sp.wait_ge(out_ready[0], T)
                load_half(q)
            store_tables(1)
            load_rows(0, lno_w, 'ln2')
            load_rows(1, lno_b, 'ln2')
            load_rows(3, proj_b, 'proj')
            sp.wait_ge(tables_written, 64)
            sp.dma_start(pmt[0:MD, :], proj_matT).then_inc(mixc_loaded, 16)
            sp.dma_start(pmt[MD:128, :], proj_matT).then_inc(mixc_loaded, 16)
            sp.dma_start(v_row[:, :], v_brow).then_inc(mixc_loaded, 16)
            qkv_pairs = qkv_wT.rearrange("(k p) (s r m) -> r p k s m", p=128, s=3, m=128)
            for r in range(KC):
                if r >= 2:
                    sp.wait_ge(mix_full, mix_count("v", r - 2, 0))
                for s in range(3):
                    sp.dma_start(mix_w[:, r % 2, :, s * 128:(s + 1) * 128], qkv_pairs[r][:, :, s, :]).then_inc(mixw_loaded[r % 2], 16)
            sp.wait_ge(mix_full, mix_count("v", KC - 1, 0))
            load_half(8)
            load_half(9)
            load_logits(1)
            sp.wait_ge(out_ready[1], T)
            sp.wait_ge(mm_used, 50)
            sp.dma_start(fs[:, :, 0:D], x.rearrange("(t p) d -> p t d", p=P)).then_inc(xagain_loaded, 16)

            def load_piece(e, q):
                sp.dma_start(eraw[:, q % 3, :], moe_w[bass.ds(e, 1) if not isinstance(e, int) else slice(e, e + 1), q, :, :]
                             .rearrange("a p n -> (a p) n")).then_inc(eraw_loaded[q % 3], 16)

            sp.wait_ge(tr_lo, 4 * TR)
            sp.wait_ge(gate_full, 1)
            for q in range(6):
                if q >= 3:
                    sp.wait_ge(e_lo, q - 2)
                load_piece(0, q)
            with sp.Fori(1, EXPERTS) as e:
                for q in range(6):
                    sp.wait_ge(e_lo, 6 * e + q - 2)
                    load_piece(e, q)
            sp.wait_ge(down_used, EXPERTS * 10)
            sp.dma_start(out.rearrange("(t p) d -> p t d", p=P), x2).then_inc(out_stored, 16)
            sp.wait_ge(out_stored, 16)

        @block.gpsimd
        def _(pool):
            pool.memset(ident[:, :], 0.0).then_inc(const_ready, 1)
            pool.wait_ge(const_ready, 1)
            pool.affine_select(out=ident[:, :], in_=ident[:, :], compare_op=ALU.not_equal, fill=1.0, base=0,
                               pattern=[[-1, 128]], channel_multiplier=1).then_inc(const_ready, 1)
            pool.iota(iota_i[:, :], pattern=[[1, TP]], base=0, channel_multiplier=0).then_inc(const_ready, 1)
            pool.memset(eps_ln[:, :], LN_EPS).then_inc(const_ready, 1)
            pool.memset(neg[:, :], NEG).then_inc(neg_ready, 1)

            def edges(l):
                pool.wait_ge(tables_written, 32 * (l + 1))
                pool.wait_ge(prep_done, 1)
                pool.wait_ge(filled, 160)

                def gather(j):
                    pool.indirect_dma_start(
                        out=ring_s[:, j, 0:WL[l]], out_offset=None, in_=table_src[l],
                        in_offset=bass.IndirectOffsetOnAxis(ap=idx_cur[:, j, 0:1], axis=0)).then_inc(gathered[l][j], 16)
                    pool.indirect_dma_start(
                        out=ring_d[:, j, 0:WL[l]], out_offset=None, in_=table_dst[l],
                        in_offset=bass.IndirectOffsetOnAxis(ap=idx_cur[:, j, 1:2], axis=0)).then_inc(gathered[l][j], 16)

                def scatter(j):
                    pool.indirect_dma_start(
                        out=dense_logits[l], out_offset=bass.IndirectOffsetOnAxis(ap=idx_cur[:, j, 2:3], axis=0),
                        in_=logits[:, j, 0:HL[l]], in_offset=None).then_inc(scattered[l], 16)

                for j in range(G):
                    gather(j)
                def gather_scatter(i, j):
                    pool.wait_ge(edge_done[l], G * i + j + 1)
                    pool.sem_inc(pool_turn, 1)
                    gather(j)
                    if not (isinstance(i, int) and i + j == 0):
                        pool.wait_ge(scattered[l], 16 * (G * i + j))
                    pool.sem_inc(pool_turn, 1)
                    scatter(j)

                for j in range(G):
                    gather_scatter(0, j)
                with pool.Fori(1, NG - 1) as i:
                    for j in range(G):
                        gather_scatter(i, j)
                for j in range(G):
                    pool.wait_ge(edge_done[l], G * (NG - 1) + j + 1)
                    pool.wait_ge(scattered[l], 16 * (G * (NG - 1) + j))
                    scatter(j)

            edges(0)
            pool.wait_ge(prep_done, 2)
            edges(1)

        @block.scalar
        def _(act):
            ticks = [0]

            def after(ins):
                ticks[0] += 1
                ins.then_inc(astep, 1)
                act.wait_ge(astep, ticks[0])

            def ln_sqrt(n):
                act.wait_ge(ln_var, n + 1)
                act.activation(std[:, :], mv[:, :, 1], ACT.Sqrt, bias=eps_ln[0:P, :]).then_inc(ln_std, 1)

            def transposed_hi(n, keep=False):
                for k in range(KC):
                    u = n * TR + k
                    a = 4 + 2 * (u % 2)
                    act.wait_ge(tr_full, u + 1)
                    act.copy(at[:, 0, k, 0:4 * P], ps[:, a, 0:4 * P])
                    act.copy(at[:, 0, k, 4 * P:N], ps[:, a + 1, 0:P]).then_inc(tr_hi, 1)

            def weights_hi(qs):
                for q in qs:
                    act.wait_ge(raw_loaded[q % 2], 16 * (q // 2 + 1))
                    if q >= 2:
                        act.wait_ge(mm_full, 5 * (q - 1))
                    act.copy(wp[q][:, 0, :, :], wraw[q][:, :, :]).then_inc(w_hi, 1)

            act.wait_ge(const_ready, 4)
            ln_sqrt(0)
            weights_hi([0, 1])
            transposed_hi(0)
            weights_hi([2, 3])
            def relu(t, j):
                act.wait_ge(z_ready, t + 1)
                act.activation(ring_s[:, j, 0:D], ring_s[:, j, 0:D], ACT.Relu, scale=0.8).then_inc(relu_ready, 1)

            for j in range(G):
                relu(j, j)
            with act.Fori(1, NG) as i:
                for j in range(G):
                    relu(G * i + j, j)
            act.wait_ge(hot_used, ET)
            for c in range(T):
                act.copy(counts[:, c, 0:512], ps[0:P, c, :])
                b, o = (5, c * 113) if c < 4 else (6, 0)
                last = act.copy(counts[:, c, 512:N], ps[0:P, b, o:o + 113])
            last.then_inc(counts_ready, 1)

            def dense(l):
                H = HL[l]
                bufs = [dl1[0], dl1[1]] if l == 0 else [dl2a, dl2b]
                ebufs = [dl1[2], dl1[3]] if l == 0 else [de2a, de2b]
                pt = dl1[4] if l == 0 else dpt2

                def exps(c):
                    act.wait_ge(max_ready[l], c + 1)
                    if c >= 2:
                        act.wait_ge(pt_full[l], gd_groups[l] * (c - 1))
                    lv = bufs[c % 2][:, :].rearrange("p (s h) -> p h s", h=H)
                    for h in range(H):
                        act.activation(ebufs[c % 2][:, h, :], lv[:, h, :], ACT.Exp,
                                       bias=mxv[:, c, h:h + 1]).then_inc(exp_ready[l], 1)

                def copies(c):
                    for g in range(gd_groups[l]):
                        act.wait_ge(pt_full[l], gd_groups[l] * c + g + 1)
                        if g == 0 and c >= 1:
                            act.wait_ge(agg_full[l], c)
                        n = min(4, T * H - 4 * g)
                        act.copy(pt[:, 4 * g * P:(4 * g + n) * P], ps[0:P, g % 4, 0:n * P]).then_inc(pt_copied[l], 1)

                exps(0)
                for c in range(T):
                    copies(c)
                    if c + 1 < T:
                        exps(c + 1)
                    act.wait_ge(elu_min[l], c + 1)
                    elu_m = (elu_m_t, elu_m2)[l][:, :]
                    act.activation(elu_m, elu_m, ACT.Exp).then_inc(elu_exp[l], 1)

            dense(0)
            ln_sqrt(1)
            weights_hi([4, 5])
            transposed_hi(1)
            weights_hi([6, 7])

            act.wait_ge(edge_done[1], 1)
            act.wait_ge(tables_written, 64)

            def features(o, src):
                after(act.activation(o, src, ACT.Relu, scale=1.0 / 16))
                return act.activation(o, o, ACT.Copy, bias=1e-3)

            for n, (kind, r, h, i) in enumerate(MIX_STEPS):
                act.wait_ge(mix_full, n + 1)
                b, m = mix_bank(n), r % 2
                if kind in ("q", "k"):
                    which, dstt = (0, mix_qt) if kind == "q" else (1, mix_kt)
                    c0, c1 = MIX_COLS[i]
                    last = act.activation(dstt[:, m, c0:c1], ps[:, b, 0:c1 - c0], ACT.Identity,
                                          bias=qk_bias[:, which * KC + r:which * KC + r + 1])
                elif kind == "v":
                    t0, t1 = (0, 4) if i == 0 else (4, T)
                    last = act.copy(mix_v[:, m, t0:t1, :, 0:MD],
                                    ps[0:P, b, 0:(t1 - t0) * 128].rearrange("p (t h d) -> p t h d", h=2, d=MD))
                elif kind == "kp":
                    t0, t1 = 2 * i, min(2 * i + 2, T)
                    last = features(mix_kp[:, h, t0:t1, :], ps[0:P, b, 0:(t1 - t0) * MF].rearrange("p (t m) -> p t m", m=MF))
                elif kind == "qp":
                    c0, c1 = MIX_COLS[i % 2]
                    last = features(mix_qp[:, h, i // 2, c0:c1], ps[:, b, 0:c1 - c0])
                elif kind == "kv":
                    last = act.copy(mix_kv[:, h, :, :], ps[:, b, 0:2 * (MD + 1)].rearrange("p (m d) -> p m d", m=2))
                else:
                    last = act.copy(mix_out[:, :, 2 * r + h, :], ps[0:P, b, 0:T * (MD + 1)].rearrange("p (t d) -> p t d", t=T))
                last.then_inc(mix_used, 1)

            act.wait_ge(mixo_done, 1)
            weights_hi([8, 9])
            transposed_hi(2)
            dense(1)
            ln_sqrt(2)
            act.wait_ge(small_loaded, 48)
            act.copy(gate_w_hi[:, :, :], gate_w_raw[:, :, :]).then_inc(gw_hi, 1)
            ln_sqrt(3)
            transposed_hi(3)
            act.wait_ge(gate_full, 1)
            act.activation(gate_s[:, :, :], ps[0:P, 0, 0:T * 8].rearrange("p (t e) -> p t e", t=T), ACT.Exp,
                           scale=-1.0).then_inc(gate_exp, 1)

            def split_hi(e, qs):
                for q in qs:
                    act.wait_ge(eraw_loaded[q % 3], 32 * e + 16 * (q // 3 + 1))
                    m, h = q // 2, q % 2
                    act.copy(we[:, 2 * m, h * PIECE:(h + 1) * PIECE], eraw[:, q % 3, :]).then_inc(e_hi, 1)

            def expert(e, first):
                if not first:
                    act.wait_ge(up_full, IC * e)
                split_hi(e, range(4))
                if not first:
                    act.wait_ge(down_full, 10 * e)
                split_hi(e, (4, 5))
                for j in range(IC):
                    a = 4 * (j % 2)
                    act.wait_ge(up_full, IC * e + j + 1)
                    if not first or j >= 2:
                        act.wait_ge(hid_lo, IC * e + j - 1)
                    act.activation(silu[:, j % 2, 0:314], ps[:, a, 0:314], ACT.Silu)
                    act.activation(silu[:, j % 2, 314:TP], ps[:, a + 1, 0:312], ACT.Silu).then_inc(silu_done, 1)
                    act.wait_ge(hid_f, IC * e + j + 1)
                    act.copy(hid[:, 0, j, :], silu[:, j % 2, :]).then_inc(hid_hi, 1)

            expert(0, True)
            with act.Fori(1, EXPERTS) as e:
                expert(e, False)

        @block.vector
        def _(dve):
            ticks = [0]

            def after(ins):
                ticks[0] += 1
                ins.then_inc(step, 1)
                dve.wait_ge(step, ticks[0])

            def layer_norm(n, srct, dstt, wb=None):
                for t in range(T):
                    for h in range(2):
                        last = dve.bn_stats(stats[:, t, h, :], srct[:, t, h * HALF:(h + 1) * HALF])
                after(last)
                for t in range(T):
                    last = dve.bn_aggr(mv[:, t, :], stats[:, t, :, :].rearrange("p a b -> p (a b)"))
                last.then_inc(ln_var, 1)
                dve.wait_ge(ln_std, n + 1)
                after(dve.reciprocal(rstd[:, :], std[:, :]))
                for t in range(T):
                    last = dve.tensor_scalar(dstt[:, t, :], srct[:, t, :], mv[:, t, 0:1], rstd[:, t:t + 1],
                                             ALU.subtract, ALU.mult)
                if wb is None:
                    last.then_inc(ln_done, 1)
                    dve.wait_ge(ln_done, n + 1)
                    return
                after(last)
                for op, s in ((ALU.mult, 0), (ALU.add, 1)):
                    for t in range(T):
                        last = dve.tensor_tensor(dstt[:, t, :], dstt[:, t, :], rows[:, s, :], op)
                    if s == 0:
                        after(last)
                last.then_inc(ln_done, 1)
                dve.wait_ge(ln_done, n + 1)

            def transposed_lo(n):
                for k in range(KC):
                    u = n * TR + k
                    a = 4 + 2 * (u % 2)
                    dve.wait_ge(tr_hi, u + 1)
                    if n == 0:
                        dve.tensor_copy(xt_v[:, k, 0:4 * P], ps[:, a, 0:4 * P])
                        dve.tensor_copy(xt_v[:, k, 4 * P:N], ps[:, a + 1, 0:P])
                    dve.tensor_tensor(at[:, 1, k, 0:4 * P], ps[:, a, 0:4 * P], at[:, 0, k, 0:4 * P].bitcast(F32), ALU.subtract)
                    dve.tensor_tensor(at[:, 1, k, 4 * P:N], ps[:, a + 1, 0:P], at[:, 0, k, 4 * P:N].bitcast(F32),
                                      ALU.subtract).then_inc(tr_lo, 1)

            def weights_lo(qs):
                for q in qs:
                    dve.wait_ge(w_hi, q + 1)
                    dve.tensor_tensor(wp[q][:, 1, :, :], wraw[q][:, :, :], wp[q][:, 0, :, :].bitcast(F32),
                                      ALU.subtract).then_inc(w_lo, 1)

            def products_out(q, dest, bias_row, name, attention=False, tiles=range(T)):
                h = q % 2
                dve.wait_ge(rows_loaded[name], 48 if name == "gat1" else 32 if name == "gat2" else 16)
                for t in tiles:
                    u = 5 * q + t
                    dve.wait_ge(mm_full, u + 1)
                    dve.tensor_tensor(dest[:, t, h * HALF:(h + 1) * HALF], ps[0:P, u % 4, 0:HALF],
                                      rows[:, bias_row, h * HALF:(h + 1) * HALF], ALU.add).then_inc(mm_used, 1)
                    if attention:
                        dve.wait_ge(mm_used, u + 1)
                        DH = D // HEADS1
                        for a in range(4 * h, 4 * h + 4):
                            part = slice(a * DH, (a + 1) * DH)
                            last = dve.tensor_tensor_reduce(elu_o_t[:, part], dest[:, t, part], rows[:, 2, part], 0.2, 0.0,
                                                            ALU.mult, ALU.add, dest[:, t, D + a:D + a + 1])
                        if h == 1:
                            last.then_inc(ext_ready, 1)

            def first_indices():
                dve.tensor_copy(idx_cur[:, :, 0], src_i[:, 0:G])
                dve.tensor_copy(idx_cur[:, :, 1], dst_i[:, 0:G]).then_inc(prep_done, 1)

            dve.wait_ge(idx_loaded, 32)
            dve.wait_ge(const_ready, 3)
            dve.tensor_copy(iota_h[:, :], iota_i[:, :])
            dve.tensor_copy(src_f[:, :], src_i[:, :])
            dve.tensor_copy(dst_f[:, :], dst_i[:, :])
            dve.memset(idx_all[:, ET - G:ET, 0:2], 0)
            dve.tensor_copy(idx_all[:, 0:ET - G, 0], src_i[:, G:ET])
            dve.tensor_copy(idx_all[:, 0:ET - G, 1], dst_i[:, G:ET])
            dve.memset(ones_row[:, :], 1.0)
            after(dve.memset(cw[:, :, 8:9], 1.0))
            after(dve.scalar_tensor_tensor(out=idx_all[:, :, 2], in0=dst_f[:, :], scalar=float(N), in1=src_f[:, :],
                                           op0=ALU.mult, op1=ALU.add))
            first_indices()

            dve.wait_ge(x_loaded, 16)
            layer_norm(0, b1, b1)
            weights_lo([0, 1])
            transposed_lo(0)
            products_out(0, fs, 0, "gat1", attention=True)
            weights_lo([2])
            products_out(1, fs, 0, "gat1", attention=True)
            weights_lo([3])
            products_out(2, fd_stage, 1, "gat1", attention=True)
            products_out(3, fd_stage, 1, "gat1", attention=True)

            def edges_first():
                DH = D // HEADS1
                dve.wait_ge(prep_done, 1)

                def head(i, j, first):
                    t = i * G + j
                    one = slice(t, t + 1) if isinstance(t, int) else bass.ds(t, 1)
                    if not first:
                        dve.wait_ge(hot_used, t - G + 1)
                    dve.tensor_scalar(hot_s[:, j, :], iota_h[0:P, :], src_f[:, one], None, ALU.is_equal)
                    dve.tensor_scalar(hot_d[:, j, :], iota_h[0:P, :], dst_f[:, one], None, ALU.is_equal).then_inc(hot_ready, 1)
                    dve.wait_ge(gathered[0][j], 32 * (i + 1))
                    if not first:
                        dve.wait_ge(scattered[0], 16 * (t - G + 1))
                    dve.tensor_copy(idx_cur[:, j, :], idx_all[:, one, :].rearrange("p a b -> p (a b)"))
                    dve.tensor_tensor(ring_s[:, j, :], ring_s[:, j, :], ring_d[:, j, :], ALU.add).then_inc(z_ready, 1)

                def tail(t, j):
                    dve.wait_ge(relu_ready, t + 1)
                    for h in range(HEADS1):
                        part = slice(h * DH, (h + 1) * DH)
                        last = dve.tensor_tensor_reduce(ring_d[:, j, part], ring_s[:, j, part], rows[:, 2, part], 1.0,
                                                        ring_s[:, j, D + h:D + h + 1], ALU.mult, ALU.add,
                                                        logits[:, j, h:h + 1])
                    last.then_inc(edge_done[0], 1)

                for j in range(G):
                    head(0, j, True)
                    if j > 0:
                        tail(j - 1, j - 1)
                with dve.Fori(1, NG) as i:
                    for j in range(G):
                        head(i, j, False)
                        tail(G * i + j - 1, (j - 1) % G)
                tail(ET - 1, G - 1)

            def edges_second():
                done = [0]
                dve.wait_ge(prep_done, 2)
                dve.wait_ge(rows_loaded["attn2"], 16)

                def tile(i, j, first, base):
                    t = i * G + j
                    one = slice(t, t + 1) if isinstance(t, int) else bass.ds(t, 1)
                    n = base + 2 * t
                    dve.wait_ge(gathered[1][j], 32 * (i + 1))
                    if not first:
                        dve.wait_ge(scattered[1], 16 * (t - G + 1))
                    dve.tensor_copy(idx_cur[:, j, :], idx_all[:, one, :].rearrange("p a b -> p (a b)"))
                    z = ring_s[:, j, 0:D]
                    dve.tensor_tensor(z, z, ring_d[:, j, 0:D], ALU.add).then_inc(step, 1)
                    dve.wait_ge(step, n + 1)
                    dve.scalar_tensor_tensor(out=z, in0=z, scalar=0.2, in1=z, op0=ALU.mult, op1=ALU.max).then_inc(step, 1)
                    dve.wait_ge(step, n + 2)
                    dve.tensor_tensor_reduce(ring_d[:, j, 0:D], z, rows[:, 2, :], 1.0, 0.0, ALU.mult, ALU.add,
                                             logits[:, j, 0:1]).then_inc(edge_done[1], 1)

                base = ticks[0]
                for j in range(G):
                    tile(0, j, True, base)
                with dve.Fori(1, NG - 3) as i:
                    for j in range(G):
                        tile(i, j, False, base)

                def divide():
                    dve.wait_ge(mix_used, len(MIX_STEPS))
                    dve.reciprocal(mix_rden[:, :, :], mix_out[:, :, :, MD]).then_inc(mixr_done, 1)
                    dve.wait_ge(mixr_done, 1)
                    for t in range(T):
                        last = dve.tensor_tensor(b1[:, t, :].rearrange("p (h d) -> p h d", d=MD), mix_out[:, t, :, 0:MD],
                                                 mix_rden[:, t, :].unsqueeze(2).to_broadcast([P, MH, MD]), ALU.mult)
                    last.then_inc(mixo_done, 1)

                DIV_AT, TR_AT = 2, 4
                for n in range(3 * G):
                    tile(NG - 3 + n // G, n % G, False, base)
                    if n == DIV_AT:
                        divide()
                    if n in (DIV_AT + 2, DIV_AT + 3):
                        weights_lo([8 + n - DIV_AT - 2])
                    if n == DIV_AT + TR_AT:
                        transposed_lo(2)
                    if n > DIV_AT + TR_AT + 1:
                        u = n - DIV_AT - TR_AT - 2
                        products_out(8 + u // T, x2, 3, "proj", tiles=(u % T,))
                for u in range(3 * G - DIV_AT - TR_AT - 2, 2 * T):
                    products_out(8 + u // T, x2, 3, "proj", tiles=(u % T,))
                ticks[0] = base + 2 * ET

            edges_first()

            def dense(l, dest):
                H = HL[l]
                DH = D // H
                bufs = [dl1[0], dl1[1]] if l == 0 else [dl2a, dl2b]
                ebufs = [dl1[2], dl1[3]] if l == 0 else [de2a, de2b]
                elu_o, elu_m = (elu_o_t[:, :], elu_m_t[:, :]) if l == 0 else (elu_o2[:, :], elu_m2[:, :])

                def maxima(c):
                    dve.wait_ge(dl_loaded[l][c % 2], 16 * (c // 2 + 1))
                    lv = bufs[c % 2][:, :].rearrange("p (s h) -> p h s", h=H)
                    after(dve.tensor_reduce(mxv[:, c, 0:H], lv, AX.X, ALU.max))
                    dve.tensor_scalar(mxv[:, c, 0:H], mxv[:, c, 0:H], -1.0, None, ALU.mult).then_inc(max_ready[l], 1)

                maxima(0)
                for c in range(T):
                    for h in range(H):
                        dve.wait_ge(exp_ready[l], H * c + h + 1)
                        last = dve.tensor_tensor_reduce(ebufs[c % 2][:, h, :], ebufs[c % 2][:, h, :], counts[:, c, :],
                                                        1.0, 0.0, ALU.mult, ALU.add, den[:, c, h:h + 1])
                    last.then_inc(probs_ready[l], 1)
                    if c + 1 < T:
                        maxima(c + 1)
                    dve.wait_ge(probs_ready[l], c + 1)
                    after(dve.tensor_scalar(rden[:, c, 0:H], den[:, c, 0:H], 1e-30, None, ALU.max))
                    after(dve.reciprocal(rden[:, c, 0:H], rden[:, c, 0:H]))
                    dve.wait_ge(agg_full[l], c + 1)
                    pv = ps[0:P, 4 + 2 * (c % 2):6 + 2 * (c % 2), 0:HALF]
                    if H == 1:
                        last = dve.tensor_scalar(elu_o.rearrange("p (a d) -> p a d", a=2), pv, rden[:, c, 0:1], None, ALU.mult)
                    else:
                        for b in range(2):
                            last = dve.tensor_tensor(
                                elu_o[:, b * HALF:(b + 1) * HALF].rearrange("p (h d) -> p h d", d=DH),
                                pv[:, b, :].rearrange("p (h d) -> p h d", d=DH),
                                rden[:, c, 4 * b:4 * b + 4].unsqueeze(2).to_broadcast([P, 4, DH]), ALU.mult)
                    after(last)
                    dve.tensor_scalar(elu_m, elu_o, 0.0, None, ALU.min).then_inc(elu_min[l], 1)
                    dve.wait_ge(elu_exp[l], c + 1)
                    after(dve.scalar_tensor_tensor(out=elu_o, in0=elu_o, scalar=0.0, in1=elu_m, op0=ALU.max, op1=ALU.add))
                    if l == 0:
                        dve.scalar_tensor_tensor(out=dest[:, c, :], in0=elu_o, scalar=-1.0, in1=b1[:, c, :],
                                                 op0=ALU.add, op1=ALU.add).then_inc(out_ready[l], 1)
                    else:
                        dve.tensor_scalar(dest[:, c, :], elu_o, -1.0, None, ALU.add).then_inc(out_ready[l], 1)
                dve.wait_ge(out_ready[l], T)

            dve.wait_ge(counts_ready, 1)
            dve.wait_ge(scattered[0], 16 * ET)
            first_indices()
            dense(0, b1)
            dve.wait_ge(rows_loaded["ln1"], 32)
            layer_norm(1, b1, b1, wb=True)
            weights_lo([4, 5])
            transposed_lo(1)
            products_out(4, fs, 0, "gat2")
            weights_lo([6])
            products_out(5, fs, 0, "gat2")
            weights_lo([7])
            products_out(6, fd_stage, 1, "gat2")
            products_out(7, fd_stage, 1, "gat2")
            dve.memset(mix_v[:, :, :, :, MD:MD + 1], 1.0).then_inc(prep_done, 1)
            edges_second()
            dense(1, gnn)
            dve.wait_ge(rows_loaded["ln2"], 32)
            layer_norm(2, gnn, gnn, wb=True)
            dve.wait_ge(mm_used, 50)
            dve.wait_ge(xagain_loaded, 16)
            for t in range(T):
                last = dve.tensor_tensor(x2[:, t, :], x2[:, t, :], gnn[:, t, :], ALU.add)
            after(last)
            for t in range(T):
                last = dve.tensor_tensor(x2[:, t, :], x2[:, t, :], fs[:, t, 0:D], ALU.add)
            after(last)
            dve.wait_ge(gw_hi, 1)
            dve.tensor_tensor(gate_w_lo[:, :, :], gate_w_raw[:, :, :], gate_w_hi[:, :, :].bitcast(F32), ALU.subtract).then_inc(gw_lo, 1)
            layer_norm(3, x2, b1)
            dve.memset(at[:, :, :, N:TP].bitcast(F32), 0.0)
            transposed_lo(3)

            def cmp(o, a, b, op):
                after(dve.tensor_tensor(o, a, b, op))

            dve.wait_ge(gate_exp, 1)
            after(dve.tensor_scalar(gate_s[:, :, :], gate_s[:, :, :], 1.0, None, ALU.add))
            after(dve.reciprocal(gate_s[:, :, :], gate_s[:, :, :]))
            after(dve.tensor_tensor(gate_k[:, :, :], gate_s[:, :, :], gate_b[:, :].unsqueeze(1).to_broadcast([P, T, 8]), ALU.add))
            pairs = gate_k[:, :, :].rearrange("p t (g e) -> p t g e", e=2)
            after(dve.tensor_tensor(gate_g[:, :, :], pairs[:, :, :, 0], pairs[:, :, :, 1], ALU.add))

            def ranks(score, n):
                after(dve.memset(gate_r[:, :, 0:n], 0.0))
                for i in range(n):
                    o = score[:, :, i:i + 1]
                    if i > 0:
                        dve.tensor_tensor(gate_t[:, :, 0:i], o.to_broadcast([P, T, i]), score[:, :, 0:i], ALU.is_gt)
                    if i + 1 < n:
                        dve.tensor_tensor(gate_t[:, :, i + 1:n], o.to_broadcast([P, T, n - i - 1]), score[:, :, i + 1:n], ALU.is_ge)
                    after(dve.memset(gate_t[:, :, i:i + 1], 0.0))
                    after(dve.tensor_tensor(gate_r[:, :, 0:n], gate_r[:, :, 0:n], gate_t[:, :, 0:n], ALU.add))

            ranks(gate_g, 4)
            after(dve.tensor_scalar(gate_t[:, :, 0:4], gate_r[:, :, 0:4], 2.0, -BIG, ALU.is_ge, ALU.mult))
            gt2 = gate_t[:, :, 0:4].unsqueeze(3).to_broadcast([P, T, 4, 2])
            after(dve.tensor_tensor(pairs, pairs, gt2, ALU.add))
            ranks(gate_k, 8)
            after(dve.tensor_scalar(gate_t[:, :, :], gate_r[:, :, :], 2.0, None, ALU.is_lt))
            after(dve.tensor_tensor(gate_s[:, :, :], gate_s[:, :, :], gate_t[:, :, :], ALU.mult))
            after(dve.tensor_reduce(gate_g[:, :, 0:1].rearrange("p t a -> p (t a)"), gate_s[:, :, :], AX.X, ALU.add))
            after(dve.tensor_scalar(gate_g[:, :, 0:1], gate_g[:, :, 0:1], 1e-6, None, ALU.add))
            after(dve.reciprocal(gate_g[:, :, 0:1], gate_g[:, :, 0:1]))
            after(dve.tensor_tensor(cw[:, :, 0:8], gate_s[:, :, :], gate_g[:, :, 0:1].to_broadcast([P, T, 8]), ALU.mult))

            def split_lo(e, qs):
                for q in qs:
                    dve.wait_ge(e_hi, 6 * e + q + 1)
                    m, h = q // 2, q % 2
                    part = slice(h * PIECE, (h + 1) * PIECE)
                    dve.tensor_tensor(we[:, 2 * m + 1, part], eraw[:, q % 3, :], we[:, 2 * m, part].bitcast(F32),
                                      ALU.subtract).then_inc(e_lo, 1)

            def down_out(e):
                for u in range(10):
                    t, h = u // 2, u % 2
                    w = cw[:, t, slice(e, e + 1) if isinstance(e, int) else bass.ds(e, 1)]
                    dve.wait_ge(down_full, 10 * e + u + 1)
                    if u > 0:
                        dve.wait_ge(down_used, 10 * e + u)
                    dve.scalar_tensor_tensor(out=x2[:, t, h * HALF:(h + 1) * HALF], in0=ps[0:P, u % 8, 0:HALF], scalar=w,
                                             in1=x2[:, t, h * HALF:(h + 1) * HALF], op0=ALU.mult, op1=ALU.add).then_inc(down_used, 1)

            def hidden(e, first):
                for j in range(IC):
                    a = 4 * (j % 2) + 2
                    dve.wait_ge(silu_done, IC * e + j + 1)
                    dve.tensor_tensor(silu[:, j % 2, 0:314], silu[:, j % 2, 0:314], ps[:, a, 0:314], ALU.mult)
                    dve.tensor_tensor(silu[:, j % 2, 314:TP], silu[:, j % 2, 314:TP], ps[:, a + 1, 0:312], ALU.mult).then_inc(hid_f, 1)
                    dve.wait_ge(hid_hi, IC * e + j + 1)
                    dve.tensor_tensor(hid[:, 1, j, :], silu[:, j % 2, :], hid[:, 0, j, :].bitcast(F32),
                                      ALU.subtract).then_inc(hid_lo, 1)

            split_lo(0, range(6))
            hidden(0, True)
            with dve.Fori(1, EXPERTS) as e:
                split_lo(e, range(4))
                down_out(e - 1)
                split_lo(e, (4, 5))
                hidden(e, False)
            down_out(EXPERTS - 1)

        @block.tensor
        def _(pe):
            def mm3(o, lt, r, start, stop):
                pe.matmul(o, lt(0), r(0), start=start, stop=False)
                pe.matmul(o, lt(0), r(1), start=False, stop=False)
                return pe.matmul(o, lt(1), r(0), start=False, stop=stop)

            def transposes(n, srct):
                for k in range(KC):
                    u = n * TR + k
                    a = 4 + 2 * (u % 2)
                    if u >= 2:
                        pe.wait_ge(tr_lo, u - 1)
                    for t in range(T):
                        o = ps[:, a, t * P:(t + 1) * P] if t < 4 else ps[:, a + 1, 0:P]
                        last = pe.transpose(o, srct[:, t, k * 128:(k + 1) * 128], ident[0:P, 0:P])
                    last.then_inc(tr_full, 1)

            def products(q):
                pe.wait_ge(w_lo, q + 1)
                for t in range(T):
                    u = 5 * q + t
                    if u >= 4:
                        pe.wait_ge(mm_used, u - 3)
                    for k in range(KC):
                        last = mm3(ps[0:P, u % 4, 0:HALF],
                                   lambda s: at[:, s, k, t * P:(t + 1) * P],
                                   lambda s: wp[q][:, s, k, :], k == 0, k == KC - 1)
                    last.then_inc(mm_full, 1)

            pe.wait_ge(const_ready, 2)
            pe.wait_ge(ln_done, 1)
            transposes(0, b1)
            pe.wait_ge(tr_lo, TR)
            for q in range(4):
                products(q)

            pe.wait_ge(mm_used, 20)
            pe.wait_ge(prep_done, 1)
            pe.wait_ge(hot_ready, 1)
            cbanks = [(c, 0, 0, 512) for c in range(T)] + [(5 if c < 4 else 6, c * 113 if c < 4 else 0, 512, N) for c in range(T)]

            def count(j, start):
                for n, (b, o, s0, s1) in enumerate(cbanks):
                    c = n % T
                    last = pe.matmul(ps[0:P, b, o:o + s1 - s0], hot_d[:, j, c * P:(c + 1) * P], hot_s[:, j, s0:s1],
                                     start=start and (n <= 5 or n == 9), stop=False, skip_group_check=True)
                last.then_inc(hot_used, 1)

            count(0, True)
            for j in range(1, G):
                pe.wait_ge(hot_ready, j + 1)
                count(j, False)
            with pe.Fori(1, NG) as i:
                for j in range(G):
                    pe.wait_ge(hot_ready, G * i + j + 1)
                    count(j, False)

            def dense(l):
                H = HL[l]
                DH = D // H
                ebufs = [dl1[2], dl1[3]] if l == 0 else [de2a, de2b]
                pt = dl1[4] if l == 0 else dpt2
                for c in range(T):
                    pe.wait_ge(probs_ready[l], c + 1)
                    for g in range(gd_groups[l]):
                        if g >= 4:
                            pe.wait_ge(pt_copied[l], gd_groups[l] * c + g - 3)
                        for n in range(4 * g, min(4 * g + 4, H * T)):
                            h, s = n // T, n % T
                            last = pe.transpose(ps[0:P, g % 4, (n % 4) * P:(n % 4 + 1) * P],
                                                ebufs[c % 2][:, h, s * P:(s + 1) * P], ident[0:P, 0:P])
                        last.then_inc(pt_full[l], 1)
                    pe.wait_ge(pt_copied[l], gd_groups[l] * (c + 1))
                    if c >= 2:
                        pe.wait_ge(elu_min[l], c - 1)
                    for h in range(H):
                        for part in range(1 if H > 1 else 2):
                            w = DH if H > 1 else HALF
                            col = h * DH + part * HALF
                            o = ps[0:P, 4 + 2 * (c % 2) + col // HALF, col % HALF:col % HALF + w]
                            for s in range(T):
                                last = pe.matmul(o, pt[:, (h * T + s) * P:(h * T + s + 1) * P], fs[:, s, col:col + w],
                                                 start=s == 0, stop=s == T - 1)
                    last.then_inc(agg_full[l], 1)

            pe.wait_ge(counts_ready, 1)
            dense(0)
            pe.wait_ge(out_ready[0], T)
            pe.wait_ge(ln_done, 2)
            transposes(1, b1)
            pe.wait_ge(tr_lo, 2 * TR)
            for q in range(4, 8):
                products(q)

            pe.wait_ge(mm_used, 40)
            pe.wait_ge(prep_done, 3)

            pe.wait_ge(mixc_loaded, 48)

            def emptied(kind, r, h):
                pe.wait_ge(mix_used, mix_count(kind, r, h))

            for n, (kind, r, h, i) in enumerate(MIX_STEPS):
                b, m = mix_bank(n), r % 2
                before = [k for k in range(n) if mix_bank(k) == b]
                if before:
                    pe.wait_ge(mix_used, before[-1] + 1)
                hp = slice(h * MD, (h + 1) * MD)
                if kind in ("q", "k"):
                    if kind == "q":
                        pe.wait_ge(mixw_loaded[m], 48 * (r // 2 + 1))
                    s = 0 if kind == "q" else 1
                    c0, c1 = MIX_COLS[i]
                    for k in range(KC):
                        last = pe.matmul(ps[:, b, 0:c1 - c0], mix_w[:, m, k, s * 128:(s + 1) * 128], xt_v[:, k, c0:c1],
                                         start=k == 0, stop=k == KC - 1)
                elif kind == "v":
                    for x_, t in enumerate(range(4) if i == 0 else range(4, T)):
                        o = ps[0:P, b, x_ * 128:(x_ + 1) * 128]
                        pe.matmul(o, ones_row[:, :], v_row[:, r * 128:(r + 1) * 128], start=True, stop=False)
                        for k in range(KC):
                            last = pe.matmul(o, xt_v[:, k, t * P:(t + 1) * P], mix_w[:, m, k, 256:384], start=False, stop=k == KC - 1)
                elif kind == "kp":
                    emptied("k", r, 0)
                    for t in range(2 * i, min(2 * i + 2, T)):
                        last = pe.matmul(ps[0:P, b, (t % 2) * MF:(t % 2 + 1) * MF], mix_kt[hp, m, t * P:(t + 1) * P],
                                         pmt[hp, :], start=True, stop=True)
                elif kind == "qp":
                    emptied("q", r, 0)
                    c0, c1 = MIX_COLS[i % 2]
                    last = pe.matmul(ps[:, b, 0:c1 - c0], pmt[hp, (i // 2) * 128:(i // 2 + 1) * 128], mix_qt[hp, m, c0:c1],
                                     start=True, stop=True)
                elif kind == "kv":
                    emptied("v", r, 0)
                    emptied("kp", r, h)
                    for f in range(2):
                        for t in range(T):
                            last = pe.matmul(ps[:, b, f * (MD + 1):(f + 1) * (MD + 1)], mix_kp[:, h, t, f * 128:(f + 1) * 128],
                                             mix_v[:, m, t, h, :], start=t == 0, stop=t == T - 1)
                else:
                    emptied("qp", r, h)
                    emptied("kv", r, h)
                    for t in range(T):
                        for f in range(2):
                            last = pe.matmul(ps[0:P, b, t * (MD + 1):(t + 1) * (MD + 1)], mix_qp[:, h, f, t * P:(t + 1) * P],
                                             mix_kv[:, h, f, :], start=f == 0, stop=f == 1)
                last.then_inc(mix_full, 1)

            pe.wait_ge(mixo_done, 1)
            transposes(2, b1)
            pe.wait_ge(tr_lo, 3 * TR)
            for q in (8, 9):
                products(q)
            pe.wait_ge(mm_used, 50)
            dense(1)
            pe.wait_ge(ln_done, 4)
            transposes(3, b1)
            pe.wait_ge(tr_lo, 4 * TR)
            pe.wait_ge(gw_lo, 1)
            for t in range(T):
                for k in range(KC):
                    last = mm3(ps[0:P, 0, t * 8:(t + 1) * 8], lambda s: at[:, s, k, t * P:(t + 1) * P],
                               lambda s: (gate_w_hi, gate_w_lo)[s][:, k, :], k == 0, k == KC - 1)
            last.then_inc(gate_full, 1)
            pe.wait_ge(gate_exp, 1)

            w13 = [[we[:, 2 * m + s, :].rearrange("p (k i) -> p k i", i=INTER) for s in range(2)] for m in range(2)]
            w2v = [we[:, 4 + s, :].rearrange("p (k d) -> p k d", d=D) for s in range(2)]

            def expert(e, first):
                pe.wait_ge(e_lo, 6 * e + 4)
                for j in range(IC):
                    if j >= 2:
                        pe.wait_ge(hid_f, IC * e + j - 1)
                    elif not first:
                        pe.wait_ge(down_used, 10 * e - (0 if j == 0 else 2))
                    for m in range(2):
                        for n, (a, b_) in enumerate(((0, 314), (314, TP))):
                            o = ps[:, 4 * (j % 2) + 2 * m + n, 0:b_ - a]
                            for k in range(KC):
                                last = mm3(o, lambda s: w13[m][s][:, k, j * 128:(j + 1) * 128],
                                           lambda s: at[:, s, k, a:b_], k == 0, k == KC - 1)
                    last.then_inc(up_full, 1)
                pe.wait_ge(e_lo, 6 * e + 6)
                pe.wait_ge(hid_f, IC * e + IC - 1)
                for us in (range(4), range(4, 8), range(8, 10)):
                    for k in range(IC):
                        if us[0] == 0:
                            pe.wait_ge(hid_lo, IC * e + k + 1)
                        for u in us:
                            t, h = u // 2, u % 2
                            if u >= 8 and k == 0:
                                pe.wait_ge(down_used, 10 * e + u - 7)
                            last = mm3(ps[0:P, u % 8, 0:HALF], lambda s: hid[:, s, k, t * P:(t + 1) * P],
                                       lambda s: w2v[s][:, k, h * HALF:(h + 1) * HALF], k == 0, k == IC - 1)
                            if k == IC - 1:
                                last.then_inc(down_full, 1)

            expert(0, True)
            with pe.Fori(1, EXPERTS) as e:
                expert(e, False)


def mixer_steps():
    def feed(kind, r):
        return [(kind, r, 0, i) for i in range(2)] if r < KC else []

    def features(r, h):
        return [("kp", r, h, i) for i in range(3)] + [("qp", r, h, i) for i in range(4)]

    steps = feed("q", 0) + feed("k", 0) + feed("v", 0)
    for r in range(KC):
        steps += (features(r, 0) + feed("q", r + 1) + [("kv", r, 0, 0)] + features(r, 1) + feed("k", r + 1)
                  + [("num", r, 0, 0), ("kv", r, 1, 0)] + feed("v", r + 1) + [("num", r, 1, 0)])
    return steps


MIX_STEPS = mixer_steps()
MIX_COLS = ((0, 313), (313, N))


def mix_count(kind, r, h):
    return 1 + max(n for n, s in enumerate(MIX_STEPS) if s[:3] == (kind, r, h))


def mix_bank(n):
    kind, _, h, _ = MIX_STEPS[n]
    if kind == "kv":
        return 4 + h
    if kind == "num":
        return 6 + h
    return sum(s[0] not in ("kv", "num") for s in MIX_STEPS[:n]) % 4


_ORDER = ['x', 'src', 'dst', 'W1s', 'b1s', 'W1d', 'b1d', 'attn1', 'ln1_w', 'ln1_b', 'Wos', 'bos', 'Wod', 'bod',
          'attno', 'lno_w', 'lno_b', 'qkv_wT', 'qk_bcols', 'v_brow', 'proj_wT', 'proj_b', 'proj_matT', 'gate_wT',
          'gate_bias', 'moe_w']


def lay_out(inputs):
    import numpy as np
    a = {k: np.asarray(v) for k, v in inputs.items()}
    g = {k: a['L0_gnn_' + k] for k in ('W1s', 'b1s', 'W1d', 'b1d', 'ln1_w', 'ln1_b', 'Wos', 'bos', 'Wod', 'bod', 'lno_w', 'lno_b')}
    g['attn1'] = a['L0_gnn_attn1'].reshape(-1)
    g['attno'] = a['L0_gnn_attno'].reshape(-1)
    g['x'], g['src'], g['dst'] = a['x'], a['src'], a['dst']
    g['qkv_wT'] = a['L0_mix_qkv_w'].T
    g['qk_bcols'] = a['L0_mix_qkv_b'][:2 * D].reshape(2 * KC, 128).T
    g['v_brow'] = a['L0_mix_qkv_b'][2 * D:].reshape(1, D)
    g['proj_wT'] = a['L0_mix_proj_w'].T
    g['proj_b'] = a['L0_mix_proj_b']
    g['proj_matT'] = a['L0_mix_proj_mat'].T
    g['gate_wT'] = a['L0_ffn_gate_weight'].T
    g['gate_bias'] = a['L0_ffn_gate_bias']

    def pieces(w, chunks):
        e, o, i = w.shape
        t = w.transpose(0, 2, 1).reshape(e, 2, chunks // 2, 128, o)
        return t.transpose(0, 1, 3, 2, 4).reshape(e, 2, 128, PIECE)

    cat = lambda w, s: np.concatenate([a['L0_ffn_' + w], a['L0_ffn_' + s][None]], 0)
    g['moe_w'] = np.concatenate([pieces(cat('w1', 'sw1'), KC), pieces(cat('w3', 'sw3'), KC),
                                 pieces(cat('w2', 'sw2'), IC)], 1)
    return {k: np.ascontiguousarray(g[k]) for k in _ORDER}


def kernel(**inputs):
    import numpy as _np
    import concourse.bacc as _bacc
    from concourse import mybir as _mybir
    from concourse.bass_utils import run_bass_kernel_spmd as _run

    nc = _bacc.Bacc("TRN2", target_bir_lowering=False, num_devices=1)
    laid = lay_out(inputs)
    arrays, args = {}, {}
    for name in _ORDER:
        v = laid[name]
        arrays[f"in_{name}_dram"] = v
        args[name] = nc.dram_tensor(f"in_{name}_dram", v.shape, _mybir.dt.from_np(v.dtype), kind="ExternalInput").ap()
    args['out'] = nc.dram_tensor("out_0_dram", (N, D), _mybir.dt.from_np(_np.dtype('float32')), kind="ExternalOutput").ap()
    build(nc, **args)
    r = _run(nc, [arrays], core_ids=[0])
    return r.results[0]["out_0_dram"]
```

```python
from contextlib import ExitStack

import concourse.bass as bass
from concourse import mybir

ACT = mybir.ActivationFunctionType
ALU = mybir.AluOpType
AX = mybir.AxisListType
F32 = mybir.dt.float32
F32R = mybir.dt.float32r
F16 = mybir.dt.float16
I32 = mybir.dt.int32

N = 625
P = 125
T = N // P
D = 768
KC = D // 128
HALF = D // 2
TP = 626
EDGES = 10625
ET = EDGES // P
G = 5
NG = ET // G
HEADS1 = 8
DX = D + HEADS1
MH = 12
MD = 64
MF = 256
EXPERTS = 9
ROUTED = EXPERTS - 1
CAP = 256
BL = CAP // 128
JOBS_MIN = -(-2 * N // CAP) // 2 * 2
JOBS = -(-((2 * N + ROUTED * (CAP - 1)) // CAP) // 2) * 2
NB = (JOBS + 1) * BL
INTER = 512
IC = INTER // 128
LN_EPS = 1e-5
NEG = -1.0e30
BIG = 1.0e30
PIECE = 1536


def build(nc, x, src, dst, W1s, b1s, W1d, b1d, attn1, ln1_w, ln1_b, Wos, bos, Wod, bod, attno, lno_w,
          lno_b, qkv_wT, qk_bcols, v_brow, proj_wT, proj_b, proj_matT, gate_wT, gate_bias, moe_w, out):
    ctx = ExitStack()
    with ctx:
        def sem(name):
            return ctx.enter_context(nc.semaphore(name))

        def sb(name, shape, dt, stack=ctx):
            return stack.enter_context(nc.sbuf_tensor(name, shape, dt))

        def zone(tensors):
            with ExitStack() as here:
                return [sb(name, shape, dt, here) for name, shape, dt in tensors]

        def dram(name, shape, dt=F32):
            return nc.dram_tensor(name, shape, dt, kind="Internal").ap()

        WL = [DX, D + 1]
        table_src = [dram(f"table_src{l}", (N, WL[l])) for l in range(2)]
        table_dst = [dram(f"table_dst{l}", (N, WL[l])) for l in range(2)]
        HL = [HEADS1, 1]
        dense_logits = [dram(f"dense_logits{l}", (N * N, HL[l])) for l in range(2)]

        xf_rows = dram("xf_rows", (N, D))
        y_rows = dram("y_rows", (2 * N + 128, D))

        ident = sb("ident", [128, 128], F32)
        iota_i = sb("iota_i", [128, TP], I32)
        iota_h = sb("iota_h", [128, TP], F16)
        src_i = sb("src_i", [P, ET], I32)
        dst_i = sb("dst_i", [P, ET], I32)
        src_f = sb("src_f", [P, ET], F32)
        dst_f = sb("dst_f", [P, ET], F32)
        dst_bias = sb("dst_bias", [P, ET], F32)
        idx_all = sb("idx_all", [P, ET, 3], I32)
        idx_cur = sb("idx_cur", [P, G, 3], I32)
        logits = sb("logits", [P, G, HEADS1], F32)
        relu_dot = sb("relu_dot", [P, G], F32)
        stats = sb("stats", [P, T, 2, 6], F32)
        mv = sb("mv", [P, T, 2], F32)
        std = sb("std", [P, T], F32)
        rstd = sb("rstd", [P, T], F32)
        eps_ln = sb("eps_ln", [128, 1], F32)
        mxv = sb("mxv", [P, T, HEADS1], F32)
        den = sb("den", [P, T, HEADS1], F32)
        rden = sb("rden", [P, T, HEADS1], F32)
        mix_rden = sb("mix_rden", [P, T, MH], F32)
        qk_bias = sb("qk_bias", [128, 2 * KC], F32)
        cw = sb("cw", [P, T, EXPERTS], F32)
        gate_s = sb("gate_s", [P, T, 8], F32)
        gate_k = sb("gate_k", [P, T, 8], F32)
        gate_r = sb("gate_r", [P, T, 8], F32)
        gate_t = sb("gate_t", [P, T, 8], F32)
        gate_g = sb("gate_g", [P, T, 4], F32)
        gate_b = sb("gate_b", [P, 8], F32)
        gate_w_raw = sb("gate_w_raw", [128, KC, 8], F32)
        gate_w_hi = sb("gate_w_hi", [128, KC, 8], F32R)
        gate_w_lo = sb("gate_w_lo", [128, KC, 8], F32R)
        ones_row = sb("ones_row", [1, P], F32)
        token_i = sb("token_i", [P, T, 2, 2], I32)
        token_f = sb("token_f", [P, T, 2, 2], F32)
        empty_i = sb("empty_i", [128, 1], I32)
        empty_f = sb("empty_f", [128, 1], F32)
        choice = sb("choice", [P, 3, T, 2], F32)
        block_hot = sb("block_hot", [P, 2 * T, NB], F32)
        empty_row = sb("empty_row", [128, NB], F32)
        place = sb("place", [P, T, 8], F32)
        step_f = sb("step_f", [P, T, 8], F32)
        routed = sb("routed", [P, T, 8], F32)
        numbers = sb("numbers", [P, 128], F32)
        job_count = sb("job_count", [P, 8], F32)
        job_end = sb("job_end", [P, 9], F32)
        job_cmp = sb("job_cmp", [P, JOBS + 1, 8], F32)
        job_expert_f = sb("job_expert_f", [P, JOBS + 1], F32)
        job_expert = sb("job_expert", [P, JOBS + 1], I32)
        jobs_i = sb("jobs_i", [P, 1], I32)
        blocks_f = sb("blocks_f", [P, T, 8], F32)
        list_block = sb("list_block", [P, T, 8], F32)
        before = sb("before", [P, T + 1, 8], F32)
        lower = sb("lower", [P, P], F32)
        ones = sb("ones", [P, P], F32)
        lst = sb("lst", [128, NB, 4], I32)
        gather_i = sb("gather_i", [128, BL], I32)
        scatter_i = sb("scatter_i", [128, BL], I32)

        counts, rows = zone([("counts", [P, T, N], F32), ("rows", [P, 4, D], F32)])
        (hid,) = zone([("hid", [128, 2, IC, TP], F32R)])
        hid_s, raw4, raw5, y_1 = zone([("hid_s", [128, 2, IC, CAP], F32R), ("raw4", [128, PIECE], F32),
                                       ("raw5", [128, PIECE], F32), ("y_1", [128, D], F32)])
        sb("zone_d", [128, T * N + 4 * D], F32)
        raw3, xg = zone([("raw3", [128, PIECE], F32), ("xg", [128, BL, D], F32)])
        _, slot_hot, entries = zone([("under_hot", [128, PIECE], F32), ("slot_hot", [P, 2 * T, 128], F32), ("entries", [P, 2 * T, NB, 3], F32)])
        fs = sb("fs", [P, T, DX], F32)
        (wraw8,) = zone([("wraw8", [128, KC, HALF], F32)])
        xt = sb("xt", [128, T * D], F32)
        xt_v = xt[:, 0:KC * N].rearrange("p (k n) -> p k n", k=KC)
        x2 = xt[0:P, :].rearrange("p (t d) -> p t d", t=T)
        (at,) = zone([("at", [128, 2, KC, TP], F32R)])
        mix_qt, mix_kt, mix_v, mix_kp, mix_kv = zone([
            ("mix_qt", [128, 2, N], F32), ("mix_kt", [128, 2, N], F32), ("mix_v", [P, 2, T, 2, MD + 1], F32),
            ("mix_kp", [P, 2, T, MF], F32), ("mix_kv", [128, 2, 2, MD + 1], F32)])
        dl1 = zone([("dl_a", [P, N * 8], F32), ("dl_b", [P, N * 8], F32), ("de_a", [P, 8, N], F32),
                    ("de_b", [P, 8, N], F32), ("under_raw", [P, 2 * KC * TP - 5000 + 1], F32), ("dpt", [P, 4 * N], F32)])
        atg0, atg1, y_0 = zone([("atg0", [128, 2, KC, CAP], F32R), ("atg1", [128, 2, KC, CAP], F32R), ("y_0", [128, D], F32)])
        atg, y_sb = [atg0, atg1], [y_0, y_1]
        sb("zone_a", [128, 2 * KC * TP], F32)
        wp0, wp1, wraw0, wraw1, fd_stage = zone([
            ("wp0", [128, 2, KC, HALF], F32R), ("wp1", [128, 2, KC, HALF], F32R),
            ("wraw0", [128, KC, HALF], F32), ("wraw1", [128, KC, HALF], F32), ("fd_stage", [P, T, DX], F32)])
        ring_s, ring_d, hot_s, hot_d = zone([
            ("ring_s", [P, G, DX], F32), ("ring_d", [P, G, DX], F32),
            ("hot_s", [P, G, TP], F16), ("hot_d", [P, G, TP], F16)])
        _, mix_w, pmt, v_row, mix_out, mix_qp = zone([
            ("under_ring", [P, 2 * G * DX], F32), ("mix_w", [128, 2, KC, 3 * 128], F32),
            ("pmt", [128, MF], F32), ("v_row", [1, D], F32), ("mix_out", [P, T, MH, MD + 1], F32),
            ("mix_qp", [128, 2, 2, N], F32)])
        _, wraw9, wp8, wp9 = zone([
            ("under_ring2", [P, 2 * G * DX], F32), ("wraw9", [128, KC, HALF], F32),
            ("wp8", [128, 2, KC, HALF], F32R), ("wp9", [128, 2, KC, HALF], F32R)])
        wp, wraw = [wp0, wp1] * 4 + [wp8, wp9], [wraw0, wraw1] * 4 + [wraw8, wraw9]
        _, neg, elu_o_t, elu_m_t = zone([
            ("under_neg", [P, 6 * KC * HALF + T * DX], F32), ("neg", [P, N], F32),
            ("elu_o", [P, D], F32), ("elu_m", [P, D], F32)])
        dl2, dpt2, elu_o2, elu_m2 = zone([
            ("dl2", [P, T, N], F32), ("dpt2", [P, 4 * N], F32), ("elu_o2", [P, D], F32), ("elu_m2", [P, D], F32)])
        _, gnn, _, xf = zone([
            ("under_gnn", [P, 2 * G * DX], F32), ("gnn", [P, T, D], F32),
            ("under_xf", [P, 6 * 6 * INTER - 2 * G * DX - 2 * T * D], F32), ("xf", [P, T, D], F32)])
        (we,) = zone([("we", [128, 6, 6 * INTER], F32R)])
        _, eraw, silu = zone([("under_we", [128, 6 * 6 * INTER], F32), ("eraw", [128, 3, PIECE], F32),
                              ("silu", [128, 2, TP], F32)])
        (y_in,) = zone([("y_in", [P, T, 2, D], F32)])
        raws = [eraw[:, 0, :], eraw[:, 1, :], eraw[:, 2, :], raw3[:, :], raw4[:, :], raw5[:, :]]
        sb("zone_c", [128, 6 * 6 * INTER + 3 * PIECE + 2 * TP - T * D], F32)
        b1 = sb("b1", [P, T, D], F32)
        ps = ctx.enter_context(nc.psum_tensor("ps", [128, 8, 512], F32))

        x_loaded = [sem(f"x_loaded{t}") for t in range(T)]
        idx_loaded, const_ready, prep_done = (sem(n) for n in
            ("idx_loaded", "const_ready", "prep_done"))
        small_loaded = sem("small_loaded")
        rows_loaded = {name: sem("rows_" + name) for name in ("gat1", "ln1", "attn2", "gat2s", "gat2d", "ln2", "proj")}
        ln_var, ln_std, ln_done = sem("ln_var"), sem("ln_std"), sem("ln_done")
        tr_full, tr_hi, tr_lo = sem("tr_full"), sem("tr_hi"), sem("tr_lo")
        raw_loaded = [sem(f"raw_loaded{i}") for i in range(2)]
        w_hi, w_lo = sem("w_hi"), sem("w_lo")
        mm_full, mm_used = sem("mm_full"), sem("mm_used")
        tables_written = sem("tables_written")
        pool_turn = sem("pool_turn")
        pool_const = sem("pool_const")
        neg_ready, filled = sem("neg_ready"), sem("filled")
        gathered = [[sem(f"gathered{l}_{j}") for j in range(G)] for l in range(2)]
        ext_ready, z_ready, relu_ready = sem("ext_ready"), sem("z_ready"), sem("relu_ready")
        edge_done = [sem(f"edge_done{l}") for l in range(2)]
        scattered = [sem(f"scattered{l}") for l in range(2)]
        hot_square, hot_d_ready = sem("hot_square"), sem("hot_d_ready")
        hot_ready, hot_used, counts_ready = sem("hot_ready"), sem("hot_used"), sem("counts_ready")
        dl_loaded = [[sem(f"dl_loaded{l}_{i}") for i in range((2, T)[l])] for l in range(2)]
        max_ready = [sem(f"max_ready{l}") for l in range(2)]
        exp_ready = [sem(f"exp_ready{l}") for l in range(2)]
        probs_ready = [sem(f"probs_ready{l}") for l in range(2)]
        pt_full = [sem(f"pt_full{l}") for l in range(2)]
        pt_copied = [sem(f"pt_copied{l}") for l in range(2)]
        agg_full = [sem(f"agg_full{l}") for l in range(2)]
        elu_min = [sem(f"elu_min{l}") for l in range(2)]
        elu_max = [sem(f"elu_max{l}") for l in range(2)]
        elu_exp = [sem(f"elu_exp{l}") for l in range(2)]
        out_ready = [sem(f"out_ready{l}") for l in range(2)]
        mixc_loaded = sem("mixc_loaded")
        mixw_loaded = [sem(f"mixw_loaded{i}") for i in range(2)]
        mix_full, mix_used = sem("mix_full"), sem("mix_used")
        mixr_done = sem("mixr_done")
        mixo_done = sem("mixo_done")
        xagain_loaded, xagain_used = sem("xagain_loaded"), sem("xagain_used")
        gate_full, gate_exp, gate_done = sem("gate_full"), sem("gate_exp"), sem("gate_done")
        gw_hi, gw_lo = sem("gw_hi"), sem("gw_lo")
        eraw_loaded = [sem(f"eraw_loaded{i}") for i in range(6)]
        dispatch_const, xf_stored = sem("dispatch_const"), sem("xf_stored")
        routed_ready, place_full, place_read = sem("routed_ready"), sem("place_full"), sem("place_read")
        jobs_ready, entries_ready, list_full, list_ready = (sem(n) for n in ("jobs_ready", "entries_ready", "list_full", "list_ready"))
        landed = sem("landed")
        gather_i_ready, scatter_i_ready = sem("gather_i_ready"), sem("scatter_i_ready")
        xg_loaded = [sem(f"xg_loaded{i}") for i in range(BL)]
        tg_full, tg_hi, tg_lo, w1_used = sem("tg_full"), sem("tg_hi"), sem("tg_lo"), sem("w1_used")
        y_loaded = [sem(f"y_loaded{t}") for t in range(T)]
        sum_done = sem("sum_done")
        e_hi, e_lo = sem("e_hi"), sem("e_lo")
        up_full, silu_done, hid_f, hid_hi, hid_lo = (sem(n) for n in
            ("up_full", "silu_done", "hid_f", "hid_hi", "hid_lo"))
        down_full, down_used = sem("down_full"), sem("down_used")
        out_stored = sem("out_stored")
        step = sem("step")
        astep = sem("astep")

        def pt_psum(u):
            return ps[0:P, 2 * (u % 2):2 * (u % 2) + 2, :].rearrange("p a b -> p (a b)")[:, 512 - 4 * P:512 + P]

        def tr_psum(n, t):
            if n == 0:
                b = 2 * ((t + 2) % 4)
            elif n == 1:
                b = 6
            else:
                b = (0 if n == 3 else 4) + 2 * (t % 2)
            return (ps[:, b:b + 2, :].rearrange("p a b -> p (a b)")[:, 512 - 4 * P:512 + 2 * P]
                    .rearrange("p (k n) -> p k n", k=KC))

        def first(g):
            return isinstance(g, int) and g == 0

        def jobs(eng, start, body):
            start()
            for g in range(2):
                body(g, g)
            with eng.Fori(1, JOBS_MIN // 2) as m:
                for parity in range(2):
                    body(2 * m + parity, parity)
            eng.wait_ge(jobs_ready, 1)
            count = eng.value_load(jobs_i[0:1, 0:1], min_val=JOBS_MIN, max_val=JOBS)
            with eng.Fori(JOBS_MIN // 2, JOBS // 2) as m:
                for parity in range(2):
                    with eng.If(count > 2 * m + parity):
                        body(2 * m + parity, parity)

        def tg_psum(b):
            return (ps[:, 4 + 2 * b:6 + 2 * b, :].rearrange("p a b -> p (a b)")[:, 1024 - D:1024]
                    .rearrange("p (k n) -> p k n", k=KC))

        def down_bank(u):
            return u if u < 8 else u - 6

        def ln_count(n, t):
            return n * T + t + 1 if n < 2 else 2 * T + 2 * t + (n - 2) + 1

        block = ctx.enter_context(nc.Block())
        TABLES = 16 * 2 * T
        cell_rows = [dense_logits[l].rearrange("(t p s) h -> t p (s h)", t=T, p=P) for l in range(2)]
        weights = [W1s, W1d, Wos, Wod, proj_wT]
        half_of = [(w, h) for w in weights for h in range(2)]
        PT_SLOTS = 4
        AGG_LAG, COPY_LAG, NORM_LAG, ELU_LAG, OUT_LAG = 2, (3, 0), (4, 2), (5, 2), (6, 2)

        def row(v):
            return v.rearrange("(a d) -> a d", a=1).to_broadcast([P, D])

        @block.sync
        def _(sp):
            for t in range(T):
                sp.dma_start(b1[:, t, :], x[t * P:(t + 1) * P, :]).then_inc(x_loaded[t], 16)
            sp.dma_start(src_i[:, :], src.rearrange("(p t) -> p t", p=P)).then_inc(idx_loaded, 16)
            sp.dma_start(dst_i[:, :], dst.rearrange("(p t) -> p t", p=P)).then_inc(idx_loaded, 16)

            def load_rows(slot, v, name):
                sp.dma_start(rows[:, slot, :], row(v)).then_inc(rows_loaded[name], 16)

            def load_half(q):
                if q >= 2:
                    sp.wait_ge(w_lo, q - 1)
                w, h = half_of[q]
                sp.dma_start(wraw[q][:, :, :], w.rearrange("(k p) n -> p k n", p=128)
                             [:, :, h * HALF:(h + 1) * HALF]).then_inc(raw_loaded[q % 2], 16)

            load_half(0)
            load_rows(0, b1s, 'gat1')
            load_rows(1, b1d, 'gat1')
            load_rows(2, attn1, 'gat1')
            load_half(1)
            sp.dma_start(qk_bias[:, :], qk_bcols).then_inc(small_loaded, 16)
            sp.dma_start(gate_b[:, :], gate_bias.rearrange("(a d) -> a d", a=1).to_broadcast([P, 8])).then_inc(small_loaded, 16)
            sp.dma_start(gate_w_raw[:, :, :], gate_wT.rearrange("(k p) n -> p k n", p=128)).then_inc(small_loaded, 16)

            def fill(l, cs):
                for c in cs:
                    sp.dma_start(cell_rows[l][c].rearrange("p (h s) -> p h s", s=N),
                                 neg[:, :].unsqueeze(1).to_broadcast([P, HL[l], N])).then_inc(filled, 16)

            load_half(2)
            sp.wait_ge(neg_ready, 1)
            fill(0, (0,))
            load_half(3)
            fill(0, range(1, T))
            fill(1, range(T))

            def store_table(l, n):
                table, rows_of = ((table_src[l], fs), (table_dst[l], fd_stage))[n]
                for t in range(T):
                    sp.wait_ge(mm_used, 20 * l + 10 * n + 5 + t + 1)
                    sp.wait_ge(ext_ready, (2 * l + n) * T + t + 1)
                    sp.dma_start(table[t * P:(t + 1) * P, :], rows_of[:, t, 0:WL[l]]).then_inc(tables_written, 16)

            def load_logits(l):
                sp.wait_ge(scattered[l], 16 * ET)
                sp.wait_ge(edge_done[l], ET)
                if l == 0:
                    sp.wait_ge(hot_used, ET)
                for c in range(T):
                    if l == 1:
                        sp.dma_start(dl2[:, c, :], cell_rows[l][c]).then_inc(dl_loaded[l][c], 16)
                        continue
                    if c >= 2:
                        sp.wait_ge(exp_ready[l], (c - 1) * HL[l])
                    sp.dma_start(dl1[c % 2][:, :], cell_rows[l][c]).then_inc(dl_loaded[l][c % 2], 16)

            store_table(0, 0)
            store_table(0, 1)
            load_rows(0, ln1_w, 'ln1')
            load_rows(1, ln1_b, 'ln1')
            load_logits(0)
            load_rows(2, attno, 'attn2')
            load_rows(3, bos, 'gat2s')

            def load_gat2():
                sp.wait_ge(ln_done, 2 * T)
                load_rows(1, bod, 'gat2d')

            sp.wait_ge(pt_full[0], 4 * HEADS1)
            for q in range(4, 8):
                load_half(q)
                if q == 5:
                    load_gat2()
            store_table(1, 0)
            sp.wait_ge(w_lo, 8)
            sp.dma_start(pmt[0:MD, :], proj_matT).then_inc(mixc_loaded, 16)
            sp.dma_start(pmt[MD:128, :], proj_matT).then_inc(mixc_loaded, 16)
            sp.dma_start(v_row[:, :], v_brow).then_inc(mixc_loaded, 16)
            qkv_pairs = qkv_wT.rearrange("(k p) (s r m) -> r p k s m", p=128, s=3, m=128)
            for r in range(KC):
                if r == 1:
                    store_table(1, 1)
                if r == 2:
                    load_rows(0, lno_w, 'ln2')
                    load_rows(1, lno_b, 'ln2')
                    load_rows(3, proj_b, 'proj')
                if r >= 2:
                    sp.wait_ge(mix_full, mix_count("v", r - 2, 0))
                for s in range(3):
                    if r >= 1:
                        sp.wait_ge(edge_done[1], 2 + 2 * s if r == 1 else 13 * (r - 2) + 10 + s)
                    sp.dma_start(mix_w[:, 1 - r % 2, :, s * 128:(s + 1) * 128], qkv_pairs[r][:, :, s, :]).then_inc(mixw_loaded[r % 2], 16)
            sp.wait_ge(mix_full, mix_count("v", KC - 1, 0))
            load_half(8)
            load_half(9)
            sp.wait_ge(tr_full, 3 * T)
            sp.dma_start(b1[:, :, :], x.rearrange("(t p) d -> p t d", p=P)).then_inc(xagain_loaded, 16)
            load_logits(1)

            def load_piece(e, q, slot):
                sp.dma_start(raws[slot], moe_w[bass.ds(e, 1) if not isinstance(e, int) else slice(e, e + 1), q, :, :]
                             .rearrange("a p n -> (a p) n")).then_inc(eraw_loaded[slot], 16)

            def store_xf():
                for t in range(T):
                    sp.wait_ge(ln_done, 2 * T + t + 1)
                    sp.dma_start(xf_rows[t * P:(t + 1) * P, :], xf[:, t, :]).then_inc(xf_stored, 16)

            sp.wait_ge(xagain_used, 1)
            for q in range(6):
                if q == 3:
                    sp.wait_ge(agg_full[1], T)
                if q == 4:
                    store_xf()
                if q >= 4:
                    sp.wait_ge(e_lo, q - 3)
                load_piece(ROUTED, q, q % 4)

            def load_pieces(g, qs):
                at_job = slice(g, g + 1) if isinstance(g, int) else bass.ds(g, 1)
                e = sp.value_load(job_expert[0:1, at_job], min_val=0, max_val=ROUTED)
                for q in qs:
                    if not isinstance(g, int):
                        sp.wait_ge(e_lo, 6 * g + q + 1)
                    elif q < 4:
                        sp.wait_ge(e_lo, (5, 6, 3, 4)[q])
                    load_piece(e, q, q)

            sp.wait_ge(jobs_ready, 1)
            load_pieces(0, range(4))
            sp.wait_ge(down_full, 10)
            load_pieces(0, (4, 5))
            with sp.Fori(1, JOBS_MIN) as g:
                load_pieces(g, range(6))
            count = sp.value_load(jobs_i[0:1, 0:1], min_val=JOBS_MIN, max_val=JOBS)
            with sp.Fori(JOBS_MIN, JOBS) as g:
                with sp.If(count > g):
                    load_pieces(g, range(6))
            load_pieces(count, range(4))
            sp.wait_ge(landed, 16 * BL * count)
            for t in range(T):
                sp.dma_start(y_in[:, t, :, :], y_rows[2 * P * t:2 * P * (t + 1), :]
                             .rearrange("(p j) d -> p j d", j=2)).then_inc(y_loaded[t], 16)
            for t in range(T):
                sp.wait_ge(sum_done, 2 * t + 2)
                sp.dma_start(out[t * P:(t + 1) * P, :], x2[:, t, :]).then_inc(out_stored, 16)
            sp.wait_ge(out_stored, 16 * T)

        @block.gpsimd
        def _(pool):
            pool.memset(ident[:, :], 0.0).then_inc(const_ready, 1)
            pool.wait_ge(const_ready, 1)
            pool.affine_select(out=ident[:, :], in_=ident[:, :], compare_op=ALU.not_equal, fill=1.0, base=0,
                               pattern=[[-1, 128]], channel_multiplier=1).then_inc(const_ready, 1)
            pool.iota(iota_i[:, :], pattern=[[1, TP]], base=0, channel_multiplier=0).then_inc(const_ready, 1)
            pool.memset(eps_ln[:, :], LN_EPS).then_inc(const_ready, 1)
            pool.memset(neg[:, :], NEG).then_inc(neg_ready, 1)
            pool.memset(ones[:, :], 1.0)
            pool.memset(lower[:, :], 1.0).then_inc(pool_const, 1)
            pool.wait_ge(pool_const, 1)
            pool.iota(empty_i[:, :], pattern=[[0, 1]], base=2 * N + 1, channel_multiplier=1)
            pool.iota(token_i[:, :, :, 0], pattern=[[P, T], [0, 2]], base=0, channel_multiplier=1)
            pool.iota(token_i[:, :, :, 1], pattern=[[2 * P, T], [1, 2]], base=1, channel_multiplier=2).then_inc(dispatch_const, 1)
            pool.affine_select(out=lower[:, :], in_=lower[:, :], compare_op=ALU.is_gt, fill=0.0, base=0,
                               pattern=[[1, P]], channel_multiplier=-1).then_inc(dispatch_const, 1)

            def edges(l):
                pool.wait_ge(tables_written, TABLES * (l + 1))
                pool.wait_ge(prep_done, 1)
                pool.wait_ge(filled, 160)

                def gather(j):
                    pool.indirect_dma_start(
                        out=ring_s[:, j, 0:WL[l]], out_offset=None, in_=table_src[l],
                        in_offset=bass.IndirectOffsetOnAxis(ap=idx_cur[:, j, 0:1], axis=0)).then_inc(gathered[l][j], 16)
                    pool.indirect_dma_start(
                        out=ring_d[:, j, 0:WL[l]], out_offset=None, in_=table_dst[l],
                        in_offset=bass.IndirectOffsetOnAxis(ap=idx_cur[:, j, 1:2], axis=0)).then_inc(gathered[l][j], 16)

                def scatter(j):
                    pool.indirect_dma_start(
                        out=dense_logits[l], out_offset=bass.IndirectOffsetOnAxis(ap=idx_cur[:, j, 2:3], axis=0),
                        in_=logits[:, j, 0:HL[l]], in_offset=None).then_inc(scattered[l], 16)

                for j in range(G):
                    gather(j)
                def gather_scatter(i, j):
                    pool.wait_ge(edge_done[l], G * i + j + 1)
                    pool.sem_inc(pool_turn, 1)
                    gather(j)
                    if not (isinstance(i, int) and i + j == 0):
                        pool.wait_ge(scattered[l], 16 * (G * i + j))
                    pool.sem_inc(pool_turn, 1)
                    scatter(j)

                for j in range(G):
                    gather_scatter(0, j)
                with pool.Fori(1, NG - 1) as i:
                    for j in range(G):
                        gather_scatter(i, j)
                for j in range(G):
                    pool.wait_ge(edge_done[l], G * (NG - 1) + j + 1)
                    pool.wait_ge(scattered[l], 16 * (G * (NG - 1) + j))
                    scatter(j)

            edges(0)
            pool.wait_ge(prep_done, 2)
            edges(1)

            def gather_tokens(g):
                blocks = slice(BL * g, BL * g + BL) if isinstance(g, int) else bass.ds(BL * g, BL)
                pool.tensor_copy(gather_i[:, :], lst[:, blocks, 0]).then_inc(gather_i_ready, 1)
                pool.wait_ge(gather_i_ready, g + 1)
                for b in range(BL):
                    pool.sem_inc(pool_turn, 1)
                    pool.indirect_dma_start(
                        out=xg[:, b, :], out_offset=None, in_=xf_rows,
                        in_offset=bass.IndirectOffsetOnAxis(ap=gather_i[:, b:b + 1], axis=0)).then_inc(xg_loaded[b], 16)

            def start():
                pool.wait_ge(list_ready, 1)
                pool.wait_ge(xf_stored, 16 * T)
                gather_tokens(0)

            def body(g, parity):
                pool.wait_ge(tg_full, BL * g + BL)
                gather_tokens(g + 1)
                if not first(g):
                    pool.wait_ge(landed, 16 * BL * g)
                pool.tensor_copy(scatter_i[:, :], lst[:, bass.ds(BL * g, BL), 1]).then_inc(scatter_i_ready, 1)
                pool.wait_ge(scatter_i_ready, g + 1)
                for b in range(BL):
                    pool.wait_ge(down_used, 4 * g + 10 + 2 * b + 2)
                    if b > 0:
                        pool.wait_ge(landed, 16 * BL * g + 16 * b)
                    pool.sem_inc(pool_turn, 1)
                    pool.indirect_dma_start(
                        out=y_rows, out_offset=bass.IndirectOffsetOnAxis(ap=scatter_i[:, b:b + 1], axis=0),
                        in_=y_sb[b][:, :], in_offset=None).then_inc(landed, 16)

            jobs(pool, start, body)

        @block.scalar
        def _(act):
            ticks = [0]

            def after(ins):
                ticks[0] += 1
                ins.then_inc(astep, 1)
                act.wait_ge(astep, ticks[0])

            def ln_sqrt(n, t):
                act.wait_ge(ln_var, ln_count(n, t))
                act.activation(std[:, t:t + 1], mv[:, t, 1:2], ACT.Sqrt, bias=eps_ln[0:P, :]).then_inc(ln_std, 1)

            def transposed_hi(n, t):
                cols = slice(t * P, (t + 1) * P)
                act.wait_ge(tr_full, n * T + t + 1)
                if n == 0:
                    act.copy(xt_v[:, :, cols], tr_psum(n, t))
                act.copy(at[:, 0, :, cols], tr_psum(n, t)).then_inc(tr_hi, 1)

            def weights_hi(qs):
                for q in qs:
                    act.wait_ge(raw_loaded[q % 2], 16 * (q // 2 + 1))
                    if q >= 2:
                        act.wait_ge(mm_full, 5 * (q - 1))
                    act.copy(wp[q][:, 0, :, :], wraw[q][:, :, :]).then_inc(w_hi, 1)

            act.wait_ge(const_ready, 4)
            for t in range(T + 2):
                if t < T:
                    ln_sqrt(0, t)
                if t == T:
                    weights_hi([0])
                if t >= 2:
                    transposed_hi(0, t - 2)
            weights_hi([1])
            weights_hi([2, 3])
            act.wait_ge(prep_done, 1)

            def relu(t, j, first=False):
                one = slice(t, t + 1) if first else bass.ds(t, 1)
                if not first:
                    act.wait_ge(hot_used, t - G + 1)
                act.activation(hot_d[:, j, :], iota_h[0:P, :], ACT.Square, scale=0.25,
                               bias=dst_bias[:, one]).then_inc(hot_square, 1)
                act.wait_ge(hot_square, t + 1)
                act.activation(hot_d[:, j, :], hot_d[:, j, :], ACT.Relu, scale=-16.0, bias=1.0).then_inc(hot_d_ready, 1)
                act.wait_ge(z_ready, t + 1)
                act.activation(ring_s[:, j, 0:D], ring_s[:, j, 0:D], ACT.Relu, scale=0.8).then_inc(relu_ready, 1)

            for j in range(G):
                relu(j, j, first=True)
            with act.Fori(1, NG) as i:
                for j in range(G):
                    relu(G * i + j, j)
            act.wait_ge(hot_used, ET)
            for c in range(T):
                act.copy(counts[:, c, 0:512], ps[0:P, c, :])
                b, o = (5, c * 113) if c < 4 else (6, 0)
                last = act.copy(counts[:, c, 512:N], ps[0:P, b, o:o + 113])
            last.then_inc(counts_ready, 1)

            def dense(l):
                H = HL[l]
                pt = dl1[5] if l == 0 else dpt2

                def exps(u):
                    c, h = divmod(u, H)
                    if l == 1:
                        act.wait_ge(max_ready[l], c + 1)
                    elif c == 0:
                        act.wait_ge(max_ready[l], h // 2 + 1)
                    elif h == 0:
                        act.wait_ge(max_ready[l], H // 2 + c)
                    if l == 0:
                        if c >= 2:
                            act.wait_ge(pt_full[l], u - 2 * H + 1)
                        o, i = dl1[2 + c % 2][:, h, :], dl1[c % 2][:, :].rearrange("p (s h) -> p h s", h=H)[:, h, :]
                    else:
                        o = i = dl2[:, c, :]
                    act.activation(o, i, ACT.Exp, bias=mxv[:, c, h:h + 1]).then_inc(exp_ready[l], 1)

                if l == 1:
                    for u in range(T):
                        exps(u)
                for u in range(H * T + OUT_LAG[l] + (2 if l == 0 else 0)):
                    if l == 0 and u < H * T:
                        exps(u)
                    v = u - COPY_LAG[l]
                    if 0 <= v < H * T:
                        act.wait_ge(pt_full[l], v + 1)
                        if v >= PT_SLOTS:
                            act.wait_ge(agg_full[l], v - PT_SLOTS + 1)
                        m = v % PT_SLOTS
                        act.copy(pt[:, m * N:(m + 1) * N], pt_psum(v)).then_inc(pt_copied[l], 1)
                    if l == 0 and v == H * T - 1:
                        weights_hi([4])
                        transposed_hi(1, 0)
                    c, rest = divmod(u - ELU_LAG[l] + 1, H)
                    if rest == 0 and 1 <= c <= T:
                        elu_m = (elu_m_t, elu_m2)[l][:, :]
                        act.wait_ge(elu_min[l], c)
                        act.activation(elu_m, elu_m, ACT.Exp).then_inc(elu_exp[l], 1)
                        if l == 1:
                            ln_sqrt(2, c - 1)
                            if c >= 3:
                                transposed_hi(3, c - 3)
                            ln_sqrt(3, c - 1)
                        elif c == T:
                            transposed_hi(1, 1)
                    c, rest = divmod(u - OUT_LAG[l], H)
                    if l == 0 and rest == 0 and 1 <= c <= T:
                        ln_sqrt(1, c - 1)

            dense(0)
            for t in range(2, T):
                transposed_hi(1, t)
            weights_hi([5, 6, 7])

            act.wait_ge(edge_done[1], 1)

            def features(o, src):
                after(act.activation(o, src, ACT.Relu, scale=1.0 / 16))
                return act.activation(o, o, ACT.Copy, bias=1e-3)

            for n, (kind, r, h, i) in enumerate(MIX_STEPS):
                act.wait_ge(mix_full, n + 1)
                b, m = mix_bank(n), r % 2
                if (kind, r, h, i) == ("qp", 0, 0, 0):
                    act.wait_ge(tables_written, 2 * TABLES)
                if kind in ("q", "k"):
                    which, dstt = (0, mix_qt) if kind == "q" else (1, mix_kt)
                    c0, c1 = MIX_COLS[i]
                    last = act.activation(dstt[:, m, c0:c1], ps[:, b, 0:c1 - c0], ACT.Identity,
                                          bias=qk_bias[:, which * KC + r:which * KC + r + 1])
                elif kind == "v":
                    t0, t1 = (0, 4) if i == 0 else (4, T)
                    last = act.copy(mix_v[:, m, t0:t1, :, 0:MD],
                                    ps[0:P, b, 0:(t1 - t0) * 128].rearrange("p (t h d) -> p t h d", h=2, d=MD))
                elif kind == "kp":
                    t0, t1 = 2 * i, min(2 * i + 2, T)
                    last = features(mix_kp[:, h, t0:t1, :], ps[0:P, b, 0:(t1 - t0) * MF].rearrange("p (t m) -> p t m", m=MF))
                elif kind == "qp":
                    c0, c1 = MIX_COLS[i % 2]
                    last = features(mix_qp[:, h, i // 2, c0:c1], ps[:, b, 0:c1 - c0])
                elif kind == "kv":
                    last = act.copy(mix_kv[:, h, :, :], ps[:, b, 0:2 * (MD + 1)].rearrange("p (m d) -> p m d", m=2))
                else:
                    last = act.copy(mix_out[:, :, 2 * r + h, :], ps[0:P, b, 0:T * (MD + 1)].rearrange("p (t d) -> p t d", t=T))
                last.then_inc(mix_used, 1)

            act.wait_ge(mixo_done, T)
            weights_hi([8, 9])
            for t in range(T):
                transposed_hi(2, t)
            act.wait_ge(small_loaded, 48)
            act.copy(gate_w_hi[:, :, :], gate_w_raw[:, :, :]).then_inc(gw_hi, 1)
            def split_hi(g, qs):
                for q in qs:
                    if g is None:
                        act.wait_ge(eraw_loaded[q % 4], 16 * (q // 4 + 1))
                    else:
                        act.wait_ge(eraw_loaded[q], 16 * g + 16 * (3, 3, 2, 2, 1, 1)[q])
                    src = raws[q % 4 if g is None else q]
                    m, h = q // 2, q % 2
                    act.copy(we[:, 2 * m, h * PIECE:(h + 1) * PIECE], src).then_inc(e_hi, 1)

            dense(1)
            split_hi(None, (0, 1))
            transposed_hi(3, 3)
            transposed_hi(3, 4)
            split_hi(None, (2, 3))
            act.wait_ge(gate_full, 1)
            act.activation(gate_s[:, :, :], ps[0:P, 7, 0:T * 8].rearrange("p (t e) -> p t e", t=T), ACT.Exp,
                           scale=-1.0).then_inc(gate_exp, 1)

            act.wait_ge(xf_stored, 16 * T)
            split_hi(None, (4, 5))
            for j in range(IC):
                a = 4 * (j % 2)
                act.wait_ge(up_full, j + 1)
                if j >= 2:
                    act.wait_ge(hid_lo, j - 1)
                act.activation(silu[:, j % 2, 0:314], ps[:, a, 0:314], ACT.Silu)
                act.activation(silu[:, j % 2, 314:TP], ps[:, a + 1, 0:312], ACT.Silu).then_inc(silu_done, 1)
                act.wait_ge(hid_f, j + 1)
                act.copy(hid[:, 0, j, :], silu[:, j % 2, :]).then_inc(hid_hi, 1)

            def tokens_hi(g, parity):
                for b in range(BL):
                    act.wait_ge(tg_full, BL * g + b + 1)
                    act.copy(atg[parity][:, 0, :, b * 128:(b + 1) * 128], tg_psum(b)).then_inc(tg_hi, 1)

            def start():
                act.wait_ge(up_full, IC)
                split_hi(0, range(4))
                tokens_hi(0, 0)

            def body(g, parity):
                act.wait_ge(down_full, 4 * g + 10)
                split_hi(g, (4, 5))
                act.wait_ge(w1_used, g + 1)
                split_hi(g + 1, (0, 1))
                for j in range(IC):
                    if j == IC - 2:
                        tokens_hi(g + 1, 1 - parity)
                    act.wait_ge(up_full, 4 * g + IC + j + 1)
                    act.wait_ge(hid_lo, 4 * g + IC + j - 1)
                    act.activation(silu[:, j % 2, 0:CAP], ps[:, j, 0:CAP], ACT.Silu).then_inc(silu_done, 1)
                    act.wait_ge(hid_f, 4 * g + IC + j + 1)
                    act.copy(hid_s[:, 0, j, :], silu[:, j % 2, 0:CAP]).then_inc(hid_hi, 1)
                split_hi(g + 1, (2, 3))

            jobs(act, start, body)

        @block.vector
        def _(dve):
            ticks = [0]

            def after(ins):
                ticks[0] += 1
                ins.then_inc(step, 1)
                dve.wait_ge(step, ticks[0])

            def ln_stats(t, src):
                for h in range(2):
                    last = dve.bn_stats(stats[:, t, h, :], src[:, h * HALF:(h + 1) * HALF])
                after(last)
                dve.bn_aggr(mv[:, t, :], stats[:, t, :, :].rearrange("p a b -> p (a b)")).then_inc(ln_var, 1)

            def ln_rstd(n, t):
                dve.wait_ge(ln_std, ln_count(n, t))
                after(dve.reciprocal(rstd[:, t:t + 1], std[:, t:t + 1]))

            def normalise(t, src, dst):
                return dve.tensor_scalar(dst, src, mv[:, t, 0:1], rstd[:, t:t + 1], ALU.subtract, ALU.mult)

            def normalise_rows(t, v):
                after(dve.scalar_tensor_tensor(out=v, in0=v, scalar=mv[:, t, 0:1], in1=rows[:, 0, :],
                                               op0=ALU.subtract, op1=ALU.mult))
                return dve.scalar_tensor_tensor(out=v, in0=v, scalar=rstd[:, t:t + 1], in1=rows[:, 1, :],
                                                op0=ALU.mult, op1=ALU.add)

            def transposed_lo(n, t):
                cols = slice(t * P, (t + 1) * P)
                dve.wait_ge(tr_hi, n * T + t + 1)
                dve.tensor_tensor(at[:, 1, :, cols], tr_psum(n, t), at[:, 0, :, cols].bitcast(F32), ALU.subtract).then_inc(tr_lo, 1)

            def weights_lo(qs):
                for q in qs:
                    dve.wait_ge(w_hi, q + 1)
                    dve.tensor_tensor(wp[q][:, 1, :, :], wraw[q][:, :, :], wp[q][:, 0, :, :].bitcast(F32),
                                      ALU.subtract).then_inc(w_lo, 1)

            def products_out(q, dest, bias_row, name, attention=False, tiles=range(T)):
                h = q % 2
                dve.wait_ge(rows_loaded[name], 48 if name == "gat1" else 16)
                for t in tiles:
                    u = 5 * q + t
                    dve.wait_ge(mm_full, u + 1)
                    dve.tensor_tensor(dest[:, t, h * HALF:(h + 1) * HALF], ps[0:P, u % 4, 0:HALF],
                                      rows[:, bias_row, h * HALF:(h + 1) * HALF], ALU.add).then_inc(mm_used, 1)
                    if attention:
                        dve.wait_ge(mm_used, u + 1)
                        heads = HL[q // 4]
                        DH = D // heads
                        for a in range(heads * h // 2, heads * (h + 1) // 2):
                            part = slice(a * DH, (a + 1) * DH)
                            last = dve.tensor_tensor_reduce(elu_o_t[:, part], dest[:, t, part], rows[:, 2, part], 0.2, 0.0,
                                                            ALU.mult, ALU.add, dest[:, t, D + a:D + a + 1])
                        if h == 1:
                            last.then_inc(ext_ready, 1)

            def first_indices():
                dve.tensor_copy(idx_cur[:, :, 0], src_i[:, 0:G])
                dve.tensor_copy(idx_cur[:, :, 1], dst_i[:, 0:G]).then_inc(prep_done, 1)

            for t in range(T + 3):
                if t < T:
                    dve.wait_ge(x_loaded[t], 16)
                    ln_stats(t, b1[:, t, :])
                if 1 <= t <= T:
                    ln_rstd(0, t - 1)
                    normalise(t - 1, b1[:, t - 1, :], b1[:, t - 1, :]).then_inc(ln_done, 1)
                if t == T:
                    weights_lo([0])
                if t >= 3:
                    transposed_lo(0, t - 3)
            weights_lo([1])
            products_out(0, fs, 0, "gat1", attention=True)
            dve.wait_ge(idx_loaded, 32)
            dve.wait_ge(const_ready, 3)
            dve.tensor_copy(iota_h[:, :], iota_i[:, :])
            dve.tensor_copy(src_f[:, :], src_i[:, :])
            dve.tensor_copy(dst_f[:, :], dst_i[:, :])
            dve.memset(idx_all[:, ET - G:ET, 0:2], 0)
            dve.tensor_copy(idx_all[:, 0:ET - G, 0], src_i[:, G:ET])
            dve.tensor_copy(idx_all[:, 0:ET - G, 1], dst_i[:, G:ET])
            dve.memset(ones_row[:, :], 1.0)
            after(dve.memset(cw[:, :, 8:9], 1.0))
            after(dve.scalar_tensor_tensor(out=idx_all[:, :, 2], in0=dst_f[:, :], scalar=float(N), in1=src_f[:, :],
                                           op0=ALU.mult, op1=ALU.add))
            dve.tensor_scalar(dst_bias[:, :], dst_f[:, :], -0.25, None, ALU.mult)
            first_indices()
            dve.wait_ge(dispatch_const, 2)
            dve.tensor_copy(numbers[:, :], iota_i[0:P, 0:128])
            dve.tensor_copy(token_f[:, :, :, :], token_i[:, :, :, :])
            dve.tensor_copy(empty_f[:, :], empty_i[:, :])

            weights_lo([2])
            products_out(1, fs, 0, "gat1", attention=True)
            weights_lo([3])
            products_out(2, fd_stage, 1, "gat1", attention=True)
            products_out(3, fd_stage, 1, "gat1", attention=True)

            def edges_first():
                DH = D // HEADS1
                dve.wait_ge(prep_done, 1)

                def head(i, j, first):
                    t = i * G + j
                    one = slice(t, t + 1) if isinstance(t, int) else bass.ds(t, 1)
                    if not first:
                        dve.wait_ge(hot_used, t - G + 1)
                    dve.tensor_scalar(hot_s[:, j, :], iota_h[0:P, :], src_f[:, one], None, ALU.is_equal).then_inc(hot_ready, 1)
                    dve.wait_ge(gathered[0][j], 32 * (i + 1))
                    if not first:
                        dve.wait_ge(scattered[0], 16 * (t - G + 1))
                    dve.tensor_copy(idx_cur[:, j, :], idx_all[:, one, :].rearrange("p a b -> p (a b)"))
                    dve.tensor_tensor(ring_s[:, j, :], ring_s[:, j, :], ring_d[:, j, :], ALU.add).then_inc(z_ready, 1)

                def tail(t, j):
                    dve.wait_ge(relu_ready, t + 1)
                    for h in range(HEADS1):
                        part = slice(h * DH, (h + 1) * DH)
                        last = dve.tensor_tensor_reduce(ring_d[:, j, part], ring_s[:, j, part], rows[:, 2, part], 1.0,
                                                        ring_s[:, j, D + h:D + h + 1], ALU.mult, ALU.add,
                                                        logits[:, j, h:h + 1])
                    last.then_inc(edge_done[0], 1)

                for j in range(G):
                    head(0, j, True)
                    if j > 0:
                        tail(j - 1, j - 1)
                with dve.Fori(1, NG) as i:
                    for j in range(G):
                        head(i, j, False)
                        tail(G * i + j - 1, (j - 1) % G)
                tail(ET - 1, G - 1)

            def edges_second():
                done = [0]
                dve.wait_ge(prep_done, 2)
                after(dve.tensor_scalar(rows[:, 2, :], rows[:, 2, :], 0.8, None, ALU.mult))

                def tile(i, j, first, base):
                    t = i * G + j
                    one = slice(t, t + 1) if isinstance(t, int) else bass.ds(t, 1)
                    n = base + 2 * t
                    dve.wait_ge(gathered[1][j], 32 * (i + 1))
                    if not first:
                        dve.wait_ge(scattered[1], 16 * (t - G + 1))
                    dve.tensor_copy(idx_cur[:, j, :], idx_all[:, one, :].rearrange("p a b -> p (a b)"))
                    dve.tensor_tensor(ring_s[:, j, 0:D + 1], ring_s[:, j, 0:D + 1], ring_d[:, j, 0:D + 1], ALU.add).then_inc(step, 1)
                    dve.wait_ge(step, n + 1)
                    dve.scalar_tensor_tensor(out=ring_d[:, j, 0:D], in0=ring_s[:, j, 0:D], scalar=0.0, in1=rows[:, 2, :],
                                             op0=ALU.max, op1=ALU.mult, accum_out=relu_dot[:, j:j + 1]).then_inc(step, 1)
                    dve.wait_ge(step, n + 2)
                    dve.tensor_tensor(logits[:, j, 0:1], relu_dot[:, j:j + 1], ring_s[:, j, D:D + 1], ALU.add).then_inc(edge_done[1], 1)

                base = ticks[0]
                for j in range(G):
                    tile(0, j, True, base)
                with dve.Fori(1, NG - 3) as i:
                    for j in range(G):
                        tile(i, j, False, base)

                def divide():
                    dve.wait_ge(mix_used, len(MIX_STEPS))
                    dve.reciprocal(mix_rden[:, :, :], mix_out[:, :, :, MD]).then_inc(mixr_done, 1)
                    dve.wait_ge(mixr_done, 1)
                    for t in range(T):
                        dve.tensor_tensor(b1[:, t, :].rearrange("p (h d) -> p h d", d=MD), mix_out[:, t, :, 0:MD],
                                          mix_rden[:, t, :].unsqueeze(2).to_broadcast([P, MH, MD]), ALU.mult).then_inc(mixo_done, 1)

                DIV_AT, TR_AT = 2, 4
                for n in range(3 * G):
                    tile(NG - 3 + n // G, n % G, False, base)
                    if n == DIV_AT:
                        divide()
                    if n in (DIV_AT + 2, DIV_AT + 3):
                        weights_lo([8 + n - DIV_AT - 2])
                    if n == DIV_AT + TR_AT:
                        for t in range(T):
                            transposed_lo(2, t)
                    if n > DIV_AT + TR_AT + 1:
                        u = n - DIV_AT - TR_AT - 2
                        products_out(8 + u // T, x2, 3, "proj", tiles=(u % T,))
                for u in range(3 * G - DIV_AT - TR_AT - 2, 2 * T):
                    products_out(8 + u // T, x2, 3, "proj", tiles=(u % T,))
                ticks[0] = base + 2 * ET

            edges_first()

            def dense(l, dest):
                H = HL[l]
                DH = D // H
                elu_o, elu_m = (elu_o_t[:, :], elu_m_t[:, :]) if l == 0 else (elu_o2[:, :], elu_m2[:, :])

                def maxima(c, h0, h1):
                    if h0 == 0:
                        dve.wait_ge(dl_loaded[l][(c % 2, c)[l]], 16 * (c // 2 + 1) if l == 0 else 16)
                    lv = dl1[c % 2][:, :].rearrange("p (s h) -> p h s", h=H) if l == 0 else dl2[:, c:c + 1, :]
                    return dve.tensor_reduce(mxv[:, c, h0:h1], lv[:, h0:h1, :], AX.X, ALU.max)

                def negate(c, h0=0, h1=H):
                    dve.tensor_scalar(mxv[:, c, h0:h1], mxv[:, c, h0:h1], -1.0, None, ALU.mult).then_inc(max_ready[l], 1)

                def probs(u):
                    c, h = divmod(u, H)
                    dve.wait_ge(exp_ready[l], u + 1)
                    e = dl1[2 + c % 2][:, h, :] if l == 0 else dl2[:, c, :]
                    dve.tensor_tensor_reduce(e, e, counts[:, c, :], 1.0, 0.0, ALU.mult, ALU.add,
                                             den[:, c, h:h + 1]).then_inc(probs_ready[l], 1)

                if l == 0:
                    for h in range(0, H, 2):
                        after(maxima(0, h, h + 2))
                        negate(0, h, h + 2)
                else:
                    for c in range(T):
                        after(maxima(c, 0, 1))
                        negate(c)
                    for u in range(T):
                        probs(u)
                for u in range(H * T + OUT_LAG[l] + (2 if l == 0 else 0)):
                    if l == 0 and u < H * T:
                        c, h = divmod(u, H)
                        probs(u)
                        if c + 1 < T and 1 <= h <= 4:
                            last = maxima(c + 1, 2 * (h - 1), 2 * h)
                            if h == 4:
                                after(last)
                                negate(c + 1)
                    if l == 1 and u == 0:
                        dve.memset(at[:, :, :, N:TP].bitcast(F32), 0.0)
                        dve.wait_ge(xagain_loaded, 16)
                        dve.wait_ge(mm_used, 50)
                        for t in range(T):
                            last = dve.tensor_tensor(x2[:, t, :], x2[:, t, :], b1[:, t, :], ALU.add)
                        last.then_inc(xagain_used, 1)
                        dve.wait_ge(xagain_used, 1)
                    c, rest = divmod(u - NORM_LAG[l] + 1, H)
                    if l == 0 and rest == 0 and c == T:
                        weights_lo([4])
                    if rest == 0 and 1 <= c <= T:
                        c -= 1
                        dve.wait_ge(probs_ready[l], H * (c + 1))
                        after(dve.tensor_scalar(rden[:, c, 0:H], den[:, c, 0:H], 1e-30, None, ALU.max))
                        after(dve.reciprocal(rden[:, c, 0:H], rden[:, c, 0:H]))
                        dve.wait_ge(agg_full[l], H * (c + 1))
                        pv = ps[0:P, 4 + 2 * (c % 2):6 + 2 * (c % 2), 0:HALF]
                        if H == 1:
                            last = dve.tensor_scalar(elu_o.rearrange("p (a d) -> p a d", a=2), pv, rden[:, c, 0:1], None, ALU.mult)
                        else:
                            for b in range(2):
                                last = dve.tensor_tensor(
                                    elu_o[:, b * HALF:(b + 1) * HALF].rearrange("p (h d) -> p h d", d=DH),
                                    pv[:, b, :].rearrange("p (h d) -> p h d", d=DH),
                                    rden[:, c, 4 * b:4 * b + 4].unsqueeze(2).to_broadcast([P, 4, DH]), ALU.mult)
                        after(last)
                        dve.tensor_scalar(elu_m, elu_o, 0.0, None, ALU.min).then_inc(elu_min[l], 1)
                        if l == 0:
                            last = dve.scalar_tensor_tensor(out=elu_o, in0=elu_o, scalar=0.0, in1=b1[:, c, :],
                                                            op0=ALU.max, op1=ALU.add)
                        else:
                            last = dve.tensor_scalar(elu_o, elu_o, 0.0, -1.0, ALU.max, ALU.add)
                        last.then_inc(elu_max[l], 1)
                    c, rest = divmod(u - OUT_LAG[l] + 1, H)
                    if rest == 0 and 1 <= c <= T:
                        c -= 1
                        dve.wait_ge(elu_exp[l], c + 1)
                        dve.wait_ge(elu_max[l], c + 1)
                        if l == 0:
                            last = dve.scalar_tensor_tensor(out=dest[:, c, :], in0=elu_m, scalar=-1.0, in1=elu_o,
                                                            op0=ALU.add, op1=ALU.add)
                        else:
                            last = dve.tensor_tensor(dest[:, c, :], elu_m, elu_o, ALU.add)
                        last.then_inc(out_ready[l], 1)
                        dve.wait_ge(out_ready[l], c + 1)
                        if l == 1:
                            finish(c)
                        else:
                            ln_stats(c, b1[:, c, :])
                    if l == 0 and u in (H * T + 4, H * T + 6):
                        transposed_lo(1, (u - H * T - 4) // 2)
                    c, rest = divmod(u - OUT_LAG[l] - 1, H)
                    if l == 0 and rest == 0 and 1 <= c <= T:
                        if c == 1:
                            dve.wait_ge(rows_loaded["ln1"], 32)
                        ln_rstd(1, c - 1)
                        normalise_rows(c - 1, b1[:, c - 1, :]).then_inc(ln_done, 1)

            def finish(c):
                o = gnn[:, c, :]
                ln_stats(c, o)
                ln_rstd(2, c)
                after(normalise_rows(c, o))
                after(dve.tensor_tensor(x2[:, c, :], x2[:, c, :], o, ALU.add))
                if c >= 2:
                    transposed_lo(3, c - 2)
                ln_stats(c, x2[:, c, :])
                ln_rstd(3, c)
                normalise(c, x2[:, c, :], xf[:, c, :]).then_inc(ln_done, 1)

            dve.wait_ge(counts_ready, 1)
            dve.wait_ge(scattered[0], 16 * ET)
            first_indices()
            dense(0, b1)
            for t in range(2, T):
                transposed_lo(1, t)
            weights_lo([5])
            dve.wait_ge(rows_loaded["attn2"], 16)
            products_out(4, fs, 3, "gat2s", attention=True)
            weights_lo([6])
            products_out(5, fs, 3, "gat2s", attention=True)
            weights_lo([7])
            products_out(6, fd_stage, 1, "gat2d", attention=True)
            products_out(7, fd_stage, 1, "gat2d", attention=True)
            dve.memset(mix_v[:, :, :, :, MD:MD + 1], 1.0).then_inc(prep_done, 1)
            edges_second()
            dve.wait_ge(rows_loaded["ln2"], 32)
            dve.wait_ge(gw_hi, 1)
            dve.tensor_tensor(gate_w_lo[:, :, :], gate_w_raw[:, :, :], gate_w_hi[:, :, :].bitcast(F32), ALU.subtract).then_inc(gw_lo, 1)
            dense(1, gnn)
            def split_lo(g, qs):
                for q in qs:
                    dve.wait_ge(e_hi, q + 1 if g is None else 6 * g + 6 + q + 1)
                    src = raws[q % 4 if g is None else q]
                    m, h = q // 2, q % 2
                    part = slice(h * PIECE, (h + 1) * PIECE)
                    dve.tensor_tensor(we[:, 2 * m + 1, part], src, we[:, 2 * m, part].bitcast(F32),
                                      ALU.subtract).then_inc(e_lo, 1)

            split_lo(None, (0, 1))
            transposed_lo(3, 3)
            transposed_lo(3, 4)

            split_lo(None, (2, 3))

            def cmp(o, a, b, op):
                after(dve.tensor_tensor(o, a, b, op))

            dve.wait_ge(gate_exp, 1)
            after(dve.tensor_scalar(gate_s[:, :, :], gate_s[:, :, :], 1.0, None, ALU.add))
            after(dve.reciprocal(gate_s[:, :, :], gate_s[:, :, :]))
            after(dve.tensor_tensor(gate_k[:, :, :], gate_s[:, :, :], gate_b[:, :].unsqueeze(1).to_broadcast([P, T, 8]), ALU.add))
            pairs = gate_k[:, :, :].rearrange("p t (g e) -> p t g e", e=2)
            after(dve.tensor_tensor(gate_g[:, :, :], pairs[:, :, :, 0], pairs[:, :, :, 1], ALU.add))

            def ranks(score, n):
                after(dve.memset(gate_r[:, :, 0:n], 0.0))
                for i in range(n):
                    o = score[:, :, i:i + 1]
                    if i > 0:
                        dve.tensor_tensor(gate_t[:, :, 0:i], o.to_broadcast([P, T, i]), score[:, :, 0:i], ALU.is_gt)
                    if i + 1 < n:
                        dve.tensor_tensor(gate_t[:, :, i + 1:n], o.to_broadcast([P, T, n - i - 1]), score[:, :, i + 1:n], ALU.is_ge)
                    after(dve.memset(gate_t[:, :, i:i + 1], 0.0))
                    after(dve.tensor_tensor(gate_r[:, :, 0:n], gate_r[:, :, 0:n], gate_t[:, :, 0:n], ALU.add))

            ranks(gate_g, 4)
            after(dve.tensor_scalar(gate_t[:, :, 0:4], gate_r[:, :, 0:4], 2.0, -BIG, ALU.is_ge, ALU.mult))
            gt2 = gate_t[:, :, 0:4].unsqueeze(3).to_broadcast([P, T, 4, 2])
            after(dve.tensor_tensor(pairs, pairs, gt2, ALU.add))
            ranks(gate_k, 8)
            after(dve.tensor_scalar(gate_t[:, :, :], gate_r[:, :, :], 2.0, None, ALU.is_lt))
            after(dve.tensor_tensor(gate_s[:, :, :], gate_s[:, :, :], gate_t[:, :, :], ALU.mult))
            after(dve.tensor_reduce(gate_g[:, :, 0:1].rearrange("p t a -> p (t a)"), gate_s[:, :, :], AX.X, ALU.add))
            after(dve.tensor_scalar(gate_g[:, :, 0:1], gate_g[:, :, 0:1], 1e-6, None, ALU.add))
            after(dve.reciprocal(gate_g[:, :, 0:1], gate_g[:, :, 0:1]))
            after(dve.tensor_tensor(cw[:, :, 0:8], gate_s[:, :, :], gate_g[:, :, 0:1].to_broadcast([P, T, 8]), ALU.mult))

            dve.tensor_scalar(routed[:, :, :], gate_r[:, :, :], 2.0, None, ALU.is_lt).then_inc(routed_ready, 1)

            def entry(j, values, o):
                after(dve.tensor_scalar(step_f[:, :, :], gate_r[:, :, :], float(j), None, ALU.is_equal))
                after(dve.tensor_tensor(step_f[:, :, :], step_f[:, :, :], values, ALU.mult))
                after(dve.tensor_reduce(o, step_f[:, :, :], AX.X, ALU.add))

            for j in range(2):
                entry(j, cw[:, :, 0:8], choice[:, 2, :, j])
            after(dve.memset(before[:, 0, :], 0.0))

            def places():
                dve.wait_ge(place_full, 1)
                dve.tensor_copy(place[:, :, :], ps[0:P, 3, 320:360].rearrange("p (t e) -> p t e", t=T))
                dve.tensor_copy(step_f[:, :, :], ps[0:P, 3, 360:400].rearrange("p (t e) -> p t e", t=T)).then_inc(place_read, 1)
                dve.wait_ge(place_read, 1)
                for t in range(T):
                    after(dve.tensor_tensor(before[:, t + 1, :], before[:, t, :], step_f[:, t, :], ALU.add))
                after(dve.tensor_scalar(job_count[:, :], before[:, T, :], 0.0, None, ALU.is_gt))
                for m in range(CAP, N, CAP):
                    after(dve.scalar_tensor_tensor(out=job_count[:, :], in0=before[:, T, :], scalar=float(m),
                                                   in1=job_count[:, :], op0=ALU.is_gt, op1=ALU.add))
                after(dve.memset(job_end[:, 0:1], 0.0))
                for e in range(ROUTED):
                    after(dve.tensor_tensor(job_end[:, e + 1:e + 2], job_end[:, e:e + 1], job_count[:, e:e + 1], ALU.add))
                after(dve.tensor_tensor(job_cmp[:, :, :], numbers[:, 0:JOBS + 1].unsqueeze(2).to_broadcast([P, JOBS + 1, 8]),
                                        job_end[:, 1:9].unsqueeze(1).to_broadcast([P, JOBS + 1, 8]), ALU.is_ge))
                after(dve.tensor_reduce(job_expert_f[:, :], job_cmp[:, :, :], AX.X, ALU.add))
                dve.tensor_copy(job_expert[:, :], job_expert_f[:, :])
                dve.tensor_copy(jobs_i[:, :], job_end[:, 8:9]).then_inc(jobs_ready, 1)
                after(dve.tensor_tensor(place[:, :, :], place[:, :, :], before[:, 0:T, :], ALU.add))
                after(dve.tensor_scalar(list_block[:, :, :], job_end[:, 0:8].unsqueeze(1).to_broadcast([P, T, 8]), float(BL), None, ALU.mult))
                after(dve.tensor_scalar(blocks_f[:, :, :], place[:, :, :], 128.0, None, ALU.is_ge))
                for m in range(256, N, 128):
                    after(dve.scalar_tensor_tensor(out=blocks_f[:, :, :], in0=place[:, :, :], scalar=float(m),
                                                   in1=blocks_f[:, :, :], op0=ALU.is_ge, op1=ALU.add))
                dve.scalar_tensor_tensor(out=place[:, :, :], in0=blocks_f[:, :, :], scalar=-128.0, in1=place[:, :, :],
                                         op0=ALU.mult, op1=ALU.add)
                after(dve.tensor_tensor(list_block[:, :, :], list_block[:, :, :], blocks_f[:, :, :], ALU.add))
                for j in range(2):
                    entry(j, place[:, :, :], choice[:, 0, :, j])
                    entry(j, list_block[:, :, :], choice[:, 1, :, j])
                def of_choice(c, width):
                    return choice[:, c, :, :].rearrange("p t j -> p (t j)").unsqueeze(2).to_broadcast([P, 2 * T, width])

                dve.tensor_tensor(slot_hot[:, :, :], numbers[:, :].unsqueeze(1).to_broadcast([P, 2 * T, 128]), of_choice(0, 128), ALU.is_equal)
                after(dve.tensor_tensor(block_hot[:, :, :], numbers[:, 0:NB].unsqueeze(1).to_broadcast([P, 2 * T, NB]), of_choice(1, NB), ALU.is_equal))
                for c in range(3):
                    v = (of_choice(2, NB) if c == 2 else
                         token_f[:, :, :, c].rearrange("p t j -> p (t j)").unsqueeze(2).to_broadcast([P, 2 * T, NB]))
                    last = dve.tensor_tensor(entries[:, :, :, c], block_hot[:, :, :], v, ALU.mult)
                last.then_inc(entries_ready, 1)

            def read_list():
                dve.wait_ge(list_full, 1)
                v = ps[:, 3, 400:400 + 3 * NB].rearrange("p (b c) -> p b c", c=3)
                dve.tensor_copy(lst[:, :, 0], v[:, :, 0])
                dve.tensor_copy(lst[:, :, 2].bitcast(F32), v[:, :, 2])
                after(dve.tensor_scalar(empty_row[:, :], v[:, :, 1], 0.0, empty_f[:, 0:1], ALU.is_equal, ALU.mult))
                dve.scalar_tensor_tensor(out=lst[:, :, 1], in0=v[:, :, 1], scalar=-1.0, in1=empty_row[:, :],
                                         op0=ALU.add, op1=ALU.add).then_inc(list_ready, 1)

            dve.wait_ge(xf_stored, 16 * T)
            split_lo(None, (4, 5))
            for j in range(IC):
                a = 4 * (j % 2) + 2
                dve.wait_ge(silu_done, j + 1)
                dve.tensor_tensor(silu[:, j % 2, 0:314], silu[:, j % 2, 0:314], ps[:, a, 0:314], ALU.mult)
                dve.tensor_tensor(silu[:, j % 2, 314:TP], silu[:, j % 2, 314:TP], ps[:, a + 1, 0:312], ALU.mult).then_inc(hid_f, 1)
                dve.wait_ge(hid_hi, j + 1)
                dve.tensor_tensor(hid[:, 1, j, :], silu[:, j % 2, :], hid[:, 0, j, :].bitcast(F32),
                                  ALU.subtract).then_inc(hid_lo, 1)
                if j == 0:
                    places()
                if j == 2:
                    read_list()
            for u in range(10):
                if u in (0, 4):
                    split_lo(0, (0, 1) if u == 0 else (2, 3))
                t, h = u // 2, u % 2
                dve.wait_ge(down_full, u + 1)
                dve.tensor_tensor(x2[:, t, h * HALF:(h + 1) * HALF], x2[:, t, h * HALF:(h + 1) * HALF],
                                  ps[0:P, down_bank(u), 0:HALF], ALU.add).then_inc(down_used, 1)

            def tokens_lo(g, parity):
                for b in range(BL):
                    cols = slice(b * 128, (b + 1) * 128)
                    dve.wait_ge(tg_hi, BL * g + b + 1)
                    dve.tensor_tensor(atg[parity][:, 1, :, cols], tg_psum(b), atg[parity][:, 0, :, cols].bitcast(F32),
                                      ALU.subtract).then_inc(tg_lo, 1)

            def start():
                tokens_lo(0, 0)

            def body(g, parity):
                split_lo(g, (4, 5))
                split_lo(g + 1, (0, 1))
                for j in range(IC):
                    if j == IC - 2:
                        tokens_lo(g + 1, 1 - parity)
                    dve.wait_ge(silu_done, 4 * g + IC + j + 1)
                    v = silu[:, j % 2, 0:CAP]
                    dve.tensor_tensor(v, v, ps[:, j, CAP:2 * CAP], ALU.mult).then_inc(hid_f, 1)
                    dve.wait_ge(hid_hi, 4 * g + IC + j + 1)
                    dve.tensor_tensor(hid_s[:, 1, j, :], v, hid_s[:, 0, j, :].bitcast(F32), ALU.subtract).then_inc(hid_lo, 1)
                split_lo(g + 1, (2, 3))
                if not first(g):
                    dve.wait_ge(landed, 16 * BL * g)
                for u in range(4):
                    b, h = u // 2, u % 2
                    w = lst[:, bass.ds(BL * g + b, 1), 2].bitcast(F32)
                    dve.wait_ge(down_full, 4 * g + 10 + u + 1)
                    dve.tensor_scalar(y_sb[b][:, h * HALF:(h + 1) * HALF], ps[:, 4 + u, 0:HALF], w, None, ALU.mult).then_inc(down_used, 1)

            jobs(dve, start, body)

            for t in range(T):
                dve.wait_ge(y_loaded[t], 16)
                for j in range(2):
                    dve.tensor_tensor(x2[:, t, :], x2[:, t, :], y_in[:, t, j, :], ALU.add).then_inc(sum_done, 1)
                    if j == 0:
                        dve.wait_ge(sum_done, 2 * t + 1)

        @block.tensor
        def _(pe):
            def mm3(o, lt, r, start, stop):
                pe.matmul(o, lt(0), r(0), start=start, stop=False)
                pe.matmul(o, lt(0), r(1), start=False, stop=False)
                return pe.matmul(o, lt(1), r(0), start=False, stop=stop)

            def transposes(n, t, src):
                if n == 2:
                    pe.wait_ge(mixo_done, t + 1)
                else:
                    pe.wait_ge(ln_done, (n - (n == 3)) * T + t + 1)
                back = (4, 1, 2, 2)[n]
                if t >= back:
                    pe.wait_ge(tr_lo, n * T + t - back + 1)
                elif n == 1:
                    pe.wait_ge(elu_min[0], 4)
                elif n == 3:
                    pe.wait_ge(pt_copied[1], T)
                for k in range(KC):
                    last = pe.transpose(tr_psum(n, t)[:, k, :], src[:, t, k * 128:(k + 1) * 128], ident[0:P, 0:P])
                last.then_inc(tr_full, 1)

            def products(q, n, tiles=range(T)):
                pe.wait_ge(w_lo, q + 1)
                for t in tiles:
                    pe.wait_ge(tr_lo, n * T + t + 1)
                    u = 5 * q + t
                    if u >= 4:
                        pe.wait_ge(mm_used, u - 3)
                    for k in range(KC):
                        last = mm3(ps[0:P, u % 4, 0:HALF],
                                   lambda s: at[:, s, k, t * P:(t + 1) * P],
                                   lambda s: wp[q][:, s, k, :], k == 0, k == KC - 1)
                    last.then_inc(mm_full, 1)

            pe.wait_ge(const_ready, 2)
            for t in range(T):
                transposes(0, t, b1)
            pe.wait_ge(tr_lo, 4)
            for q in range(4):
                products(q, 0)

            pe.wait_ge(mm_used, 20)
            pe.wait_ge(prep_done, 1)
            pe.wait_ge(hot_ready, 1)
            pe.wait_ge(hot_d_ready, 1)
            cbanks = [(c, 0, 0, 512) for c in range(T)] + [(5 if c < 4 else 6, c * 113 if c < 4 else 0, 512, N) for c in range(T)]

            def count(j, start):
                for n, (b, o, s0, s1) in enumerate(cbanks):
                    c = n % T
                    last = pe.matmul(ps[0:P, b, o:o + s1 - s0], hot_d[:, j, c * P:(c + 1) * P], hot_s[:, j, s0:s1],
                                     start=start and (n <= 5 or n == 9), stop=False, skip_group_check=True)
                last.then_inc(hot_used, 1)

            count(0, True)
            for j in range(1, G):
                pe.wait_ge(hot_ready, j + 1)
                pe.wait_ge(hot_d_ready, j + 1)
                count(j, False)
            with pe.Fori(1, NG) as i:
                for j in range(G):
                    pe.wait_ge(hot_ready, G * i + j + 1)
                    pe.wait_ge(hot_d_ready, G * i + j + 1)
                    count(j, False)

            def dense(l):
                H = HL[l]
                DH = D // H
                pt = dl1[5] if l == 0 else dpt2
                for u in range(H * T + AGG_LAG):
                    if u < H * T:
                        c, h = divmod(u, H)
                        pe.wait_ge(probs_ready[l], u + 1)
                        if u >= 2:
                            pe.wait_ge(pt_copied[l], u - 1)
                        e = dl1[2 + c % 2][:, h, :] if l == 0 else dl2[:, c, :]
                        for s in range(T):
                            last = pe.transpose(pt_psum(u)[:, s * P:(s + 1) * P], e[:, s * P:(s + 1) * P], ident[0:P, 0:P])
                        last.then_inc(pt_full[l], 1)
                    v = u - AGG_LAG
                    if v >= 0:
                        c, h = divmod(v, H)
                        m = v % PT_SLOTS
                        pe.wait_ge(pt_copied[l], v + 1)
                        if h == 0 and c >= 2:
                            pe.wait_ge(elu_min[l], c - 1)
                        for part in range(1 if H > 1 else 2):
                            w = DH if H > 1 else HALF
                            col = h * DH + part * HALF
                            o = ps[0:P, 4 + 2 * (c % 2) + col // HALF, col % HALF:col % HALF + w]
                            for s in range(T):
                                last = pe.matmul(o, pt[:, m * N + s * P:m * N + (s + 1) * P], fs[:, s, col:col + w],
                                                 start=s == 0, stop=s == T - 1)
                        last.then_inc(agg_full[l], 1)
                        if l == 1 and c >= 2:
                            transposes(3, c - 2, xf)

            pe.wait_ge(counts_ready, 1)
            dense(0)
            transposes(1, 0, b1)
            transposes(1, 1, b1)
            pe.wait_ge(pt_copied[0], HEADS1 * T)
            for t in range(T):
                products(4, 1, (t,))
                if t + 2 < T:
                    transposes(1, t + 2, b1)
            for q in range(5, 8):
                products(q, 1)

            pe.wait_ge(mm_used, 40)
            pe.wait_ge(prep_done, 3)

            pe.wait_ge(mixc_loaded, 48)

            def emptied(kind, r, h):
                pe.wait_ge(mix_used, mix_count(kind, r, h))

            for n, (kind, r, h, i) in enumerate(MIX_STEPS):
                b, m = mix_bank(n), r % 2
                before = [k for k in range(n) if mix_bank(k) == b]
                if before:
                    pe.wait_ge(mix_used, before[-1] + 1)
                hp = slice(h * MD, (h + 1) * MD)
                if kind in ("q", "k"):
                    if kind == "q":
                        pe.wait_ge(mixw_loaded[m], 48 * (r // 2 + 1))
                    s = 0 if kind == "q" else 1
                    c0, c1 = MIX_COLS[i]
                    for k in range(KC):
                        last = pe.matmul(ps[:, b, 0:c1 - c0], mix_w[:, 1 - m, k, s * 128:(s + 1) * 128], xt_v[:, k, c0:c1],
                                         start=k == 0, stop=k == KC - 1)
                elif kind == "v":
                    for x_, t in enumerate(range(4) if i == 0 else range(4, T)):
                        o = ps[0:P, b, x_ * 128:(x_ + 1) * 128]
                        pe.matmul(o, ones_row[:, :], v_row[:, r * 128:(r + 1) * 128], start=True, stop=False)
                        for k in range(KC):
                            last = pe.matmul(o, xt_v[:, k, t * P:(t + 1) * P], mix_w[:, 1 - m, k, 256:384], start=False, stop=k == KC - 1)
                elif kind == "kp":
                    emptied("k", r, 0)
                    for t in range(2 * i, min(2 * i + 2, T)):
                        last = pe.matmul(ps[0:P, b, (t % 2) * MF:(t % 2 + 1) * MF], mix_kt[hp, m, t * P:(t + 1) * P],
                                         pmt[hp, :], start=True, stop=True)
                elif kind == "qp":
                    emptied("q", r, 0)
                    c0, c1 = MIX_COLS[i % 2]
                    last = pe.matmul(ps[:, b, 0:c1 - c0], pmt[hp, (i // 2) * 128:(i // 2 + 1) * 128], mix_qt[hp, m, c0:c1],
                                     start=True, stop=True)
                elif kind == "kv":
                    emptied("v", r, 0)
                    emptied("kp", r, h)
                    for f in range(2):
                        for t in range(T):
                            last = pe.matmul(ps[:, b, f * (MD + 1):(f + 1) * (MD + 1)], mix_kp[:, h, t, f * 128:(f + 1) * 128],
                                             mix_v[:, m, t, h, :], start=t == 0, stop=t == T - 1)
                else:
                    emptied("qp", r, h)
                    emptied("kv", r, h)
                    for t in range(T):
                        for f in range(2):
                            last = pe.matmul(ps[0:P, b, t * (MD + 1):(t + 1) * (MD + 1)], mix_qp[:, h, f, t * P:(t + 1) * P],
                                             mix_kv[:, h, f, :], start=f == 0, stop=f == 1)
                last.then_inc(mix_full, 1)

            for t in range(T):
                transposes(2, t, b1)
            for q in (8, 9):
                products(q, 2)
            pe.wait_ge(mm_used, 50)
            dense(1)

            def gate_product(t):
                pe.wait_ge(tr_lo, 3 * T + t + 1)
                for k in range(KC):
                    last = mm3(ps[0:P, 7, t * 8:(t + 1) * 8], lambda s: at[:, s, k, t * P:(t + 1) * P],
                               lambda s: (gate_w_hi, gate_w_lo)[s][:, k, :], k == 0, k == KC - 1)
                return last

            transposes(3, 3, xf)
            pe.wait_ge(gw_lo, 1)
            pe.wait_ge(elu_min[1], 4)
            for t in range(3):
                gate_product(t)
            transposes(3, 4, xf)
            gate_product(3)
            gate_product(4).then_inc(gate_full, 1)

            w13 = [[we[:, 2 * m + s, :].rearrange("p (k i) -> p k i", i=INTER) for s in range(2)] for m in range(2)]
            w2v = [we[:, 4 + s, :].rearrange("p (k d) -> p k d", d=D) for s in range(2)]

            pe.wait_ge(e_lo, 4)
            for j in range(IC):
                if j == 1:
                    pe.wait_ge(gate_exp, 1)
                if j >= 2:
                    pe.wait_ge(hid_f, j - 1)
                for m in range(2):
                    for n, (a, b_) in enumerate(((0, 314), (314, TP))):
                        bank = 4 * (j % 2) + 2 * m + n
                        if j == 2 and bank == 3:
                            pe.wait_ge(place_read, 1)
                        for k in range(KC):
                            last = mm3(ps[:, bank, 0:b_ - a], lambda s: w13[m][s][:, k, j * 128:(j + 1) * 128],
                                       lambda s: at[:, s, k, a:b_], k == 0, k == KC - 1)
                last.then_inc(up_full, 1)
                if j == 1:
                    pe.wait_ge(hid_f, 1)
                    pe.wait_ge(dispatch_const, 2)
                    pe.wait_ge(routed_ready, 1)
                    rt = routed[:, :, :].rearrange("p t e -> p (t e)")
                    pe.matmul(ps[0:P, 3, 320:360], lower[:, :], rt, start=True, stop=True)
                    pe.matmul(ps[0:P, 3, 360:400], ones[:, :], rt, start=True, stop=True).then_inc(place_full, 1)
            pe.wait_ge(e_lo, 6)
            pe.wait_ge(hid_f, IC - 1)
            pe.wait_ge(entries_ready, 1)
            for n in range(2 * T):
                last = pe.matmul(ps[:, 3, 400:400 + 3 * NB], slot_hot[:, n, :], entries[:, n, :, :].rearrange("p b c -> p (b c)"),
                                 start=n == 0, stop=n == 2 * T - 1)
            last.then_inc(list_full, 1)
            for us in (range(4), range(4, 8), range(8, 10)):
                for k in range(IC):
                    if us[0] == 0:
                        pe.wait_ge(hid_lo, k + 1)
                    for u in us:
                        t, h = u // 2, u % 2
                        if u == 3 and k == 0:
                            pe.wait_ge(list_ready, 1)
                        if u >= 8 and k == 0:
                            pe.wait_ge(down_used, down_bank(u) + 1)
                        last = mm3(ps[0:P, down_bank(u), 0:HALF], lambda s: hid[:, s, k, t * P:(t + 1) * P],
                                   lambda s: w2v[s][:, k, h * HALF:(h + 1) * HALF], k == 0, k == IC - 1)
                        if k == IC - 1:
                            last.then_inc(down_full, 1)

            def transpose_tokens(g):
                for b in range(BL):
                    pe.wait_ge(xg_loaded[b], 16 * g + 16)
                    for k in range(KC):
                        last = pe.transpose(tg_psum(b)[:, k, :], xg[:, b, k * 128:(k + 1) * 128], ident[:, :])
                    last.then_inc(tg_full, 1)

            def start():
                pe.wait_ge(down_used, 10)
                transpose_tokens(0)

            def up(g, parity, m, j):
                for k in range(KC):
                    last = mm3(ps[:, j, m * CAP:(m + 1) * CAP], lambda s: w13[m][s][:, k, j * 128:(j + 1) * 128],
                               lambda s: atg[parity][:, s, k, :], k == 0, k == KC - 1)
                return last

            def body(g, parity):
                pe.wait_ge(e_lo, 6 * g + 6 + 2)
                pe.wait_ge(tg_lo, BL * g + BL)
                for j in range(IC):
                    last = up(g, parity, 0, j)
                last.then_inc(w1_used, 1)
                pe.wait_ge(e_lo, 6 * g + 6 + 4)
                for j in range(IC):
                    if j == IC - 2:
                        pe.wait_ge(down_used, 4 * g + 10)
                        transpose_tokens(g + 1)
                    up(g, parity, 1, j).then_inc(up_full, 1)
                pe.wait_ge(e_lo, 6 * g + 6 + 6)
                pe.wait_ge(tg_lo, BL * g + 2 * BL)
                for k in range(IC):
                    pe.wait_ge(hid_lo, 4 * g + IC + k + 1)
                    for u in range(4):
                        b, h = u // 2, u % 2
                        last = mm3(ps[:, 4 + u, 0:HALF], lambda s: hid_s[:, s, k, b * 128:(b + 1) * 128],
                                   lambda s: w2v[s][:, k, h * HALF:(h + 1) * HALF], k == 0, k == IC - 1)
                        if k == IC - 1:
                            last.then_inc(down_full, 1)

            jobs(pe, start, body)


def mixer_steps():
    def feed(kind, r):
        return [(kind, r, 0, i) for i in range(2)] if r < KC else []

    def features(r, h):
        return [("kp", r, h, i) for i in range(3)] + [("qp", r, h, i) for i in range(4)]

    steps = feed("q", 0) + feed("k", 0) + feed("v", 0)
    for r in range(KC):
        steps += (features(r, 0) + feed("q", r + 1) + [("kv", r, 0, 0)] + features(r, 1) + feed("k", r + 1)
                  + [("num", r, 0, 0), ("kv", r, 1, 0)] + feed("v", r + 1) + [("num", r, 1, 0)])
    return steps


MIX_STEPS = mixer_steps()
MIX_COLS = ((0, 313), (313, N))


def mix_count(kind, r, h):
    return 1 + max(n for n, s in enumerate(MIX_STEPS) if s[:3] == (kind, r, h))


def mix_bank(n):
    kind, _, h, _ = MIX_STEPS[n]
    if kind == "kv":
        return 4 + h
    if kind == "num":
        return 6 + h
    return sum(s[0] not in ("kv", "num") for s in MIX_STEPS[:n]) % 4


_ORDER = ['x', 'src', 'dst', 'W1s', 'b1s', 'W1d', 'b1d', 'attn1', 'ln1_w', 'ln1_b', 'Wos', 'bos', 'Wod', 'bod',
          'attno', 'lno_w', 'lno_b', 'qkv_wT', 'qk_bcols', 'v_brow', 'proj_wT', 'proj_b', 'proj_matT', 'gate_wT',
          'gate_bias', 'moe_w']


def lay_out(inputs):
    import numpy as np
    a = {k: np.asarray(v) for k, v in inputs.items()}
    g = {k: a['L0_gnn_' + k] for k in ('W1s', 'b1s', 'W1d', 'b1d', 'ln1_w', 'ln1_b', 'Wos', 'bos', 'Wod', 'bod', 'lno_w', 'lno_b')}
    g['attn1'] = a['L0_gnn_attn1'].reshape(-1)
    g['attno'] = a['L0_gnn_attno'].reshape(-1)
    g['x'], g['src'], g['dst'] = a['x'], a['src'], a['dst']
    g['qkv_wT'] = a['L0_mix_qkv_w'].T
    g['qk_bcols'] = a['L0_mix_qkv_b'][:2 * D].reshape(2 * KC, 128).T
    g['v_brow'] = a['L0_mix_qkv_b'][2 * D:].reshape(1, D)
    g['proj_wT'] = a['L0_mix_proj_w'].T
    g['proj_b'] = a['L0_mix_proj_b']
    g['proj_matT'] = a['L0_mix_proj_mat'].T
    g['gate_wT'] = a['L0_ffn_gate_weight'].T
    g['gate_bias'] = a['L0_ffn_gate_bias']

    def pieces(w, chunks):
        e, o, i = w.shape
        t = w.transpose(0, 2, 1).reshape(e, 2, chunks // 2, 128, o)
        return t.transpose(0, 1, 3, 2, 4).reshape(e, 2, 128, PIECE)

    cat = lambda w, s: np.concatenate([a['L0_ffn_' + w], a['L0_ffn_' + s][None]], 0)
    g['moe_w'] = np.concatenate([pieces(cat('w1', 'sw1'), KC), pieces(cat('w3', 'sw3'), KC),
                                 pieces(cat('w2', 'sw2'), IC)], 1)
    return {k: np.ascontiguousarray(g[k]) for k in _ORDER}


def kernel(**inputs):
    import numpy as _np
    import concourse.bacc as _bacc
    from concourse import mybir as _mybir
    from concourse.bass_utils import run_bass_kernel_spmd as _run

    nc = _bacc.Bacc("TRN2", target_bir_lowering=False, num_devices=1)
    laid = lay_out(inputs)
    arrays, args = {}, {}
    for name in _ORDER:
        v = laid[name]
        arrays[f"in_{name}_dram"] = v
        args[name] = nc.dram_tensor(f"in_{name}_dram", v.shape, _mybir.dt.from_np(v.dtype), kind="ExternalInput").ap()
    args['out'] = nc.dram_tensor("out_0_dram", (N, D), _mybir.dt.from_np(_np.dtype('float32')), kind="ExternalOutput").ap()
    build(nc, **args)
    r = _run(nc, [arrays], core_ids=[0])
    return r.results[0]["out_0_dram"]
```
